# Optimizing a Trainium2 kernel written in Bass

```python
import numpy as np
import jax
import jax.numpy as jnp

def _softmax(x, axis=-1):
    return jax.nn.softmax(x, axis=axis)

def _gelu(x):
    return jax.nn.gelu(x, approximate=True)

def _silu(x):
    return jax.nn.silu(x)

def _sigmoid(x):
    return jax.nn.sigmoid(x)

def _layernorm(x, axis=-1, eps=1e-05):
    m = jnp.mean(x, axis=axis, keepdims=True)
    v = jnp.var(x, axis=axis, keepdims=True)
    return (x - m) / jnp.sqrt(v + eps)

def _scatter_add(tgt, idx, src, axis=0):
    return tgt.at[idx].add(src)

def _segment_sum(src, seg, n):
    return jax.ops.segment_sum(src, seg, n)
kernel_name = 'mk_early_fusion_d1_tok_img1024_r4_e2f5bb'

def setup_inputs(seed: int=0):
    np.random.seed(seed)
    _w = jnp.asarray

    def _rec_inputs():
        import jax
        import jax.numpy as jnp
        _rk = jax.random.key(seed)
        x = -0.000169711 + 1.00022 * jax.random.normal(jax.random.fold_in(_rk, 1), (64, 3, 128, 128), jnp.float32)
        txt = 2.36171e-05 + 0.13571 * jax.random.normal(jax.random.fold_in(_rk, 2), (64, 77, 256), jnp.float32)
        return (x, txt)
    x, txt = _rec_inputs()

    def _L0_tok_setup():
        import jax, jax.numpy as jnp
        import numpy as np
        C = 256
        H8 = 8
        DH = C // H8
        PS = 14
        CS = 3
        IMG = 168
        B = 4

        def _ln(x, g, b):
            mu = jnp.mean(x, axis=-1, keepdims=True)
            xc = x - mu
            var = jnp.mean(xc * xc, axis=-1, keepdims=True)
            return xc * jax.lax.rsqrt(var + 1e-05) * g + b

        def _forward(pixel_values, conv_w, class_emb, la_ln_q_g, la_ln_q_b, la_wq, la_ln_kv_g, la_ln_kv_b, la_wkv, la_proj_w, la_proj_b, ga_ln_q_g, ga_ln_q_b, ga_wq, ga_ln_kv_g, ga_ln_kv_b, ga_wkv, ga_proj_w, ga_proj_b, mod_w, mod_b):
            b = pixel_values.shape[0]
            pe = jax.lax.conv_general_dilated(pixel_values, conv_w, (PS, PS), 'VALID', dimension_numbers=('NCHW', 'OIHW', 'NCHW'))
            HP = pe.shape[2]
            h = HP // CS
            hw, N = (h * h, CS * CS)
            scale = C ** (-0.5)
            grid = pe.reshape(b, C, h, CS, h, CS)
            red = grid.mean(axis=(3, 5)).reshape(b, C, hw).transpose(0, 2, 1)
            win = grid.transpose(0, 2, 4, 3, 5, 1).reshape(b, hw, N, C)
            q = _ln(red, la_ln_q_g, la_ln_q_b) @ la_wq
            q = q.reshape(b, hw, H8, DH).transpose(0, 2, 1, 3)
            kv = _ln(win, la_ln_kv_g, la_ln_kv_b) @ la_wkv
            kv = kv.reshape(b, hw, N, 2, H8, DH).transpose(3, 0, 4, 1, 2, 5)
            k_, v_ = (kv[0], kv[1])
            attn = jax.nn.softmax(jnp.einsum('bhnd,bhnkd->bhnk', q * scale, k_), axis=-1)
            agg = jnp.einsum('bhnk,bhnkd->bhnd', attn, v_)
            agg = agg.transpose(0, 2, 1, 3).reshape(b, hw, C)
            local_out = red + agg @ la_proj_w + la_proj_b
            cls = jnp.broadcast_to(class_emb, (b, 1, C))
            gq = (_ln(cls, ga_ln_q_g, ga_ln_q_b) @ ga_wq).reshape(b, H8, DH)
            gkv = _ln(local_out, ga_ln_kv_g, ga_ln_kv_b) @ ga_wkv
            gkv = gkv.reshape(b, hw, 2, H8, DH).transpose(2, 0, 3, 1, 4)
            gk, gv = (gkv[0], gkv[1])
            gattn = jax.nn.softmax(jnp.einsum('bhd,bhnd->bhn', gq * scale, gk), axis=-1)
            gagg = jnp.einsum('bhn,bhnd->bhd', gattn, gv).reshape(b, 1, C)
            cls_out = cls + gagg @ ga_proj_w + ga_proj_b
            patch_out = local_out @ mod_w + mod_b
            return jnp.concatenate([patch_out, cls_out], axis=1)
        key = jax.random.key(seed)
        ks = jax.random.split(key, 16)
        nrm = lambda k, shape: jax.random.normal(k, shape, jnp.float32) * 0.02
        return {'pixel_values': jax.random.normal(ks[0], (B, 3, IMG, IMG), jnp.float32), 'pixel_masks': jnp.ones((B, 1, IMG, IMG), jnp.float32), 'conv_w': nrm(ks[1], (C, 3, PS, PS)), 'class_emb': nrm(ks[2], (C,)), 'la_ln_q_g': jnp.ones((C,)), 'la_ln_q_b': jnp.zeros((C,)), 'la_wq': nrm(ks[3], (C, C)), 'la_ln_kv_g': jnp.ones((C,)), 'la_ln_kv_b': jnp.zeros((C,)), 'la_wkv': nrm(ks[4], (C, 2 * C)), 'la_proj_w': nrm(ks[5], (C, C)), 'la_proj_b': jnp.zeros((C,)), 'ga_ln_q_g': jnp.ones((C,)), 'ga_ln_q_b': jnp.zeros((C,)), 'ga_wq': nrm(ks[6], (C, C)), 'ga_ln_kv_g': jnp.ones((C,)), 'ga_ln_kv_b': jnp.zeros((C,)), 'ga_wkv': nrm(ks[7], (C, 2 * C)), 'ga_proj_w': nrm(ks[8], (C, C)), 'ga_proj_b': jnp.zeros((C,)), 'mod_w': nrm(ks[9], (C, C)), 'mod_b': jnp.zeros((C,))}
    _L0_tok_all = _L0_tok_setup()
    _L0_tok_in = {k: v for k, v in _L0_tok_all.items() if k in ('pixel_masks', 'conv_w', 'class_emb', 'la_ln_q_g', 'la_ln_q_b', 'la_wq', 'la_ln_kv_g', 'la_ln_kv_b', 'la_wkv', 'la_proj_w', 'la_proj_b', 'ga_ln_q_g', 'ga_ln_q_b', 'ga_wq', 'ga_ln_kv_g', 'ga_ln_kv_b', 'ga_wkv', 'ga_proj_w', 'ga_proj_b', 'mod_w', 'mod_b')}
    del _L0_tok_all

    def _L0_attn_setup():
        import jax, jax.numpy as jnp
        import numpy as np
        DIM = 256
        NUM_HEADS = 16
        HEAD_DIM = DIM // NUM_HEADS
        EPS = 1e-06

        def layer_norm(x, gamma, beta):
            mu = jnp.mean(x, axis=-1, keepdims=True)
            var = jnp.mean(jnp.square(x - mu), axis=-1, keepdims=True)
            return (x - mu) / jnp.sqrt(var + EPS) * gamma + beta

        def apply_rope(q, k):
            seq_len, head_dim = (q.shape[1], q.shape[3])
            half = head_dim // 2
            freq_range = jnp.arange(half, dtype=jnp.float32) / half
            inv_freq = 1.0 / 10000.0 ** freq_range
            t = jnp.arange(seq_len, dtype=jnp.float32)
            freqs = jnp.outer(t, inv_freq)
            emb = jnp.concatenate([freqs, freqs], axis=-1)
            cos = jnp.cos(emb)[None, :, None, :]
            sin = jnp.sin(emb)[None, :, None, :]

            def rotate_half(x):
                x1, x2 = (x[..., :half], x[..., half:])
                return jnp.concatenate([-x2, x1], axis=-1)
            return (q * cos + rotate_half(q) * sin, k * cos + rotate_half(k) * sin)
        key = jax.random.key(seed)
        ks = jax.random.split(key, 4)
        B, S = (2, 512)
        x = jax.random.normal(ks[0], (B, S, DIM), dtype=jnp.float32)
        lim_qkv = float(np.sqrt(6.0 / (DIM + 3 * DIM)))
        w_qkv = jax.random.uniform(ks[1], (3 * DIM, DIM), dtype=jnp.float32, minval=-lim_qkv, maxval=lim_qkv)
        lim_p = float(np.sqrt(6.0 / (DIM + DIM)))
        w_proj = jax.random.uniform(ks[2], (DIM, DIM), dtype=jnp.float32, minval=-lim_p, maxval=lim_p)
        b_proj = jnp.zeros((DIM,), dtype=jnp.float32)
        q_gamma = jnp.ones((HEAD_DIM,), dtype=jnp.float32)
        q_beta = jnp.zeros((HEAD_DIM,), dtype=jnp.float32)
        k_gamma = jnp.ones((HEAD_DIM,), dtype=jnp.float32)
        k_beta = jnp.zeros((HEAD_DIM,), dtype=jnp.float32)
        return {'x': x, 'w_qkv': w_qkv, 'w_proj': w_proj, 'b_proj': b_proj, 'q_gamma': q_gamma, 'q_beta': q_beta, 'k_gamma': k_gamma, 'k_beta': k_beta}
    _L0_attn_all = _L0_attn_setup()
    _L0_attn_in = {k: v for k, v in _L0_attn_all.items() if k in ('w_qkv', 'w_proj', 'b_proj', 'q_gamma', 'q_beta', 'k_gamma', 'k_beta')}
    del _L0_attn_all

    def _L0_ffn_setup():
        import jax, jax.numpy as jnp
        import numpy as np
        B, S, D, O, E, R = (8, 512, 256, 256, 8, 4)
        TOP_K = 2
        SCALING = 4.0 / 4.0
        key = jax.random.key(seed)
        k0, k1, k2, k3, k4 = jax.random.split(key, 5)
        hidden_states = jax.random.normal(k0, (B, S, D), dtype=jnp.float32)
        W_lin = jax.random.normal(k1, (O, D), dtype=jnp.float32) * 0.02
        b_lin = jnp.zeros((O,), dtype=jnp.float32)
        gate_w = jax.random.normal(k2, (E, D), dtype=jnp.float32) * 0.02
        left = jax.random.normal(k3, (E, D, R), dtype=jnp.float32) * 0.02
        right = jax.random.normal(k4, (E, R, O), dtype=jnp.float32) * 0.02
        return {'hidden_states': hidden_states, 'W_lin': W_lin, 'b_lin': b_lin, 'gate_w': gate_w, 'left': left, 'right': right}
    _L0_ffn_all = _L0_ffn_setup()
    _L0_ffn_in = {k: v for k, v in _L0_ffn_all.items() if k in ('W_lin', 'b_lin', 'gate_w', 'left', 'right')}
    del _L0_ffn_all
    return {'x': x, 'txt': txt, 'L0_tok_pixel_masks': _L0_tok_in['pixel_masks'], 'L0_tok_conv_w': _L0_tok_in['conv_w'], 'L0_tok_class_emb': _L0_tok_in['class_emb'], 'L0_tok_la_ln_q_g': _L0_tok_in['la_ln_q_g'], 'L0_tok_la_ln_q_b': _L0_tok_in['la_ln_q_b'], 'L0_tok_la_wq': _L0_tok_in['la_wq'], 'L0_tok_la_ln_kv_g': _L0_tok_in['la_ln_kv_g'], 'L0_tok_la_ln_kv_b': _L0_tok_in['la_ln_kv_b'], 'L0_tok_la_wkv': _L0_tok_in['la_wkv'], 'L0_tok_la_proj_w': _L0_tok_in['la_proj_w'], 'L0_tok_la_proj_b': _L0_tok_in['la_proj_b'], 'L0_tok_ga_ln_q_g': _L0_tok_in['ga_ln_q_g'], 'L0_tok_ga_ln_q_b': _L0_tok_in['ga_ln_q_b'], 'L0_tok_ga_wq': _L0_tok_in['ga_wq'], 'L0_tok_ga_ln_kv_g': _L0_tok_in['ga_ln_kv_g'], 'L0_tok_ga_ln_kv_b': _L0_tok_in['ga_ln_kv_b'], 'L0_tok_ga_wkv': _L0_tok_in['ga_wkv'], 'L0_tok_ga_proj_w': _L0_tok_in['ga_proj_w'], 'L0_tok_ga_proj_b': _L0_tok_in['ga_proj_b'], 'L0_tok_mod_w': _L0_tok_in['mod_w'], 'L0_tok_mod_b': _L0_tok_in['mod_b'], 'L0_attn_w_qkv': _L0_attn_in['w_qkv'], 'L0_attn_w_proj': _L0_attn_in['w_proj'], 'L0_attn_b_proj': _L0_attn_in['b_proj'], 'L0_attn_q_gamma': _L0_attn_in['q_gamma'], 'L0_attn_q_beta': _L0_attn_in['q_beta'], 'L0_attn_k_gamma': _L0_attn_in['k_gamma'], 'L0_attn_k_beta': _L0_attn_in['k_beta'], 'L0_ffn_W_lin': _L0_ffn_in['W_lin'], 'L0_ffn_b_lin': _L0_ffn_in['b_lin'], 'L0_ffn_gate_w': _L0_ffn_in['gate_w'], 'L0_ffn_left': _L0_ffn_in['left'], 'L0_ffn_right': _L0_ffn_in['right']}

def reference(x, txt, L0_tok_pixel_masks, L0_tok_conv_w, L0_tok_class_emb, L0_tok_la_ln_q_g, L0_tok_la_ln_q_b, L0_tok_la_wq, L0_tok_la_ln_kv_g, L0_tok_la_ln_kv_b, L0_tok_la_wkv, L0_tok_la_proj_w, L0_tok_la_proj_b, L0_tok_ga_ln_q_g, L0_tok_ga_ln_q_b, L0_tok_ga_wq, L0_tok_ga_ln_kv_g, L0_tok_ga_ln_kv_b, L0_tok_ga_wkv, L0_tok_ga_proj_w, L0_tok_ga_proj_b, L0_tok_mod_w, L0_tok_mod_b, L0_attn_w_qkv, L0_attn_w_proj, L0_attn_b_proj, L0_attn_q_gamma, L0_attn_q_beta, L0_attn_k_gamma, L0_attn_k_beta, L0_ffn_W_lin, L0_ffn_b_lin, L0_ffn_gate_w, L0_ffn_left, L0_ffn_right):
    import jax
    import jax.numpy as jnp

    def _L0_tok_ref(pixel_values, pixel_masks, conv_w, class_emb, la_ln_q_g, la_ln_q_b, la_wq, la_ln_kv_g, la_ln_kv_b, la_wkv, la_proj_w, la_proj_b, ga_ln_q_g, ga_ln_q_b, ga_wq, ga_ln_kv_g, ga_ln_kv_b, ga_wkv, ga_proj_w, ga_proj_b, mod_w, mod_b):
        import jax, jax.numpy as jnp
        import numpy as np
        C = 256
        H8 = 8
        DH = C // H8
        PS = 14
        CS = 3
        IMG = 168
        B = 4

        def _ln(x, g, b):
            mu = jnp.mean(x, axis=-1, keepdims=True)
            xc = x - mu
            var = jnp.mean(xc * xc, axis=-1, keepdims=True)
            return xc * jax.lax.rsqrt(var + 1e-05) * g + b

        def _forward(pixel_values, conv_w, class_emb, la_ln_q_g, la_ln_q_b, la_wq, la_ln_kv_g, la_ln_kv_b, la_wkv, la_proj_w, la_proj_b, ga_ln_q_g, ga_ln_q_b, ga_wq, ga_ln_kv_g, ga_ln_kv_b, ga_wkv, ga_proj_w, ga_proj_b, mod_w, mod_b):
            b = pixel_values.shape[0]
            pe = jax.lax.conv_general_dilated(pixel_values, conv_w, (PS, PS), 'VALID', dimension_numbers=('NCHW', 'OIHW', 'NCHW'))
            HP = pe.shape[2]
            h = HP // CS
            hw, N = (h * h, CS * CS)
            scale = C ** (-0.5)
            grid = pe.reshape(b, C, h, CS, h, CS)
            red = grid.mean(axis=(3, 5)).reshape(b, C, hw).transpose(0, 2, 1)
            win = grid.transpose(0, 2, 4, 3, 5, 1).reshape(b, hw, N, C)
            q = _ln(red, la_ln_q_g, la_ln_q_b) @ la_wq
            q = q.reshape(b, hw, H8, DH).transpose(0, 2, 1, 3)
            kv = _ln(win, la_ln_kv_g, la_ln_kv_b) @ la_wkv
            kv = kv.reshape(b, hw, N, 2, H8, DH).transpose(3, 0, 4, 1, 2, 5)
            k_, v_ = (kv[0], kv[1])
            attn = jax.nn.softmax(jnp.einsum('bhnd,bhnkd->bhnk', q * scale, k_), axis=-1)
            agg = jnp.einsum('bhnk,bhnkd->bhnd', attn, v_)
            agg = agg.transpose(0, 2, 1, 3).reshape(b, hw, C)
            local_out = red + agg @ la_proj_w + la_proj_b
            cls = jnp.broadcast_to(class_emb, (b, 1, C))
            gq = (_ln(cls, ga_ln_q_g, ga_ln_q_b) @ ga_wq).reshape(b, H8, DH)
            gkv = _ln(local_out, ga_ln_kv_g, ga_ln_kv_b) @ ga_wkv
            gkv = gkv.reshape(b, hw, 2, H8, DH).transpose(2, 0, 3, 1, 4)
            gk, gv = (gkv[0], gkv[1])
            gattn = jax.nn.softmax(jnp.einsum('bhd,bhnd->bhn', gq * scale, gk), axis=-1)
            gagg = jnp.einsum('bhn,bhnd->bhd', gattn, gv).reshape(b, 1, C)
            cls_out = cls + gagg @ ga_proj_w + ga_proj_b
            patch_out = local_out @ mod_w + mod_b
            return jnp.concatenate([patch_out, cls_out], axis=1)
        del pixel_masks
        return _forward(pixel_values, conv_w, class_emb, la_ln_q_g, la_ln_q_b, la_wq, la_ln_kv_g, la_ln_kv_b, la_wkv, la_proj_w, la_proj_b, ga_ln_q_g, ga_ln_q_b, ga_wq, ga_ln_kv_g, ga_ln_kv_b, ga_wkv, ga_proj_w, ga_proj_b, mod_w, mod_b)

    def _L0_attn_ref(x, w_qkv, w_proj, b_proj, q_gamma, q_beta, k_gamma, k_beta):
        import jax, jax.numpy as jnp
        import numpy as np
        DIM = 256
        NUM_HEADS = 16
        HEAD_DIM = DIM // NUM_HEADS
        EPS = 1e-06

        def layer_norm(x, gamma, beta):
            mu = jnp.mean(x, axis=-1, keepdims=True)
            var = jnp.mean(jnp.square(x - mu), axis=-1, keepdims=True)
            return (x - mu) / jnp.sqrt(var + EPS) * gamma + beta

        def apply_rope(q, k):
            seq_len, head_dim = (q.shape[1], q.shape[3])
            half = head_dim // 2
            freq_range = jnp.arange(half, dtype=jnp.float32) / half
            inv_freq = 1.0 / 10000.0 ** freq_range
            t = jnp.arange(seq_len, dtype=jnp.float32)
            freqs = jnp.outer(t, inv_freq)
            emb = jnp.concatenate([freqs, freqs], axis=-1)
            cos = jnp.cos(emb)[None, :, None, :]
            sin = jnp.sin(emb)[None, :, None, :]

            def rotate_half(x):
                x1, x2 = (x[..., :half], x[..., half:])
                return jnp.concatenate([-x2, x1], axis=-1)
            return (q * cos + rotate_half(q) * sin, k * cos + rotate_half(k) * sin)
        B, S, C = x.shape
        H, D = (NUM_HEADS, HEAD_DIM)
        qkv = jnp.einsum('bsc,oc->bso', x, w_qkv).reshape(B, S, 3, H, D)
        q = layer_norm(qkv[:, :, 0], q_gamma, q_beta)
        k = layer_norm(qkv[:, :, 1], k_gamma, k_beta)
        v = qkv[:, :, 2]
        q, k = apply_rope(q, k)
        scale = D ** (-0.5)
        q = q.astype(jnp.float32) * scale
        k = k.astype(jnp.float32)
        v = v.astype(jnp.float32)
        attn = jnp.einsum('bqhd,bkhd->bhqk', q, k)
        attn = jax.nn.softmax(attn, axis=-1)
        out = jnp.einsum('bhqk,bkhd->bqhd', attn, v).reshape(B, S, C)
        out = jnp.einsum('bsc,oc->bso', out, w_proj) + b_proj
        return out

    def _L0_ffn_ref(hidden_states, W_lin, b_lin, gate_w, left, right):
        import jax, jax.numpy as jnp
        import numpy as np
        B, S, D, O, E, R = (8, 512, 256, 256, 8, 4)
        TOP_K = 2
        SCALING = 4.0 / 4.0
        bsz, seq, d_in = hidden_states.shape
        x = hidden_states.reshape(-1, d_in)
        logits = x @ gate_w.T
        scores = jax.nn.softmax(logits, axis=-1)
        weights, idx = jax.lax.top_k(scores, TOP_K)
        base = x @ W_lin.T + b_lin
        left_sel = left[idx]
        right_sel = right[idx]
        t = jnp.einsum('nd,nkdr->nkr', x, left_sel)
        out_k = jnp.einsum('nkr,nkro->nko', t, right_sel)
        lora = jnp.sum(weights[..., None] * out_k, axis=1) * SCALING
        return (base + lora).reshape(bsz, seq, -1)
    h = _L0_tok_ref(x, L0_tok_pixel_masks, L0_tok_conv_w, L0_tok_class_emb, L0_tok_la_ln_q_g, L0_tok_la_ln_q_b, L0_tok_la_wq, L0_tok_la_ln_kv_g, L0_tok_la_ln_kv_b, L0_tok_la_wkv, L0_tok_la_proj_w, L0_tok_la_proj_b, L0_tok_ga_ln_q_g, L0_tok_ga_ln_q_b, L0_tok_ga_wq, L0_tok_ga_ln_kv_g, L0_tok_ga_ln_kv_b, L0_tok_ga_wkv, L0_tok_ga_proj_w, L0_tok_ga_proj_b, L0_tok_mod_w, L0_tok_mod_b)
    h = jnp.concatenate([h, txt], axis=1)
    h = h + _L0_attn_ref(_layernorm(h, axis=-1), L0_attn_w_qkv, L0_attn_w_proj, L0_attn_b_proj, L0_attn_q_gamma, L0_attn_q_beta, L0_attn_k_gamma, L0_attn_k_beta)
    h = h + _L0_ffn_ref(_layernorm(h, axis=-1), L0_ffn_W_lin, L0_ffn_b_lin, L0_ffn_gate_w, L0_ffn_left, L0_ffn_right)
    return h

_drawn_inputs = setup_inputs


def setup_inputs(seed=0):
    import zlib

    import numpy as np

    out = dict(_drawn_inputs(seed))
    spreads = {'L0_tok_pixel_masks': (1.0, 0.2),
     'L0_tok_la_ln_q_g': (1.0, 0.6),
     'L0_tok_la_ln_q_b': (0.0, 0.8),
     'L0_tok_la_ln_kv_g': (1.0, 0.6),
     'L0_tok_la_ln_kv_b': (0.0, 0.488),
     'L0_tok_la_proj_b': (0.0, 0.1),
     'L0_tok_ga_ln_q_g': (1.0, 0.6),
     'L0_tok_ga_ln_q_b': (0.0, 2.0),
     'L0_tok_ga_ln_kv_g': (1.0, 0.6),
     'L0_tok_ga_ln_kv_b': (0.0, 0.663),
     'L0_tok_ga_proj_b': (0.0, 0.1),
     'L0_tok_mod_b': (0.0, 0.1),
     'L0_attn_b_proj': (0.0, 0.1),
     'L0_attn_q_gamma': (1.0, 0.2),
     'L0_attn_q_beta': (0.0, 0.1),
     'L0_attn_k_gamma': (1.0, 0.2),
     'L0_attn_k_beta': (0.0, 0.1),
     'L0_ffn_b_lin': (0.0, 0.1)}
    factors = {'L0_tok_la_wq': 8.0,
     'L0_tok_ga_wq': 8.0,
     'L0_ffn_gate_w': 7.939,
     'L0_ffn_left': 7.037,
     'L0_ffn_right': 6.847}
    for name, (base, spread) in spreads.items():
        noise = np.random.default_rng([zlib.crc32(name.encode()), seed]).standard_normal(out[name].shape)
        drawn = base * np.exp(spread * noise) if base else spread * noise
        out[name] = jnp.asarray(drawn.astype(out[name].dtype))
    for name, factor in factors.items():
        out[name] = (out[name] * factor).astype(out[name].dtype)
    return out
```

```python
import numpy as np
import concourse.bass as bass
import concourse.mybir as mybir
from contextlib import ExitStack

F32 = mybir.dt.float32
BF16 = mybir.dt.bfloat16
ALU = mybir.AluOpType
ACT = mybir.ActivationFunctionType
AX_X = mybir.AxisListType.X

P = 128
C = 256
CC = C // P
IMAGES = 64
PATCH = 14
GRID = 3
WINDOWS = GRID * GRID
CELLS = GRID * GRID
TXT = 77
SEQ = WINDOWS + 1 + TXT
ALL_W = IMAGES * WINDOWS

PIXELS = 3 * PATCH * PATCH
KROWS = 120
KCH = -(-PIXELS // KROWS)
STEPS = -(-ALL_W // P)
TOK_M = [min(P, ALL_W - P * s) for s in range(STEPS)]
LH, LD = 8, 32
CONV_SLOTS, XHT_SLOTS, KV_SLOTS = 2, 3, 2

HEADS, HD = 16, 16
GB = 4
GROUPS = IMAGES // GB
GT = GB * SEQ
TILES = 3
TP = GT // TILES
QP = 96
HALF = HEADS // 2
UNITS = 2 * GB
SPARE = 4 * QP
EXPERTS, RANK = 8, 4
LR = EXPERTS * RANK
FFN_N = C + LR + EXPERTS

ROWS = ['la_proj_b', 'class_emb', 'ga_ln_q_g', 'ga_ln_q_b', 'ga_proj_b', 'mod_b', 'b_proj', 'b_lin']
COLS = ['la_ln_q_g', 'la_ln_kv_g', 'ga_ln_kv_g', 'la_ln_q_b', 'la_ln_kv_b', 'ga_ln_kv_b']


def counted(engine, semaphore, start=0):
    n = [start]

    def link(instruction):
        n[0] = n[0] + 1
        instruction.then_inc(semaphore, 1)
        engine.wait_ge(semaphore, n[0])
        return instruction

    return link


def patch_tokens(nc, io, h_dram, patch_dram, gv_dram, gs_dram):
    with ExitStack() as ctx:
        def sb(name, shape, dt=F32):
            return ctx.enter_context(nc.sbuf_tensor(name, shape, dt))

        def sem(name):
            return ctx.enter_context(nc.semaphore(name))

        def row(name):
            return rows[:, ROWS.index(name), :]

        ident = sb("ident1", [P, P])
        xcols = sb("xcols", [KROWS, 2, KCH, CELLS * P])
        w_conv = sb("w_conv", [KROWS, KCH, C])
        w_q = sb("w_q", [P, CC, C])
        w_kv = sb("w_kv", [P, CC, 2 * C])
        w_proj = sb("w_proj", [P, CC, C])
        w_gq = sb("w_gq", [P, CC, C])
        w_gkv = sb("w_gkv", [P, CC, 2 * C])
        w_gproj = sb("w_gproj", [P, CC, C])
        w_mod = sb("w_mod", [P, CC, C])
        rows = sb("rows", [P, len(ROWS), C])
        cols = sb("cols", [P, len(COLS), CC])
        beta_wide = sb("beta_wide", [P, 3, CC, P])
        eps = sb("eps1", [P, 1])
        bias_q = sb("bias_q", [P, C])
        bias_kv = sb("bias_kv", [P, 2 * C])
        bias_gkv = sb("bias_gkv", [P, 2 * C])
        gq = sb("gq", [P, C])
        gq_kb = sb("gq_kb", [P, LH])
        cls_n = sb("cls_n", [P, C])
        pe = sb("pe", [P, 2, CELLS, C])
        stats = sb("stats", [P, 2, CELLS, 6])
        mv = sb("mv", [P, 2, CELLS, 2])
        rstd = sb("rstd", [P, 2, CELLS])
        lnv = sb("lnv", [P, CELLS])
        red = sb("red", [P, 3, C])
        qn = sb("qn", [P, C])
        s_stats = sb("s_stats", [P, 6])
        s_mv = sb("s_mv", [P, 2])
        s_rstd = sb("s_rstd", [P, 1])
        s_lnv = sb("s_lnv", [P, 1])
        smT = sb("smT", [P, CC, P])
        q = sb("q", [P, C])
        q_kb = sb("q_kb", [P, 2, LH])
        xhT = sb("xhT", [P, XHT_SLOTS, CC, P])
        prod = sb("prod", [P, C])
        score = sb("score", [P, 2, CELLS, LH])
        v = sb("v", [P, 2, CELLS, C])
        attn = sb("attn", [P, CELLS, LH])
        smax = sb("smax", [P, LH])
        ssum = sb("ssum", [P, LH])
        vw = sb("vw", [P, CELLS, C])
        agg = sb("agg", [P, C])
        redb = sb("redb", [P, C])
        lo = sb("lo", [P, C])
        ln_lo = sb("ln_lo", [P, C])
        patch = sb("patch", [P, C])
        gs = sb("gs", [P, LH])
        gv = sb("gv", [P, C])
        t_stats = sb("t_stats", [P, 6])
        t_mv = sb("t_mv", [P, 2])
        t_rstd = sb("t_rstd", [P, 1])
        t_lnv = sb("t_lnv", [P, 1])
        tT = sb("tT", [P, CC, P])
        cls_gv = sb("cls_gv", [IMAGES, WINDOWS, C])
        cls_gs = sb("cls_gs", [IMAGES, WINDOWS, LH])
        cls_out = sb("cls_out", [IMAGES, C])
        p_conv = ctx.enter_context(nc.psum_tensor("p_conv", [P, CONV_SLOTS, 2 * C], F32))
        p_xhT = ctx.enter_context(nc.psum_tensor("p_xhT", [P, 2, 4, P], F32))
        p_kv = ctx.enter_context(nc.psum_tensor("p_kv", [P, KV_SLOTS, 2 * C], F32))
        p_T = ctx.enter_context(nc.psum_tensor("p_T", [P, 4, P], F32))
        p_mm = ctx.enter_context(nc.psum_tensor("p_mm", [P, 2 * C], F32))

        names = ("w_in v_in ident_ok consts beta_ok bias_mm bias_out gamma_in cls_norm clsT cls_qT cls_q "
                 "conv_ok pe_out stat_ok rstd_ok norm_ok red_ok qv_ok qr_ok qn_ok qT_ok qT_out q_mm q_ok "
                 "xT_ok xT_out kv_ok k_read v_out score_ok m_ok e_ok att_ok vw_ok agg_ok aggT_ok aggT_out proj_ok "
                 "lo_ok loT_ok loT_out mod_ok patch_ok tv_ok tr_ok tn_ok tnT_ok tnT_out gkv_ok g_ok redb_ok "
                 "c_in c_max c_exp c_att c_agg cT_ok cT_out c_mm c_out dve_1 act_1 pool_1").split()
        S = {n: sem(n) for n in names}
        x_in = [sem("x_in0"), sem("x_in1")]
        st_patch = [sem("st_patch0"), sem("st_patch1")]
        st_g = [sem("st_g0"), sem("st_g1")]
        st_cls = sem("st_cls")
        block = ctx.enter_context(nc.Block())
        weights = [(w_q, 'la_wq'), (w_kv, 'la_wkv'), (w_gq, 'ga_wq'), (w_gkv, 'ga_wkv'),
                   (w_proj, 'la_proj_w'), (w_gproj, 'ga_proj_w'), (w_mod, 'mod_w')]
        ITER = STEPS + 3

        @block.sync
        def _(sp):
            def load_x(s):
                m = CELLS * TOK_M[s]
                if s >= 2:
                    sp.wait_ge(S['conv_ok'], CELLS * (s - 1))
                for k in range(KCH):
                    src = io['x_cols'][s, KROWS * k:KROWS * (k + 1), 0:m]
                    sp.dma_start(xcols[:, s % 2, k, 0:m], src).then_inc(x_in[s % 2], 16)

            h_rows = h_dram.rearrange("(b s) c -> b s c", s=SEQ)
            sp.dma_start(w_conv[:], io['conv_w'].rearrange("(k p) n -> p k n", p=KROWS)).then_inc(S['v_in'], 16)
            sp.dma_start(cols[:], io['cols']).then_inc(S['v_in'], 16)
            load_x(0)
            sp.dma_start(rows[:], io['rows'].unsqueeze(0).broadcast_to([P, len(ROWS), C])).then_inc(S['v_in'], 16)
            for w, name in weights:
                sp.dma_start(w[:], io[name].rearrange("(k p) n -> p k n", p=P)).then_inc(S['w_in'], 16)
            load_x(1)
            sp.dma_start(h_rows[:, WINDOWS + 1:, :], io['txt']).then_inc(st_cls, 16)
            for it in range(2, ITER + 1):
                if it < STEPS:
                    load_x(it)
                w = it - 3
                if 0 <= w < STEPS:
                    M, w0 = TOK_M[w], P * w
                    sp.wait_ge(S['patch_ok'], w + 1)
                    sp.dma_start(patch_dram[w0:w0 + M, :], patch[0:M, :]).then_inc(st_patch[w % 2], 16)
                    sp.wait_ge(S['g_ok'], 2 * (w + 1))
                    sp.dma_start(gv_dram[w0:w0 + M, :], gv[0:M, :]).then_inc(st_g[w % 2], 16)
                    sp.dma_start(gs_dram[w0:w0 + M, :], gs[0:M, :]).then_inc(st_g[w % 2], 16)
            for h in range(2):
                n = len(range(h, STEPS, 2))
                sp.wait_ge(st_patch[h], 16 * n)
                sp.wait_ge(st_g[h], 32 * n)
            sp.dma_start(h_rows[:, 0:WINDOWS, :], patch_dram.rearrange("(b n) c -> b n c", n=WINDOWS)
                         ).then_inc(st_cls, 16)
            sp.dma_start(cls_gv[:], gv_dram.rearrange("(b n) c -> b n c", n=WINDOWS)).then_inc(S['c_in'], 16)
            sp.dma_start(cls_gs[:], gs_dram.rearrange("(b n) h -> b n h", n=WINDOWS)).then_inc(S['c_in'], 16)
            sp.wait_ge(S['c_out'], 1)
            sp.dma_start(h_rows[:, WINDOWS, :], cls_out[:]).then_inc(st_cls, 16)
            sp.wait_ge(st_cls, 48)

        @block.gpsimd
        def _(pool):
            link = counted(pool, S['pool_1'])
            link(nc.gpsimd.memset(ident[:], 0.0))
            nc.gpsimd.affine_select(out=ident[:], in_=ident[:], compare_op=ALU.not_equal, fill=1.0, base=0,
                                    pattern=[[-1, P]], channel_multiplier=1).then_inc(S['ident_ok'], 1)
            nc.gpsimd.memset(eps[:], 1e-5).then_inc(S['consts'], 1)
            for it in range(ITER):
                w, u = it - 3, it - 2
                if 0 <= u < STEPS:
                    M = TOK_M[u]
                    pool.wait_ge(S['att_ok'], u + 1)
                    pool.wait_ge(S['v_out'], CELLS * (u + 1))
                    if u >= 1:
                        pool.wait_ge(S['agg_ok'], u)
                    nc.gpsimd.tensor_tensor(
                        vw[0:M].rearrange("p n (h d) -> p (n h) d", h=LH),
                        v[0:M, u % 2].rearrange("p n (h d) -> p (n h) d", h=LH),
                        attn[0:M].rearrange("p n h -> p (n h)").unsqueeze(2).broadcast_to([M, CELLS * LH, LD]),
                        ALU.mult).then_inc(S['vw_ok'], 1)
                    if u >= 1:
                        pool.wait_ge(S['lo_ok'], u)
                    pool.wait_ge(S['v_in'], 48)
                    nc.gpsimd.tensor_tensor(redb[0:M], red[0:M, u % 3], row('la_proj_b')[0:M],
                                            ALU.add).then_inc(S['redb_ok'], 1)

        @block.scalar
        def _(act):
            link = counted(act, S['act_1'])
            act.preload_act_table_set("natural_log_exp_and_others")
            act.wait_ge(S['consts'], 1)

            def rstd_of(M, var, tmp, out, signal):
                link(nc.scalar.activation(tmp, var, ACT.Ln, bias=eps[0:M, 0:1]))
                nc.scalar.activation(out, tmp, ACT.Exp, scale=-0.5).then_inc(S[signal], 1)

            act.wait_ge(S['cls_norm'], 1)
            rstd_of(P, t_mv[:, 1:2], t_lnv[:], t_rstd[:], 'tr_ok')
            act.wait_ge(S['clsT'], 1)
            nc.scalar.copy(tT[:], p_T[:, 0:CC]).then_inc(S['cls_qT'], 1)

            for it in range(ITER):
                s, r, u, w = it, it - 1, it - 2, it - 3
                if 0 <= r < STEPS:
                    M = TOK_M[r]
                    act.wait_ge(S['qv_ok'], r + 1)
                    rstd_of(M, s_mv[0:M, 1:2], s_lnv[0:M], s_rstd[0:M], 'qr_ok')
                for n in range(CELLS + 3):
                    if s < STEPS and n < CELLS:
                        M, k = TOK_M[s], CELLS * s + n
                        act.wait_ge(S['conv_ok'], k + 1)
                        if n == 0 and s >= 2:
                            act.wait_ge(S['xT_ok'], CELLS * (s - 1))
                        nc.scalar.copy(pe[0:M, s % 2, n], p_conv[0:M, k % CONV_SLOTS, 0:C]).then_inc(S['pe_out'], 1)
                    if 0 <= w < STEPS:
                        M = TOK_M[w]
                        if n == 0:
                            act.wait_ge(S['aggT_ok'], w + 1)
                            nc.scalar.copy(tT[:, :, 0:M], p_T[:, 0:CC, 0:M]).then_inc(S['aggT_out'], 1)
                        if n == 2:
                            act.wait_ge(S['tv_ok'], w + 1)
                            rstd_of(M, t_mv[0:M, 1:2], t_lnv[0:M], t_rstd[0:M], 'tr_ok')
                        if n == 3:
                            act.wait_ge(S['loT_ok'], w + 1)
                            nc.scalar.copy(tT[:, :, 0:M], p_T[:, 0:CC, 0:M]).then_inc(S['loT_out'], 1)
                        if n == 5:
                            act.wait_ge(S['tnT_ok'], w + 1)
                            nc.scalar.copy(tT[:, :, 0:M], p_T[:, 0:CC, 0:M]).then_inc(S['tnT_out'], 1)
                    if 0 <= r < STEPS and n == 1:
                        M = TOK_M[r]
                        act.wait_ge(S['qT_ok'], r + 1)
                        nc.scalar.copy(smT[:, :, 0:M], p_T[:, 0:CC, 0:M]).then_inc(S['qT_out'], 1)
                    if 0 <= r < STEPS and n >= 2 and n - 2 < CELLS:
                        M, m = TOK_M[r], n - 2
                        k = CELLS * r + m
                        act.wait_ge(S['xT_ok'], k + 1)
                        if k >= XHT_SLOTS:
                            act.wait_ge(S['kv_ok'], k - XHT_SLOTS + 1)
                        nc.scalar.copy(xhT[:, k % XHT_SLOTS, :, 0:M], p_xhT[:, k % 2, 0:CC, 0:M]).then_inc(S['xT_out'], 1)
                    if 0 <= r < STEPS and n >= 3:
                        M, m = TOK_M[r], n - 3
                        k = CELLS * r + m
                        act.wait_ge(S['k_read'], k + 1)
                        if m == 0 and r >= 2:
                            act.wait_ge(S['vw_ok'], r - 1)
                        nc.scalar.copy(v[0:M, r % 2, m], p_kv[0:M, k % KV_SLOTS, C:2 * C]).then_inc(S['v_out'], 1)
                    if 0 <= u < STEPS and n == 4:
                        M = TOK_M[u]
                        act.wait_ge(S['m_ok'], u + 1)
                        nc.scalar.activation(attn[0:M], attn[0:M], ACT.Exp).then_inc(S['e_ok'], 1)
                if s < STEPS:
                    M = TOK_M[s]
                    act.wait_ge(S['stat_ok'], CELLS * (s + 1))
                    rstd_of(M, mv[0:M, s % 2, :, 1], lnv[0:M], rstd[0:M, s % 2], 'rstd_ok')
            act.wait_ge(S['c_max'], 1)
            nc.scalar.activation(cls_gs[:], cls_gs[:], ACT.Exp).then_inc(S['c_exp'], 1)
            act.wait_ge(S['cT_ok'], 1)
            nc.scalar.copy(tT[:, :, 0:IMAGES], p_T[:, 0:CC, 0:IMAGES]).then_inc(S['cT_out'], 1)

        @block.vector
        def _(dve):
            link = counted(dve, S['dve_1'])

            def moments(M, x, st, m_v, signal):
                link(nc.vector.bn_stats(st, x))
                nc.vector.bn_aggr(m_v, st).then_inc(S[signal], 1)

            dve.wait_ge(S['v_in'], 48)
            for k in range(3):
                for c in range(CC):
                    nc.vector.tensor_copy(beta_wide[:, k, c],
                                          cols[:, 3 + k, c:c + 1].broadcast_to([P, P])).then_inc(S['beta_ok'], 1)
            moments(P, row('class_emb'), t_stats[:], t_mv[:], 'cls_norm')
            dve.wait_ge(S['tr_ok'], 1)
            link(nc.vector.tensor_scalar(cls_n[:], row('class_emb'), t_mv[:, 0:1], t_rstd[:, 0:1],
                                         ALU.subtract, ALU.mult))
            link(nc.vector.tensor_tensor(cls_n[:], cls_n[:], row('ga_ln_q_g'), ALU.mult))
            nc.vector.tensor_tensor(cls_n[:], cls_n[:], row('ga_ln_q_b'), ALU.add).then_inc(S['cls_norm'], 1)
            dve.wait_ge(S['bias_mm'], 1)
            nc.vector.tensor_scalar(bias_q[:], p_kv[:, 0, 0:C], C ** -0.5, None, ALU.mult).then_inc(S['bias_out'], 1)
            dve.wait_ge(S['bias_mm'], 2)
            nc.vector.tensor_copy(bias_kv[:], p_kv[:, 1]).then_inc(S['bias_out'], 1)
            dve.wait_ge(S['bias_mm'], 3)
            nc.vector.tensor_copy(bias_gkv[:], p_kv[:, 0]).then_inc(S['bias_out'], 1)
            for k, w in enumerate((w_q, w_kv, w_gkv)):
                for c in range(CC):
                    nc.vector.tensor_scalar(w[:, c], w[:, c], cols[:, k, c:c + 1], None,
                                            ALU.mult).then_inc(S['gamma_in'], 1)
            dve.wait_ge(S['cls_q'], 1)
            link(nc.vector.tensor_scalar(gq[:], p_mm[:, 0:C], C ** -0.5, None, ALU.mult))
            dve.wait_ge(S['bias_out'], 3)
            link(nc.vector.tensor_tensor(prod[:], gq[:], bias_gkv[:, 0:C], ALU.mult))
            link(nc.vector.reduce_sum(gq_kb[:], prod[:].rearrange("p (h d) -> p h d", h=LH), AX_X))

            def normalise(r, n):
                M = TOK_M[r]
                nc.vector.tensor_scalar(pe[0:M, r % 2, n], pe[0:M, r % 2, n], mv[0:M, r % 2, n, 0:1],
                                        rstd[0:M, r % 2, n:n + 1], ALU.subtract, ALU.mult).then_inc(S['norm_ok'], 1)

            for it in range(ITER):
                s, r, u, w = it, it - 1, it - 2, it - 3
                if 0 <= r < STEPS:
                    M = TOK_M[r]
                    dve.wait_ge(S['pe_out'], CELLS * (r + 1))
                    if r >= 3:
                        dve.wait_ge(S['redb_ok'], r - 2)
                    link(nc.vector.reduce_sum(red[0:M, r % 3], pe[0:M, r % 2].rearrange("p n c -> p c n"), AX_X))
                    link(nc.vector.tensor_scalar(red[0:M, r % 3], red[0:M, r % 3], 1.0 / CELLS, None, ALU.mult))
                    moments(M, red[0:M, r % 3], s_stats[0:M], s_mv[0:M], 'qv_ok')
                for n in range(CELLS + 3):
                    if s < STEPS and n < CELLS:
                        M, k = TOK_M[s], CELLS * s + n
                        dve.wait_ge(S['pe_out'], k + 1)
                        moments(M, pe[0:M, s % 2, n], stats[0:M, s % 2, n], mv[0:M, s % 2, n], 'stat_ok')
                    if 0 <= w < STEPS:
                        M = TOK_M[w]
                        if n == 1:
                            dve.wait_ge(S['proj_ok'], w + 1)
                            dve.wait_ge(S['redb_ok'], w + 1)
                            nc.vector.tensor_tensor(lo[0:M], p_mm[0:M, 0:C], redb[0:M], ALU.add).then_inc(S['lo_ok'], 1)
                            dve.wait_ge(S['lo_ok'], w + 1)
                            moments(M, lo[0:M], t_stats[0:M], t_mv[0:M], 'tv_ok')
                        if n == 3:
                            dve.wait_ge(S['tr_ok'], w + 2)
                            nc.vector.tensor_scalar(ln_lo[0:M], lo[0:M], t_mv[0:M, 0:1], t_rstd[0:M, 0:1],
                                                    ALU.subtract, ALU.mult).then_inc(S['tn_ok'], 1)
                        if n == 4:
                            dve.wait_ge(S['mod_ok'], w + 1)
                            if w >= 1:
                                dve.wait_ge(st_patch[(w - 1) % 2], 16 * ((w - 1) // 2 + 1))
                            nc.vector.tensor_tensor(patch[0:M], p_mm[0:M, 0:C], row('mod_b')[0:M],
                                                    ALU.add).then_inc(S['patch_ok'], 1)
                        if n == 7:
                            dve.wait_ge(S['gkv_ok'], w + 1)
                            link(nc.vector.tensor_tensor(prod[0:M], p_mm[0:M, 0:C], gq[0:M], ALU.mult))
                            if w >= 1:
                                dve.wait_ge(st_g[(w - 1) % 2], 32 * ((w - 1) // 2 + 1))
                            link(nc.vector.reduce_sum(gs[0:M], prod[0:M].rearrange("p (h d) -> p h d", h=LH), AX_X))
                            nc.vector.tensor_tensor(gs[0:M], gs[0:M], gq_kb[0:M], ALU.add).then_inc(S['g_ok'], 1)
                            nc.vector.tensor_tensor(gv[0:M], p_mm[0:M, C:2 * C], bias_gkv[0:M, C:2 * C],
                                                    ALU.add).then_inc(S['g_ok'], 1)
                            dve.wait_ge(S['g_ok'], 2 * (w + 1))
                    if 0 <= r < STEPS:
                        M = TOK_M[r]
                        if n == 0:
                            dve.wait_ge(S['qr_ok'], r + 1)
                            if r >= 1:
                                dve.wait_ge(S['qT_ok'], r)
                            nc.vector.tensor_scalar(qn[0:M], red[0:M, r % 3], s_mv[0:M, 0:1], s_rstd[0:M, 0:1],
                                                    ALU.subtract, ALU.mult).then_inc(S['qn_ok'], 1)
                            dve.wait_ge(S['rstd_ok'], r + 1)
                        if n < 3:
                            for m in range(3 * n, 3 * n + 3):
                                normalise(r, m)
                        if n == 2:
                            dve.wait_ge(S['q_mm'], r + 1)
                            nc.vector.scalar_tensor_tensor(q[0:M], p_mm[0:M, 0:C], C ** -0.5, bias_q[0:M],
                                                           ALU.mult, ALU.add).then_inc(S['q_ok'], 1)
                            dve.wait_ge(S['q_ok'], r + 1)
                            link(nc.vector.tensor_tensor(prod[0:M], q[0:M], bias_kv[0:M, 0:C], ALU.mult))
                            link(nc.vector.reduce_sum(q_kb[0:M, r % 2], prod[0:M].rearrange("p (h d) -> p h d", h=LH),
                                                      AX_X))
                        if n >= 3:
                            m = n - 3
                            k = CELLS * r + m
                            dve.wait_ge(S['kv_ok'], k + 1)
                            nc.vector.tensor_tensor(prod[0:M], p_kv[0:M, k % KV_SLOTS, 0:C], q[0:M],
                                                    ALU.mult).then_inc(S['k_read'], 1)
                            dve.wait_ge(S['k_read'], k + 1)
                            nc.vector.reduce_sum(score[0:M, r % 2, m], prod[0:M].rearrange("p (h d) -> p h d", h=LH),
                                                 AX_X).then_inc(S['score_ok'], 1)
                            dve.wait_ge(S['score_ok'], k + 1)
                    if 0 <= u < STEPS:
                        M = TOK_M[u]
                        if n == 2:
                            dve.wait_ge(S['score_ok'], CELLS * (u + 1))
                            if u >= 1:
                                dve.wait_ge(S['vw_ok'], u)
                            link(nc.vector.tensor_tensor(attn[0:M], score[0:M, u % 2],
                                                         q_kb[0:M, u % 2].unsqueeze(1).broadcast_to([M, CELLS, LH]),
                                                         ALU.add))
                            link(nc.vector.reduce_max(smax[0:M], attn[0:M].rearrange("p n h -> p h n"), AX_X))
                            nc.vector.tensor_tensor(attn[0:M], attn[0:M],
                                                    smax[0:M].unsqueeze(1).broadcast_to([M, CELLS, LH]),
                                                    ALU.subtract).then_inc(S['m_ok'], 1)
                        if n == 5:
                            dve.wait_ge(S['e_ok'], u + 1)
                            link(nc.vector.reduce_sum(ssum[0:M], attn[0:M].rearrange("p n h -> p h n"), AX_X))
                            link(nc.vector.reciprocal(ssum[0:M], ssum[0:M]))
                            nc.vector.tensor_tensor(attn[0:M], attn[0:M],
                                                    ssum[0:M].unsqueeze(1).broadcast_to([M, CELLS, LH]),
                                                    ALU.mult).then_inc(S['att_ok'], 1)
                        if n == CELLS + 2:
                            dve.wait_ge(S['vw_ok'], u + 1)
                            link(nc.vector.reduce_sum(agg[0:M], vw[0:M].rearrange("p n c -> p c n"), AX_X))
                            nc.vector.tensor_tensor(agg[0:M], agg[0:M], bias_kv[0:M, C:2 * C],
                                                    ALU.add).then_inc(S['agg_ok'], 1)
            M = IMAGES
            dve.wait_ge(S['c_in'], 32)
            link(nc.vector.reduce_max(smax[0:M], cls_gs[:].rearrange("p n h -> p h n"), AX_X))
            nc.vector.tensor_tensor(cls_gs[:], cls_gs[:], smax[0:M].unsqueeze(1).broadcast_to([M, WINDOWS, LH]),
                                    ALU.subtract).then_inc(S['c_max'], 1)
            dve.wait_ge(S['c_exp'], 1)
            link(nc.vector.reduce_sum(ssum[0:M], cls_gs[:].rearrange("p n h -> p h n"), AX_X))
            link(nc.vector.reciprocal(ssum[0:M], ssum[0:M]))
            link(nc.vector.tensor_tensor(
                cls_gv[:].rearrange("p n (h d) -> p (n h) d", h=LH), cls_gv[:].rearrange("p n (h d) -> p (n h) d", h=LH),
                cls_gs[:].rearrange("p n h -> p (n h)").unsqueeze(2).broadcast_to([M, WINDOWS * LH, LD]), ALU.mult))
            link(nc.vector.reduce_sum(agg[0:M], cls_gv[:].rearrange("p n c -> p c n"), AX_X))
            nc.vector.tensor_tensor(agg[0:M].rearrange("p (h d) -> p h d", h=LH),
                                    agg[0:M].rearrange("p (h d) -> p h d", h=LH),
                                    ssum[0:M].unsqueeze(2).broadcast_to([M, LH, LD]), ALU.mult).then_inc(S['c_agg'], 1)
            link(nc.vector.tensor_tensor(lo[0:M], row('class_emb')[0:M], row('ga_proj_b')[0:M], ALU.add))
            dve.wait_ge(S['c_mm'], 1)
            nc.vector.tensor_tensor(cls_out[:], p_mm[0:M, 0:C], lo[0:M], ALU.add).then_inc(S['c_out'], 1)

        @block.tensor
        def _(pe_):
            def mm(out, lhs, rhs, signal=None):
                for c, (a, b) in enumerate(zip(lhs, rhs)):
                    last = nc.tensor.matmul(out, a, b, start=(c == 0), stop=(c == len(lhs) - 1))
                if signal:
                    last.then_inc(S[signal], 1)

            def transpose(out, x, M, signal):
                for c in range(CC):
                    last = nc.tensor.transpose(out[:, c, 0:M], x[0:M, c * P:(c + 1) * P], ident[0:M, 0:M])
                last.then_inc(S[signal], 1)

            pe_.wait_ge(S['w_in'], 16 * len(weights))
            pe_.wait_ge(S['beta_ok'], 3 * CC)
            for k, (w, n) in enumerate(((w_q, C), (w_kv, 2 * C), (w_gkv, 2 * C))):
                if k == 2:
                    pe_.wait_ge(S['bias_out'], 1)
                mm(p_kv[:, k % 2, 0:n], [beta_wide[:, k, c] for c in range(CC)], [w[:, c] for c in range(CC)], 'bias_mm')
            pe_.wait_ge(S['ident_ok'], 1)
            pe_.wait_ge(S['cls_norm'], 2)
            transpose(p_T, cls_n, P, 'clsT')
            pe_.wait_ge(S['cls_qT'], 1)
            mm(p_mm[:, 0:C], [tT[:, c] for c in range(CC)], [w_gq[:, c] for c in range(CC)], 'cls_q')

            def xh_transpose(r, m):
                k = CELLS * r + m
                pe_.wait_ge(S['norm_ok'], k + 1)
                if k >= 2:
                    pe_.wait_ge(S['xT_out'], k - 1)
                transpose(p_xhT[:, k % 2], pe[:, r % 2, m], TOK_M[r], 'xT_ok')

            def kv(r, m):
                M, k = TOK_M[r], CELLS * r + m
                pe_.wait_ge(S['xT_out'], k + 1)
                if k >= KV_SLOTS:
                    pe_.wait_ge(S['v_out'], k - KV_SLOTS + 1)
                if k == 0:
                    pe_.wait_ge(S['gamma_in'], 6)
                    pe_.wait_ge(S['bias_out'], 3)
                mm(p_kv[0:M, k % KV_SLOTS], [xhT[:, k % XHT_SLOTS, c, 0:M] for c in range(CC)],
                   [w_kv[:, c] for c in range(CC)], 'kv_ok')

            for it in range(ITER):
                s, r, w = it, it - 1, it - 3
                for n in range(CELLS + 3):
                    if s < STEPS and n < CELLS:
                        M, k = TOK_M[s], CELLS * s + n
                        if n == 0:
                            pe_.wait_ge(x_in[s % 2], 16 * KCH * (s // 2 + 1))
                        if k >= CONV_SLOTS:
                            pe_.wait_ge(S['pe_out'], k - CONV_SLOTS + 1)
                        mm(p_conv[0:M, k % CONV_SLOTS, 0:C], [xcols[:, s % 2, j, n * M:(n + 1) * M] for j in range(KCH)],
                           [w_conv[:, j] for j in range(KCH)], 'conv_ok')
                    if 0 <= w < STEPS:
                        M = TOK_M[w]
                        if n == 0:
                            pe_.wait_ge(S['agg_ok'], w + 1)
                            transpose(p_T, agg, M, 'aggT_ok')
                            pe_.wait_ge(S['aggT_out'], w + 1)
                            mm(p_mm[0:M, 0:C], [tT[:, c, 0:M] for c in range(CC)], [w_proj[:, c] for c in range(CC)],
                               'proj_ok')
                        if n == 2:
                            pe_.wait_ge(S['lo_ok'], w + 1)
                            pe_.wait_ge(S['qT_out'], min(r + 1, STEPS))
                            transpose(p_T, lo, M, 'loT_ok')
                        if n == 3:
                            pe_.wait_ge(S['loT_out'], w + 1)
                            pe_.wait_ge(S['q_ok'], min(r + 1, STEPS))
                            mm(p_mm[0:M, 0:C], [tT[:, c, 0:M] for c in range(CC)], [w_mod[:, c] for c in range(CC)],
                               'mod_ok')
                        if n == 4:
                            pe_.wait_ge(S['tn_ok'], w + 1)
                            transpose(p_T, ln_lo, M, 'tnT_ok')
                        if n == 6:
                            pe_.wait_ge(S['tnT_out'], w + 1)
                            pe_.wait_ge(S['patch_ok'], w + 1)
                            mm(p_mm[0:M], [tT[:, c, 0:M] for c in range(CC)], [w_gkv[:, c] for c in range(CC)],
                               'gkv_ok')
                    if 0 <= r < STEPS:
                        M = TOK_M[r]
                        if n == 1:
                            pe_.wait_ge(S['qn_ok'], r + 1)
                            transpose(p_T, qn, M, 'qT_ok')
                            xh_transpose(r, 0)
                        if n == 2:
                            pe_.wait_ge(S['qT_out'], r + 1)
                            if w >= 0:
                                pe_.wait_ge(S['lo_ok'], min(w + 1, STEPS))
                            if r == 0:
                                pe_.wait_ge(S['gamma_in'], 6)
                                pe_.wait_ge(S['dve_1'], 5)
                            mm(p_mm[0:M, 0:C], [smT[:, c, 0:M] for c in range(CC)], [w_q[:, c] for c in range(CC)],
                               'q_mm')
                        if n >= 3:
                            if n - 2 < CELLS:
                                xh_transpose(r, n - 2)
                            kv(r, n - 3)
            pe_.wait_ge(S['c_agg'], 1)
            transpose(p_T, agg, IMAGES, 'cT_ok')
            pe_.wait_ge(S['cT_out'], 1)
            pe_.wait_ge(S['g_ok'], 2 * STEPS)
            mm(p_mm[0:IMAGES, 0:C], [tT[:, c, 0:IMAGES] for c in range(CC)], [w_gproj[:, c] for c in range(CC)],
               'c_mm')


class Group:

    def __init__(self, c, pair=0):
        self.c, self.pair, self.half = c, pair, c % 2

    def plus(self, n):
        return Group(self.c + n, self.pair)

    def after(self, per_group, k):
        n = per_group * self.c + k + 1
        return n if isinstance(self.pair, int) else self.pair * (2 * per_group) + n

    def uses(self, inc, back=0):
        n = inc * (self.c // 2 + 1 - back)
        return n if isinstance(self.pair, int) else self.pair * inc + n

    def index(self, scale=1):
        n = self.c * scale
        return n if isinstance(self.pair, int) else self.pair * (2 * scale) + n


def run_iterations(engine, body, first=-1, last=GROUPS, loop=(2, GROUPS - 2)):
    lo, hi = loop
    hi = lo + (hi - lo) // 2 * 2

    def one(i, group):
        body(group, i + 1 < GROUPS, 0 <= i < GROUPS, i >= 1)

    for i in range(first, lo):
        one(i, Group(i))
    with engine.Fori(0, (hi - lo) // 2) as pair:
        for n in range(2):
            one(lo, Group(lo + n, pair))
    for i in range(hi, last + 1):
        one(i, Group(i))


A_AT = {1: [('xT', 0)], 2: [('qk', 0)], 4: [('xT', 1)], 5: [('qk', 1)], 7: [('qkT', 0)], 8: [('xT', 2)],
        9: [('qk', 2)], 11: [('qkT', 1)], 12: [('v', 0)], 13: [('v', 1)], 14: [('qkT', 2)], 15: [('v', 2), ('v', 3)]}
C_AT = {0: [('proj', 0)], 2: [('yT', 0)], 3: [('ffn', 0)], 4: [('proj', 1)], 6: [('yT', 1)], 7: [('ffn', 1)],
        8: [('proj', 2)], 9: [('twT', 0)], 10: [('yT', 2)], 11: [('ffn', 2)], 12: [('lora', 0)], 13: [('twT', 1)],
        14: [('lora', 1)], 15: [('twT', 2), ('lora', 2)]}
NORM_AT = {0: 0, 2: 1, 6: 2}
K_AT = {12: 0, 15: 1}
A_BANK = [s for h in sorted(A_AT) for s in A_AT[h]]
C_BANK = [s for h in sorted(C_AT) for s in C_AT[h]]


def attention_ffn(nc, io, h_dram, out_flat):
    with ExitStack() as ctx:
        def sb(name, shape, dt=F32):
            return ctx.enter_context(nc.sbuf_tensor(name, shape, dt))

        def ps(name, shape, dt=F32):
            return ctx.enter_context(nc.psum_tensor(name, shape, dt))

        def sem(name):
            return ctx.enter_context(nc.semaphore(name))

        ident = sb("ident", [P, P])
        ident_b = sb("ident_b", [P, P], BF16)
        w_qk = sb("w_qk", [P, CC, 2 * C])
        w_v = sb("w_v", [P, CC, C])
        w_p = sb("w_p", [P, CC, C])
        w_f = sb("w_f", [P, CC, FFN_N])
        right = sb("right", [LR, C])
        b_rows = sb("b_rows", [P, 2, C])
        w_mean = sb("w_mean", [P, CC, 2 * HEADS])
        rope_in = sb("rope_in", [TP, TILES, 2, HD])
        rope_g = sb("rope_g", [TP, 8, HD])
        rope_s = sb("rope_s", [TP, 7, HD])
        tabs = sb("tabs", [TP, 3, TILES, 2 * C])
        earlier = sb("earlier", [TP, EXPERTS, EXPERTS])
        eps5 = sb("eps5", [P, 1])
        eps6 = sb("eps6", [P, 1])

        ha = sb("ha", [TP, 2, TILES, C])
        hc = sb("hc", [TP, 2, TILES, C])
        a_st, a_mv = sb("a_st", [TP, 2, 6]), sb("a_mv", [TP, 2, 3])
        a_ln, a_rs = sb("a_ln", [TP, 2]), sb("a_rs", [TP, 2])
        xn = sb("xn", [TP, 2, C])
        xnT = sb("xnT", [P, 2, CC, GT])
        sq = sb("sq", [TP, 2 * C])
        ss, ss_ln, ss_rs = sb("ss", [TP, 2, 2 * HEADS]), sb("ss_ln", [TP, 2 * HEADS]), sb("ss_rs", [TP, 2, 2 * HEADS])
        t1, t2 = sb("t1", [TP, 2, 2 * C]), sb("t2", [TP, 2, 2 * C])
        qkT = sb("qkT", [P, 2, 4, GT + QP - SEQ])
        kb = sb("kb", [P, 2, 2, HALF, GT])
        vp = sb("vp", [QP, 2, GB, HEADS, 2 * HD])
        mx = sb("mx", [QP, 2, HALF], BF16)
        pr = sb("pr", [QP, 2, 2, 4 * SEQ])
        prT = sb("prT", [QP, 2, HALF, SEQ])
        oT = sb("oT", [P, 4, SEQ])
        rd = sb("rd", [SEQ, HEADS])
        on = sb("on", [QP, C])
        onT = sb("onT", [P, 2, CC, GT])
        hb, h2, h2l = sb("hb", [TP, C]), sb("h2", [TP, 2, C]), sb("h2l", [TP, 3, C])
        c_st, c_mv = sb("c_st", [TP, 6]), sb("c_mv", [TP, 3])
        c_ln, c_rs = sb("c_ln", [TP, 1]), sb("c_rs", [TP, 1])
        yn = sb("yn", [TP, C])
        yT = sb("yT", [P, CC, TP])
        f = sb("f", [TP, 3, FFN_N])
        g_max, g_e, g_sum, g_rs = sb("g_max", [TP, 1]), sb("g_e", [TP, EXPERTS]), sb("g_sum", [TP, 1]), sb("g_rs", [TP, 1])
        g_gt, g_eq = sb("g_gt", [TP, EXPERTS, EXPERTS]), sb("g_eq", [TP, EXPERTS, EXPERTS])
        g_rank, g_w = sb("g_rank", [TP, EXPERTS]), sb("g_w", [TP, EXPERTS])
        tw = sb("tw", [TP, 2, LR])
        twT = sb("twT", [LR, TP])
        out_sb = sb("out_sb", [TP, 3, C])

        p_s = ps("p_s", [P, 2, 2, 512])
        p_o = ps("p_o", [P, 512])
        p_n = ps("p_n", [P, 512])
        p_a = ps("p_a", [P, 512])
        p_c = ps("p_c", [P, 512])

        names = ("w_in setup ident_ok rope_in w_ok tab_ok dve_a dve_n dve_r dve_c dve_g act_a act_r act_c act_g pool_r pool_1 "
                 "a_var a_rstd xn_ok xT xT_out qk sq_ok ss_ok ss_rstd rot_ok rope_ok qkT_ok qkT_out v_mm v_out "
                 "s_mm s_max s_shift s_exp pT pT_out pv o_out oN o_norm oB oB_out "
                 "proj h2_ok c_var c_rstd yn_ok yT_ok yT_out ffn ffn_out g_m g_exp tw_ok twT_ok twT_out lora out_ok "
                 "hb_ok h2l_ok fb_ok").split()
        S = {n: sem("b_" + n) for n in names}
        ha_in = [sem("ha_in0"), sem("ha_in1")]
        hc_in = [sem("hc_in0"), sem("hc_in1")]
        k_in = [[sem(f"k_in{h}{n}") for n in range(2)] for h in range(2)]
        stored = [sem(f"stored{t}") for t in range(TILES)]
        block = ctx.enter_context(nc.Block())

        h_group = h_dram.rearrange("(g t p) c -> g p t c", t=TILES, p=TP)
        out_group = out_flat.rearrange("(g t p) c -> g t p c", t=TILES, p=TP)
        K_COLS = [(0, 2 * TP), (2 * TP, GT)]

        def pick(view, g):
            return view[g.index()] if isinstance(g.pair, int) else view[bass.ds(g.index(), 1)].squeeze(0)

        @block.sync
        def _(sp):
            def value(x):
                return x if isinstance(x, int) else sp.snap(x)

            def load(dst, g, landed, sem_=None, done=None):
                src = pick(h_group, g)
                if sem_ is not None:
                    sp.wait_ge(sem_, done)
                sp.dma_start(dst[:, g.half], src).then_inc(landed[g.half], 16)

            for dst, src in ((w_qk, io['w_qkv'][:, 0:2 * C]), (w_v, io['w_qkv'][:, 2 * C:3 * C]),
                             (w_p, io['w_proj']), (w_f, io['w_ffn'])):
                sp.dma_start(dst[:], src.rearrange("(k p) n -> p k n", p=P)).then_inc(S['w_in'], 16)
            sp.dma_start(right[:], io['right']).then_inc(S['w_in'], 16)
            sp.dma_start(b_rows[:], io['rows'][6:8].unsqueeze(0).broadcast_to([P, 2, C])).then_inc(S['w_in'], 16)
            sp.dma_start(rope_in[:], io['rope']).then_inc(S['rope_in'], 16)
            sp.dma_start(rope_g[:], io['rope_g'].unsqueeze(0).broadcast_to([TP, 8, HD])).then_inc(S['rope_in'], 16)
            load(ha, Group(0), ha_in)

            def iteration(i, A, B, C_):
                g = i.plus(2)
                if i.c + 2 < GROUPS:
                    if i.c >= 0:
                        load(ha, g, ha_in, S['xn_ok'], value(i.after(3, 2)))
                    else:
                        load(ha, g, ha_in)
                if B:
                    if i.c >= 2:
                        load(hc, i, hc_in, S['hb_ok'], value(i.plus(-2).after(3, 2)))
                    else:
                        load(hc, i, hc_in)
                for h in range(16):
                    if A and h in K_AT:
                        n, g = K_AT[h], i.plus(1)
                        c0, c1 = K_COLS[n]
                        sp.wait_ge(S['qkT_out'], g.after(3, n + 1))
                        for k in range(2):
                            for hh in range(HALF):
                                r = slice(HD * hh, HD * hh + HD)
                                sp.dma_start(kb[r, g.half, k, hh, c0:c1],
                                             qkT[r, g.half, 2 + k, c0:c1]).then_inc(k_in[g.half][n], 16)
                    if C_:
                        for step, t in C_AT.get(h, []):
                            if step == 'lora':
                                g = i.plus(-1)
                                dst = out_group[g.index(), t] if isinstance(g.pair, int) else \
                                    out_group[bass.ds(g.index(), 1), t].squeeze(0)
                                sp.wait_ge(S['out_ok'], value(g.after(3, t)))
                                sp.dma_start(dst, out_sb[:, t]).then_inc(stored[t], 16)

            run_iterations(sp, iteration)
            for t in range(TILES):
                sp.wait_ge(stored[t], 16 * GROUPS)

        @block.gpsimd
        def _(pool):
            link = counted(pool, S['pool_1'])
            link(nc.gpsimd.memset(ident[:], 0.0))
            link(nc.gpsimd.memset(ident_b[:], 0.0))
            link(nc.gpsimd.memset(earlier[:], 1.0))
            link(nc.gpsimd.memset(kb[:], 0.0))
            for m in (ident, ident_b):
                link(nc.gpsimd.affine_select(out=m[:], in_=m[:], compare_op=ALU.not_equal, fill=1.0, base=0,
                                             pattern=[[-1, P]], channel_multiplier=1))
            link(nc.gpsimd.affine_select(out=earlier[:], in_=earlier[:], compare_op=ALU.is_gt, fill=0.0, base=0,
                                         pattern=[[1, EXPERTS], [-1, EXPERTS]], channel_multiplier=0))
            link(nc.gpsimd.memset(qkT[:, :, :, GT:], 0.0))
            link(nc.gpsimd.memset(on[64:QP], 0.0))
            link(nc.gpsimd.memset(prT[64:QP], 0.0))
            link(nc.gpsimd.memset(vp[:, :, :, :, HD:], 1.0))
            link(nc.gpsimd.memset(vp[64:QP], 0.0))
            link(nc.gpsimd.memset(vp[64:SEQ, :, :, :, HD:], 1.0))
            nc.gpsimd.memset(eps5[:], 1e-5).then_inc(S['setup'], 1)
            nc.gpsimd.memset(eps6[:], 1e-6).then_inc(S['setup'], 1)

            def iteration(i, A, B, C_):
                for h in range(16):
                    if A:
                        for step, t in A_AT.get(h - 1, []):
                            if step == 'qk':
                                g, b = i.plus(1), t % 2
                                pool.wait_ge(S['rot_ok'], g.after(6, 2 * t + 1))
                                nc.gpsimd.tensor_tensor(t1[:, b], t1[:, b], t2[:, b], ALU.add).then_inc(S['pool_r'], 1)
                                pool.wait_ge(S['pool_r'], g.after(6, 2 * t))
                                pool.wait_ge(S['ss_rstd'], g.after(3, t))
                                x = t1[:, b].rearrange("p (h d) -> p h d", d=HD)
                                nc.gpsimd.tensor_tensor(x, x, ss_rs[:, b].unsqueeze(2).broadcast_to([TP, 2 * HEADS, HD]),
                                                        ALU.mult).then_inc(S['pool_r'], 1)
                                pool.wait_ge(S['pool_r'], g.after(6, 2 * t + 1))
                                nc.gpsimd.tensor_tensor(t1[:, b], t1[:, b], tabs[:, 2, t],
                                                        ALU.add).then_inc(S['rope_ok'], 1)
                    if C_:
                        g = i.plus(-1)
                        for step, t in C_AT.get(h, []):
                            if step == 'proj':
                                if t == 0:
                                    pool.wait_ge(hc_in[g.half], g.uses(16))
                                if t > 0 or i.c > 1:
                                    pool.wait_ge(S['h2_ok'], g.after(3, t - 1))
                                nc.gpsimd.tensor_tensor(hb[:], hc[:, g.half, t], b_rows[0:TP, 0],
                                                        ALU.add).then_inc(S['hb_ok'], 1)
                            if step == 'yT':
                                pool.wait_ge(S['h2_ok'], g.after(3, t))
                                nc.gpsimd.tensor_tensor(h2l[:, t], h2[:, t % 2], b_rows[0:TP, 1],
                                                        ALU.add).then_inc(S['h2l_ok'], 1)
                            if step == 'ffn':
                                pool.wait_ge(S['ffn_out'], g.after(3, t))
                                pool.wait_ge(S['h2l_ok'], g.after(3, t))
                                nc.gpsimd.tensor_tensor(h2l[:, t], h2l[:, t], f[:, t, 0:C],
                                                        ALU.add).then_inc(S['fb_ok'], 1)

            run_iterations(pool, iteration)

        @block.scalar
        def _(act):
            act.preload_act_table_set("natural_log_exp_and_others")
            act.wait_ge(S['setup'], 2)

            def iteration(i, A, B, C_):
                def pT_out(g, u):
                    act.wait_ge(S['pT'], g.after(UNITS, u))
                    src = p_s[0:SEQ, u % 2, :, 0:4 * QP].rearrange("p x (h q) -> p x h q", q=QP)[:, :, :, 0:SEQ]
                    nc.scalar.copy(prT[0:SEQ, u % 2].rearrange("p (x h) q -> p x h q", x=2), src).then_inc(S['pT_out'], 1)

                def part_a(h):
                    g = i.plus(1)
                    if h in NORM_AT:
                        t = NORM_AT[h]
                        act.wait_ge(S['a_var'], g.after(3, t))
                        nc.scalar.activation(a_ln[:, t % 2:t % 2 + 1], a_mv[:, t % 2, 1:2], ACT.Ln,
                                             bias=eps5[0:TP, 0:1]).then_inc(S['act_a'], 1)
                        act.wait_ge(S['act_a'], g.after(3, t))
                        nc.scalar.activation(a_rs[:, t % 2:t % 2 + 1], a_ln[:, t % 2:t % 2 + 1], ACT.Exp,
                                             scale=-0.5).then_inc(S['a_rstd'], 1)
                    for step, t in A_AT.get(h, []):
                        c0 = t * TP
                        if step == 'xT':
                            act.wait_ge(S['xT'], g.after(3, t))
                            nc.scalar.copy(xnT[:, g.half, :, c0:c0 + TP],
                                           p_a[:, 0:CC * TP].rearrange("p (c n) -> p c n", c=CC)).then_inc(S['xT_out'], 1)
                        if step == 'qk':
                            act.wait_ge(S['qk'], g.after(3, t))
                            nc.scalar.activation(sq[:], p_a[0:TP, :], ACT.Square).then_inc(S['sq_ok'], 1)
                        if step == 'qkT':
                            act.wait_ge(S['qkT_ok'], g.after(3, t))
                            nc.scalar.copy(qkT[:, g.half, :, c0:c0 + TP],
                                           p_a[:, 0:4 * TP].rearrange("p (c n) -> p c n", c=4)).then_inc(S['qkT_out'], 1)
                        if step == 'v':
                            act.wait_ge(S['v_mm'], g.after(GB, t))
                            nc.scalar.copy(vp[0:SEQ, g.half, t, :, 0:HD],
                                           p_a[0:SEQ, 0:C].rearrange("p (h d) -> p h d", d=HD)).then_inc(S['v_out'], 1)
                    for step, t in A_AT.get(h - 1, []):
                        if step == 'qk':
                            act.wait_ge(S['ss_ok'], g.after(3, t))
                            nc.scalar.activation(ss_ln[:], ss[:, t % 2], ACT.Ln, bias=eps6[0:TP, 0:1],
                                                 scale=1.0 / HD).then_inc(S['act_r'], 1)
                            act.wait_ge(S['act_r'], g.after(3, t))
                            nc.scalar.activation(ss_rs[:, t % 2], ss_ln[:], ACT.Exp, scale=-0.5).then_inc(S['ss_rstd'], 1)

                def part_c(h):
                    g = i.plus(-1)
                    for step, t in C_AT.get(h, []):
                        if step == 'yT':
                            act.wait_ge(S['yT_ok'], g.after(3, t))
                            nc.scalar.copy(yT[:], p_c[:, 0:CC * TP].rearrange("p (c n) -> p c n", c=CC)
                                           ).then_inc(S['yT_out'], 1)
                        if step == 'ffn':
                            act.wait_ge(S['ffn'], g.after(3, t))
                            nc.scalar.copy(f[:, t], p_c[0:TP, 0:FFN_N]).then_inc(S['ffn_out'], 1)
                        if step == 'twT':
                            act.wait_ge(S['twT_ok'], g.after(3, t))
                            nc.scalar.copy(twT[:], p_c[0:LR, 0:TP]).then_inc(S['twT_out'], 1)
                    for step, t in C_AT.get(h - 1, []):
                        if step == 'proj':
                            act.wait_ge(S['c_var'], g.after(3, t))
                            nc.scalar.activation(c_ln[:], c_mv[:, 1:2], ACT.Ln, bias=eps5[0:TP, 0:1]).then_inc(S['act_c'], 1)
                            act.wait_ge(S['act_c'], g.after(3, t))
                            nc.scalar.activation(c_rs[:], c_ln[:], ACT.Exp, scale=-0.5).then_inc(S['c_rstd'], 1)
                        if step == 'ffn':
                            act.wait_ge(S['g_m'], g.after(3, t))
                            nc.scalar.activation(g_e[:], f[:, t, C + LR:FFN_N], ACT.Exp, bias=g_max[:, 0:1],
                                                 accum_out=g_sum[:, 0:1]).then_inc(S['g_exp'], 1)

                for h in range(16):
                    u, even = h // 2, h % 2 == 0
                    if even:
                        if u % 2 == 1 and (B or u == 1):
                            g, b = (i, (u - 3) // 2) if u > 1 else (i.plus(-1), GB - 1)
                            if B and u > 1 or C_ and u == 1:
                                act.wait_ge(S['pv'], g.after(UNITS, 2 * b + 1))
                                nc.scalar.copy(oT[:], p_o[:, 0:4 * SEQ].rearrange("p (c q) -> p c q", c=4)
                                               ).then_inc(S['o_out'], 1)
                        if u % 2 == 0:
                            g, b = (i, (u - 4) // 2) if u > 2 else (i.plus(-1), GB - 2 + u // 2)
                            if B and u > 2 or C_ and u <= 2:
                                act.wait_ge(S['oB'], g.after(GB, b))
                                nc.scalar.copy(onT[:, g.half, :, b * SEQ:(b + 1) * SEQ],
                                               p_n[:, 0:CC * QP].rearrange("p (c q) -> p c q", c=CC)[:, :, 0:SEQ]
                                               ).then_inc(S['oB_out'], 1)
                    elif B:
                        act.wait_ge(S['s_shift'], i.after(UNITS, u))
                        nc.scalar.activation(pr[:, u % 2], p_s[0:QP, u % 2, :, 0:4 * SEQ], ACT.Exp,
                                             scale=HD ** -0.5).then_inc(S['s_exp'], 1)
                    if A:
                        part_a(h)
                    if C_:
                        part_c(h)
                    if even:
                        if B and u > 0:
                            pT_out(i, u - 1)
                        if C_ and u == 0:
                            pT_out(i.plus(-1), UNITS - 1)

            run_iterations(act, iteration)

        @block.vector
        def _(dve):
            link = counted(dve, S['dve_a'])
            dve.wait_ge(S['w_in'], 16 * 6)
            w4 = w_qk[:].rearrange("p c (h d) -> p c h d", d=HD)
            link(nc.vector.reduce_sum(w_mean[:], w4, AX_X))
            link(nc.vector.tensor_scalar(w_mean[:], w_mean[:], 1.0 / HD, None, ALU.mult))
            for c in range(CC):
                nc.vector.tensor_tensor(w4[:, c], w4[:, c], w_mean[:, c].unsqueeze(2).broadcast_to([P, 2 * HEADS, HD]),
                                        ALU.subtract).then_inc(S['w_ok'], 1)
            dve.wait_ge(S['rope_in'], 32)
            for t in range(TILES):
                for k in range(2):
                    cos, sin = rope_in[:, t, 0], rope_in[:, t, 1]
                    link(nc.vector.tensor_tensor(rope_s[:, k], cos, rope_g[:, k], ALU.mult))
                    link(nc.vector.tensor_tensor(rope_s[:, 2 + k], sin, rope_g[:, 2 + k], ALU.mult))
                    link(nc.vector.tensor_tensor(rope_s[:, 4 + k], cos, rope_g[:, 4 + k], ALU.mult))
                    link(nc.vector.tensor_tensor(rope_s[:, 6], sin, rope_g[:, 6 + k], ALU.mult))
                    link(nc.vector.tensor_tensor(rope_s[:, 4 + k], rope_s[:, 4 + k], rope_s[:, 6], ALU.add))
                    for n in range(3):
                        nc.vector.tensor_copy(
                            tabs[:, n, t, k * C:(k + 1) * C].rearrange("p (h d) -> p h d", d=HD),
                            rope_s[:, 2 * n + k].unsqueeze(1).broadcast_to([TP, HEADS, HD])).then_inc(S['tab_ok'], 1)
                dve.wait_ge(S['tab_ok'], 6 * (t + 1))
            dve.wait_ge(S['setup'], 2)

            def iteration(i, A, B, C_):
                def a_norm(g, t):
                    b = t % 2
                    if t == 0:
                        dve.wait_ge(ha_in[g.half], g.uses(16))
                    nc.vector.bn_stats(a_st[:, b], ha[:, g.half, t]).then_inc(S['dve_r'], 1)
                    dve.wait_ge(S['dve_r'], g.after(3, t))
                    nc.vector.tensor_copy(a_mv[:, b, 2:3], a_st[:, b, 0:1])
                    nc.vector.bn_aggr(a_mv[:, b, 0:2], a_st[:, b]).then_inc(S['a_var'], 1)
                    dve.wait_ge(S['a_rstd'], g.after(3, t))
                    if g.c * 3 + t >= 2:
                        dve.wait_ge(S['xT'], g.after(3, t - 2))
                    nc.vector.tensor_scalar(xn[:, b], ha[:, g.half, t], a_mv[:, b, 0:1], a_rs[:, b:b + 1],
                                            ALU.subtract, ALU.mult).then_inc(S['xn_ok'], 1)

                def rotate(g, t):
                    b = t % 2
                    dve.wait_ge(S['sq_ok'], g.after(3, t))
                    if g.c * 3 + t >= 2:
                        dve.wait_ge(S['qkT_ok'], g.after(3, t - 2))
                    x = p_a[0:TP, :]
                    nc.vector.tensor_tensor(t1[:, b], x, tabs[:, 0, t], ALU.mult)
                    x4 = x.rearrange("p (h s d) -> p h s d", s=2, d=HD // 2)
                    o4 = t2[:, b].rearrange("p (h s d) -> p h s d", s=2, d=HD // 2)
                    w4_ = tabs[:, 1, t].rearrange("p (h s d) -> p h s d", s=2, d=HD // 2)
                    for s in range(2):
                        nc.vector.tensor_tensor(o4[:, :, s], x4[:, :, 1 - s], w4_[:, :, s],
                                                ALU.mult).then_inc(S['rot_ok'], 1)
                    nc.vector.reduce_sum(ss[:, b], sq[:].rearrange("p (h d) -> p h d", d=HD), AX_X).then_inc(S['ss_ok'], 1)

                def part_c(h):
                    g = i.plus(-1)
                    for step, t in C_AT.get(h, []):
                        if step == 'proj':
                            dve.wait_ge(S['proj'], g.after(3, t))
                            dve.wait_ge(S['hb_ok'], g.after(3, t))
                            if t > 1 or i.c > 1:
                                dve.wait_ge(S['h2l_ok'], g.after(3, t - 2))
                            nc.vector.tensor_tensor(h2[:, t % 2], p_c[0:TP, 0:C], hb[:], ALU.add).then_inc(S['h2_ok'], 1)
                            dve.wait_ge(S['h2_ok'], g.after(3, t))
                            nc.vector.bn_stats(c_st[:], h2[:, t % 2]).then_inc(S['dve_c'], 1)
                            dve.wait_ge(S['dve_c'], g.after(3, t))
                            nc.vector.tensor_copy(c_mv[:, 2:3], c_st[:, 0:1])
                            nc.vector.bn_aggr(c_mv[:, 0:2], c_st[:]).then_inc(S['c_var'], 1)
                        if step == 'lora':
                            dve.wait_ge(S['lora'], g.after(3, t))
                            dve.wait_ge(S['fb_ok'], g.after(3, t))
                            if i.c > 1:
                                n = g.after(1, -1)
                                dve.wait_ge(stored[t], n * 16)
                            nc.vector.tensor_tensor(out_sb[:, t], p_c[0:TP, 0:C], h2l[:, t], ALU.add).then_inc(S['out_ok'], 1)
                    for step, t in C_AT.get(h - 1, []):
                        if step == 'proj':
                            dve.wait_ge(S['c_rstd'], g.after(3, t))
                            if t > 0 or i.c > 1:
                                dve.wait_ge(S['yT_ok'], g.after(3, t - 1))
                            nc.vector.tensor_scalar(yn[:], h2[:, t % 2], c_mv[:, 0:1], c_rs[:, 0:1],
                                                    ALU.subtract, ALU.mult).then_inc(S['yn_ok'], 1)
                        if step == 'ffn':
                            gate(g, t)

                def gate(g, t):
                    steps = 6
                    done = [0]

                    def then(ins):
                        ins.then_inc(S['dve_g'], 1)
                        dve.wait_ge(S['dve_g'], g.after(3 * steps, steps * t + done[0]))
                        done[0] += 1

                    dve.wait_ge(S['ffn_out'], g.after(3, t))
                    lg = f[:, t, C + LR:FFN_N]
                    nc.vector.reduce_max(g_max[:], lg, AX_X, negate=True).then_inc(S['g_m'], 1)
                    by_e = lg.unsqueeze(2).broadcast_to([TP, EXPERTS, EXPERTS])
                    by_j = lg.unsqueeze(1).broadcast_to([TP, EXPERTS, EXPERTS])
                    nc.vector.tensor_tensor(g_gt[:], by_j, by_e, ALU.is_gt)
                    then(nc.vector.tensor_tensor(g_eq[:], by_j, by_e, ALU.is_equal))
                    then(nc.vector.tensor_tensor(g_eq[:], g_eq[:], earlier[:], ALU.mult))
                    then(nc.vector.tensor_tensor(g_gt[:], g_gt[:], g_eq[:], ALU.add))
                    then(nc.vector.reduce_sum(g_rank[:], g_gt[:], AX_X))
                    dve.wait_ge(S['g_exp'], g.after(3, t))
                    then(nc.vector.scalar_tensor_tensor(g_w[:], g_rank[:], 2.0, g_e[:], ALU.is_lt, ALU.mult))
                    then(nc.vector.reciprocal(g_rs[:], g_sum[:]))
                    if t > 1 or i.c > 1:
                        dve.wait_ge(S['twT_ok'], g.after(3, t - 2))
                    nc.vector.scalar_tensor_tensor(
                        tw[:, t % 2].rearrange("p (e r) -> p e r", r=RANK),
                        f[:, t, C:C + LR].rearrange("p (e r) -> p e r", r=RANK), g_rs[:, 0:1],
                        g_w[:].unsqueeze(2).broadcast_to([TP, EXPERTS, RANK]), ALU.mult, ALU.mult).then_inc(S['tw_ok'], 1)
                    assert done[0] == steps

                for h in range(16):
                    u, even = h // 2, h % 2 == 0
                    if even and B:
                        dve.wait_ge(S['s_mm'], i.after(UNITS, u))
                        if i.c * UNITS + u >= 2:
                            dve.wait_ge(S['s_shift'], i.after(UNITS, u - 2))
                        nc.vector.reduce_max(mx[:, u % 2].rearrange("p (x h) -> p x h", x=2),
                                             p_s[0:QP, u % 2, :, 0:4 * SEQ].rearrange("p x (h k) -> p x h k", k=SEQ),
                                             AX_X, negate=True).then_inc(S['s_max'], 1)
                    if not even and u % 2 == 1:
                        g, b = (i, (u - 3) // 2) if u > 1 else (i.plus(-1), GB - 1)
                        if B and u > 1 or C_ and u == 1:
                            dve.wait_ge(S['oN'], g.after(GB, b))
                            o3 = p_n[0:SEQ, :].rearrange("p (h e) -> p h e", e=2 * HD)
                            nc.vector.reciprocal(rd[:], o3[:, :, HD]).then_inc(S['dve_n'], 1)
                            dve.wait_ge(S['dve_n'], g.after(GB, b))
                            nc.vector.tensor_tensor(on[0:SEQ].rearrange("p (h d) -> p h d", d=HD), o3[:, :, 0:HD],
                                                    rd[:].unsqueeze(2).broadcast_to([SEQ, HEADS, HD]),
                                                    ALU.mult).then_inc(S['o_norm'], 1)
                    if A and h in NORM_AT:
                        a_norm(i.plus(1), NORM_AT[h])
                    if A:
                        for step, t in A_AT.get(h, []):
                            if step == 'qk':
                                rotate(i.plus(1), t)
                    if C_:
                        part_c(h)

            run_iterations(dve, iteration)

        @block.tensor
        def _(pe):
            pe.wait_ge(S['setup'], 2)
            pe.wait_ge(S['w_ok'], CC)
            pe.wait_ge(S['tab_ok'], 6 * TILES)

            def mm(out, lhs, rhs, done=None):
                for c, (a, b) in enumerate(zip(lhs, rhs)):
                    last = nc.tensor.matmul(out, a, b, start=(c == 0), stop=(c == len(lhs) - 1))
                if done is not None:
                    last.then_inc(done, 1)
                return last

            A_FREE = {'xT': ('xT_out', 3), 'qk': ('rot_ok', 6), 'qkT': ('qkT_out', 3), 'v': ('v_out', GB)}
            C_FREE = {'proj': ('h2_ok', 3), 'yT': ('yT_out', 3), 'ffn': ('ffn_out', 3), 'twT': ('twT_out', 3),
                      'lora': ('out_ok', 3)}

            def wait_bank(order, free, g, item, first):
                n = order.index(item)
                if n == 0 and first:
                    return
                step, t = order[n - 1]
                name, per = free[step]
                k = 2 * t + 1 if name == 'rot_ok' else t
                pe.wait_ge(S[name], (g if n else g.plus(-1)).after(per, k))

            def iteration(i, A, B, C_):
                def part_a(h):
                    g = i.plus(1)
                    for step, t in A_AT.get(h, []):
                        wait_bank(A_BANK, A_FREE, g, (step, t), g.c == 0)
                        c0 = t * TP
                        if step == 'xT':
                            pe.wait_ge(S['xn_ok'], g.after(3, t))
                            for c in range(CC):
                                last = nc.tensor.transpose(p_a[:, c * TP:(c + 1) * TP], xn[:, t % 2, c * P:(c + 1) * P],
                                                           ident[0:TP, 0:TP])
                            last.then_inc(S['xT'], 1)
                        if step == 'qk':
                            pe.wait_ge(S['xT_out'], g.after(3, t))
                            mm(p_a[0:TP, :], [xnT[:, g.half, c, c0:c0 + TP] for c in range(CC)],
                               [w_qk[:, c] for c in range(CC)], S['qk'])
                        if step == 'qkT':
                            pe.wait_ge(S['rope_ok'], g.after(3, t))
                            for c in range(4):
                                last = nc.tensor.transpose(p_a[:, c * TP:(c + 1) * TP], t1[:, t % 2, c * P:(c + 1) * P],
                                                           ident[0:TP, 0:TP])
                            last.then_inc(S['qkT_ok'], 1)
                        if step == 'v':
                            mm(p_a[0:SEQ, 0:C], [xnT[:, g.half, c, t * SEQ:(t + 1) * SEQ] for c in range(CC)],
                               [w_v[:, c] for c in range(CC)], S['v_mm'])

                def part_c(h):
                    g = i.plus(-1)
                    for step, t in C_AT.get(h, []):
                        wait_bank(C_BANK, C_FREE, g, (step, t), g.c == 0)
                        c0 = t * TP
                        if step == 'proj':
                            pe.wait_ge(S['oB_out'], g.after(GB, min(t + 1, GB - 1)))
                            mm(p_c[0:TP, 0:C], [onT[:, g.half, c, c0:c0 + TP] for c in range(CC)],
                               [w_p[:, c] for c in range(CC)], S['proj'])
                        if step == 'yT':
                            pe.wait_ge(S['yn_ok'], g.after(3, t))
                            for c in range(CC):
                                last = nc.tensor.transpose(p_c[:, c * TP:(c + 1) * TP], yn[:, c * P:(c + 1) * P],
                                                           ident[0:TP, 0:TP])
                            last.then_inc(S['yT_ok'], 1)
                        if step == 'ffn':
                            pe.wait_ge(S['yT_out'], g.after(3, t))
                            mm(p_c[0:TP, 0:FFN_N], [yT[:, c] for c in range(CC)], [w_f[:, c] for c in range(CC)],
                               S['ffn'])
                        if step == 'twT':
                            pe.wait_ge(S['tw_ok'], g.after(3, t))
                            nc.tensor.transpose(p_c[0:LR, 0:TP], tw[:, t % 2], ident[0:TP, 0:TP]).then_inc(S['twT_ok'], 1)
                        if step == 'lora':
                            pe.wait_ge(S['twT_out'], g.after(3, t))
                            mm(p_c[0:TP, 0:C], [twT[:]], [right[:]], S['lora'])

                def scores(u):
                    b, k = u // 2, u % 2
                    if k == 0 and b == 0:
                        pe.wait_ge(k_in[i.half][0], i.uses(16 * HEADS))
                    if k == 0 and b == 2:
                        pe.wait_ge(k_in[i.half][1], i.uses(16 * HEADS))
                    if i.c * UNITS + u >= 2:
                        pe.wait_ge(S['pT_out'], i.after(UNITS, u - 2))
                    for x in range(2):
                        last = nc.tensor.matmul(p_s[0:QP, u % 2, x, 0:4 * SEQ], qkT[:, i.half, k, b * SEQ:b * SEQ + QP],
                                                kb[:, i.half, k, 4 * x:4 * x + 4, b * SEQ:(b + 1) * SEQ],
                                                start=True, stop=False, skip_group_check=True)
                    last.then_inc(S['s_mm'], 1)

                def shift(u):
                    pe.wait_ge(S['s_max'], i.after(UNITS, u))
                    for x in range(2):
                        last = nc.tensor.matmul(p_s[0:QP, u % 2, x, 0:4 * SEQ], ident_b[0:QP, 0:QP],
                                                mx[:, u % 2, 4 * x:4 * x + 4].unsqueeze(2).broadcast_to([QP, 4, SEQ]),
                                                start=False, stop=True, skip_group_check=True)
                    last.then_inc(S['s_shift'], 1)

                def transpose_probs(g, u):
                    pe.wait_ge(S['s_exp'], g.after(UNITS, u))
                    for x in range(2):
                        for n in range(4):
                            last = nc.tensor.transpose(p_s[0:SEQ, u % 2, x, n * QP:(n + 1) * QP],
                                                       pr[:, u % 2, x, n * SEQ:(n + 1) * SEQ], ident[0:QP, 0:QP])
                    last.then_inc(S['pT'], 1)

                def weigh_values(g, u):
                    b, k = u // 2, u % 2
                    pe.wait_ge(S['pT_out'], g.after(UNITS, u))
                    if k == 0 and not (b == 0 and g.c == 0):
                        pe.wait_ge(S['o_out'], g.after(GB, b - 1))
                    for n in range(HALF):
                        c, j = 2 * k + n // 4, n % 4
                        last = nc.tensor.matmul(p_o[32 * j:32 * j + 32, c * SEQ:(c + 1) * SEQ],
                                                vp[:, g.half, b, HALF * k + n, :], prT[:, u % 2, n, :],
                                                start=True, stop=True)
                    last.then_inc(S['pv'], 1)

                for h in range(16):
                    u, even = h // 2, h % 2 == 0
                    out_of = None
                    if u % 2 == 1:
                        if u > 1 and B:
                            out_of = (i, (u - 3) // 2)
                        if u == 1 and C_:
                            out_of = (i.plus(-1), GB - 1)
                    before = (i, u - 1) if u > 0 else (i.plus(-1), UNITS - 1)
                    has_before = B if u > 0 else C_
                    if even:
                        if B:
                            scores(u)
                    elif B:
                        shift(u)
                    if A:
                        part_a(h)
                    if C_:
                        part_c(h)
                    if even:
                        if has_before:
                            transpose_probs(*before)
                        if out_of:
                            g, b = out_of
                            pe.wait_ge(S['o_out'], g.after(GB, b))
                            if not (g.c == 0 and b == 0):
                                pe.wait_ge(S['oB_out'], g.after(GB, b - 1))
                            for c in range(4):
                                last = nc.tensor.transpose(p_n[0:SEQ, c * P:(c + 1) * P], oT[:, c], ident[:])
                            last.then_inc(S['oN'], 1)
                    else:
                        if has_before:
                            weigh_values(*before)
                        if out_of:
                            g, b = out_of
                            pe.wait_ge(S['o_norm'], g.after(GB, b))
                            for c in range(CC):
                                last = nc.tensor.transpose(p_n[:, c * QP:(c + 1) * QP], on[:, c * P:(c + 1) * P],
                                                           ident[0:QP, 0:QP])
                            last.then_inc(S['oB'], 1)

            run_iterations(pe, iteration)


def build(nc, io, out):
    h_dram = nc.dram_tensor("h_tokens", [IMAGES * SEQ, C], F32).ap()
    patch_dram = nc.dram_tensor("patch_tokens", [ALL_W, C], F32).ap()
    gv_dram = nc.dram_tensor("class_values", [ALL_W, C], F32).ap()
    gs_dram = nc.dram_tensor("class_scores", [ALL_W, LH], F32).ap()
    patch_tokens(nc, io, h_dram, patch_dram, gv_dram, gs_dram)
    attention_ffn(nc, io, h_dram, out.rearrange("b s c -> (b s) c"))


def arrays_of(inputs):
    a = {k.replace('L0_tok_', '').replace('L0_attn_', '').replace('L0_ffn_', ''): np.asarray(v)
         for k, v in inputs.items()}
    side = PATCH * GRID * GRID
    x = a['x'][:, :, :side, :side].reshape(IMAGES, 3, GRID, GRID, PATCH, GRID, GRID, PATCH)
    x = x.transpose(1, 4, 7, 0, 2, 5, 3, 6).reshape(PIXELS, ALL_W, CELLS)
    x_cols = np.zeros((STEPS, KROWS * KCH, CELLS * P), x.dtype)
    for s, m in enumerate(TOK_M):
        part = x[:, P * s:P * s + m, :].transpose(0, 2, 1)
        x_cols[s, :PIXELS, :CELLS * m] = part.reshape(PIXELS, CELLS * m)
    conv_w = np.zeros((KROWS * KCH, C), a['conv_w'].dtype)
    conv_w[:PIXELS] = a['conv_w'].reshape(C, PIXELS).T
    vec = {**a, 'b_lin': a['b_lin']}
    half = HD // 2
    rope_g = np.stack([a['q_gamma'], a['k_gamma'], np.roll(a['q_gamma'], half), np.roll(a['k_gamma'], half),
                       a['q_beta'], a['k_beta'], np.roll(a['q_beta'], half), np.roll(a['k_beta'], half)])
    inv = (1.0 / 10000.0 ** (np.arange(half, dtype=np.float32) / half)).astype(np.float32)
    ang = np.outer(np.arange(GT) % SEQ, inv).astype(np.float32)
    sin = np.concatenate([-np.sin(ang), np.sin(ang)], axis=1)
    cos = np.concatenate([np.cos(ang), np.cos(ang)], axis=1)
    rope = np.stack([cos, sin]).reshape(2, TILES, TP, HD).transpose(2, 1, 0, 3)
    wf = np.concatenate([a['W_lin'].T, a['left'].transpose(1, 0, 2).reshape(C, LR), a['gate_w'].T], axis=1)
    out = {
        'x_cols': x_cols, 'conv_w': conv_w, 'txt': a['txt'],
        'rows': np.stack([vec[r] for r in ROWS]),
        'cols': np.stack([vec[c] for c in COLS]).reshape(len(COLS), CC, P).transpose(2, 0, 1),
        'w_qkv': a['w_qkv'].T, 'w_proj': a['w_proj'].T, 'w_ffn': wf, 'right': a['right'].reshape(LR, C),
        'rope_g': rope_g, 'rope': rope.astype(np.float32),
    }
    for n in ('la_wq', 'la_wkv', 'la_proj_w', 'ga_wq', 'ga_wkv', 'ga_proj_w', 'mod_w'):
        out[n] = a[n]
    return {k: np.ascontiguousarray(v) for k, v in out.items()}


def kernel(**inputs):
    import concourse.bacc as bacc
    from concourse.bass_utils import run_bass_kernel_spmd

    arrays = arrays_of(inputs)
    nc = bacc.Bacc("TRN2", target_bir_lowering=False, num_devices=1)
    io = {k: nc.dram_tensor("in_" + k, v.shape, mybir.dt.from_np(v.dtype), kind="ExternalInput").ap()
          for k, v in arrays.items()}
    out = nc.dram_tensor("out", (IMAGES, SEQ, C), F32, kind="ExternalOutput").ap()
    build(nc, io, out)
    r = run_bass_kernel_spmd(nc, [{"in_" + k: v for k, v in arrays.items()}], core_ids=[0])
    return r.results[0]["out"]
```

```python
import numpy as np
import concourse.bass as bass
import concourse.mybir as mybir
from contextlib import ExitStack

F32 = mybir.dt.float32
BF16 = mybir.dt.bfloat16
ALU = mybir.AluOpType
ACT = mybir.ActivationFunctionType
AX_X = mybir.AxisListType.X

P = 128
C = 256
CC = C // P
IMAGES = 64
PATCH = 14
GRID = 3
WINDOWS = GRID * GRID
CELLS = GRID * GRID
TXT = 77
SEQ = WINDOWS + 1 + TXT
ALL_W = IMAGES * WINDOWS

PIXELS = 3 * PATCH * PATCH
KROWS = 120
KCH = -(-PIXELS // KROWS)
STEPS = -(-ALL_W // P)
TOK_M = [min(P, ALL_W - P * s) for s in range(STEPS)]
LH, LD = 8, 32
FIRST_CELLS = 2
CONV_SLOTS, XHT_SLOTS, KV_SLOTS = 2, 3, 2

HEADS, HD = 16, 16
GB = 4
GROUPS = IMAGES // GB
GT = GB * SEQ
TILES = 3
TP = GT // TILES
QP = 96
HALF = HEADS // 2
UNITS = 2 * GB
SPARE = 4 * QP
EXPERTS, RANK = 8, 4
LR = EXPERTS * RANK
FFN_N = C + LR + EXPERTS

ROWS = ['la_proj_b', 'class_emb', 'ga_ln_q_g', 'ga_ln_q_b', 'ga_proj_b', 'mod_b', 'b_proj', 'b_lin']
COLS = ['la_ln_q_g', 'la_ln_kv_g', 'ga_ln_kv_g', 'la_ln_q_b', 'la_ln_kv_b', 'ga_ln_kv_b']


def counted(engine, semaphore, start=0):
    n = [start]

    def link(instruction):
        n[0] = n[0] + 1
        instruction.then_inc(semaphore, 1)
        engine.wait_ge(semaphore, n[0])
        return instruction

    return link


class Constants:

    def __init__(self, nc, ctx):
        def sb(name, shape, dt=F32):
            return ctx.enter_context(nc.sbuf_tensor(name, shape, dt))

        self.ident = sb("ident", [P, P])
        self.ident_b = sb("ident_b", [P, P], BF16)
        self.w_qk = sb("w_qk", [P, CC, 2 * C])
        self.w_v = sb("w_v", [P, CC, C])
        self.w_p = sb("w_p", [P, CC, C])
        self.w_f = sb("w_f", [P, CC, FFN_N])
        self.right = sb("right", [TILES * LR, TILES, C])
        self.b_rows = sb("b_rows", [P, 2, C])
        self.w_mean = sb("w_mean", [P, CC, 2 * HEADS])
        self.rope_in = sb("rope_in", [TP, TILES, 2, HD])
        self.rope_g = sb("rope_g", [TP, 8, HD])
        self.rope_s = sb("rope_s", [TP, 7, HD])
        self.tabs = sb("tabs", [TP, 3, TILES, 2 * C])
        self.earlier = sb("earlier", [TP, EXPERTS, EXPERTS])
        self.eps5 = sb("eps5", [P, 1])
        self.eps6 = sb("eps6", [P, 1])
        names = "w_in rope_in w_ok tab_ok zeroed right_in dve_k pool_k"
        self.S = {n: ctx.enter_context(nc.semaphore("k_" + n)) for n in names.split()}

    def load(self, nc, sp, io):
        for dst, src in ((self.w_qk, io['w_qkv'][:, 0:2 * C]), (self.w_v, io['w_qkv'][:, 2 * C:3 * C]),
                         (self.w_p, io['w_proj']), (self.w_f, io['w_ffn'])):
            sp.dma_start(dst[:], src.rearrange("(k p) n -> p k n", p=P)).then_inc(self.S['w_in'], 16)
        sp.dma_start(self.b_rows[:], io['rows'][6:8].unsqueeze(0).broadcast_to([P, 2, C])).then_inc(self.S['w_in'], 16)
        sp.dma_start(self.rope_in[:], io['rope']).then_inc(self.S['rope_in'], 16)
        sp.dma_start(self.rope_g[:], io['rope_g'].unsqueeze(0).broadcast_to([TP, 8, HD])).then_inc(self.S['rope_in'], 16)
        sp.wait_ge(self.S['zeroed'], 1)
        for t in range(TILES):
            sp.dma_start(self.right[LR * t:LR * (t + 1), t], io['right']).then_inc(self.S['right_in'], 16)

    def loaded(self, sp):
        sp.wait_ge(self.S['w_in'], 16 * 5)
        sp.wait_ge(self.S['right_in'], 16 * TILES)

    def fill(self, nc, pool):
        link = counted(pool, self.S['pool_k'])
        nc.gpsimd.memset(self.right[:], 0.0).then_inc(self.S['zeroed'], 1)
        link(nc.gpsimd.memset(self.ident_b[:], 0.0))
        link(nc.gpsimd.affine_select(out=self.ident_b[:], in_=self.ident_b[:], compare_op=ALU.not_equal, fill=1.0,
                                     base=0, pattern=[[-1, P]], channel_multiplier=1))
        link(nc.gpsimd.memset(self.earlier[:], 1.0))
        link(nc.gpsimd.affine_select(out=self.earlier[:], in_=self.earlier[:], compare_op=ALU.is_gt, fill=0.0, base=0,
                                     pattern=[[1, EXPERTS], [-1, EXPERTS]], channel_multiplier=0))
        link(nc.gpsimd.memset(self.eps5[:], 1e-5))
        link(nc.gpsimd.memset(self.eps6[:], 1e-6))

    def centre(self, nc, dve):
        link = counted(dve, self.S['dve_k'])
        dve.wait_ge(self.S['w_in'], 16 * 5)
        w4 = self.w_qk[:].rearrange("p c (h d) -> p c h d", d=HD)
        link(nc.vector.reduce_sum(self.w_mean[:], w4, AX_X))
        link(nc.vector.tensor_scalar(self.w_mean[:], self.w_mean[:], 1.0 / HD, None, ALU.mult))
        for c in range(CC):
            nc.vector.tensor_tensor(w4[:, c], w4[:, c], self.w_mean[:, c].unsqueeze(2).broadcast_to([P, 2 * HEADS, HD]),
                                    ALU.subtract).then_inc(self.S['w_ok'], 1)

    def table(self, nc, dve, t, k):
        unit = 2 * t + k
        link = counted(dve, self.S['dve_k'], 2 + 5 * unit)
        dve.wait_ge(self.S['rope_in'], 32)
        if unit:
            dve.wait_ge(self.S['tab_ok'], 3 * unit)
        rope_s, rope_g = self.rope_s, self.rope_g
        cos, sin = self.rope_in[:, t, 0], self.rope_in[:, t, 1]
        link(nc.vector.tensor_tensor(rope_s[:, k], cos, rope_g[:, k], ALU.mult))
        link(nc.vector.tensor_tensor(rope_s[:, 2 + k], sin, rope_g[:, 2 + k], ALU.mult))
        link(nc.vector.tensor_tensor(rope_s[:, 4 + k], cos, rope_g[:, 4 + k], ALU.mult))
        link(nc.vector.tensor_tensor(rope_s[:, 6], sin, rope_g[:, 6 + k], ALU.mult))
        link(nc.vector.tensor_tensor(rope_s[:, 4 + k], rope_s[:, 4 + k], rope_s[:, 6], ALU.add))
        for n in range(3):
            nc.vector.tensor_copy(
                self.tabs[:, n, t, k * C:(k + 1) * C].rearrange("p (h d) -> p h d", d=HD),
                rope_s[:, 2 * n + k].unsqueeze(1).broadcast_to([TP, HEADS, HD])).then_inc(self.S['tab_ok'], 1)


def patch_tokens(nc, io, consts, h_dram, patch_dram, gv_dram, gs_dram):
    with ExitStack() as ctx:
        def sb(name, shape, dt=F32):
            return ctx.enter_context(nc.sbuf_tensor(name, shape, dt))

        def sem(name):
            return ctx.enter_context(nc.semaphore(name))

        def row(name):
            return rows[:, ROWS.index(name), :]

        ident = consts.ident
        xcols = sb("xcols", [KROWS, 2, KCH, CELLS * P])
        w_conv = sb("w_conv", [KROWS, KCH, C])
        w_q = sb("w_q", [P, CC, C])
        w_kv = sb("w_kv", [P, CC, 2 * C])
        w_proj = sb("w_proj", [P, CC, C])
        w_gq = sb("w_gq", [P, CC, C])
        w_gkv = sb("w_gkv", [P, CC, 2 * C])
        w_gproj = sb("w_gproj", [P, CC, C])
        w_mod = sb("w_mod", [P, CC, C])
        rows = sb("rows", [P, len(ROWS), C])
        cols = sb("cols", [P, len(COLS), CC])
        beta_wide = sb("beta_wide", [P, 3, CC, P])
        eps = sb("eps1", [P, 1])
        bias_q = sb("bias_q", [P, C])
        bias_kv = sb("bias_kv", [P, 2 * C])
        bias_gkv = sb("bias_gkv", [P, 2 * C])
        gq = sb("gq", [P, C])
        gq_kb = sb("gq_kb", [P, LH])
        cls_n = sb("cls_n", [P, C])
        pe = sb("pe", [P, 2, CELLS, C])
        stats = sb("stats", [P, 2, CELLS, 6])
        mv = sb("mv", [P, 2, CELLS, 2])
        rstd = sb("rstd", [P, 2, CELLS])
        lnv = sb("lnv", [P, CELLS])
        red = sb("red", [P, 3, C])
        qn = sb("qn", [P, C])
        s_stats = sb("s_stats", [P, 6])
        s_mv = sb("s_mv", [P, 2])
        s_rstd = sb("s_rstd", [P, 1])
        s_lnv = sb("s_lnv", [P, 1])
        smT = sb("smT", [P, CC, P])
        q = sb("q", [P, C])
        q_kb = sb("q_kb", [P, 2, LH])
        xhT = sb("xhT", [P, XHT_SLOTS, CC, P])
        prod = sb("prod", [P, C])
        score = sb("score", [P, 2, CELLS, LH])
        v = sb("v", [P, 2, CELLS, C])
        attn = sb("attn", [P, CELLS, LH])
        smax = sb("smax", [P, LH])
        ssum = sb("ssum", [P, LH])
        vw = sb("vw", [P, CELLS, C])
        agg = sb("agg", [P, C])
        redb = sb("redb", [P, C])
        lo = sb("lo", [P, C])
        ln_lo = sb("ln_lo", [P, C])
        patch = sb("patch", [P, C])
        gs = sb("gs", [P, LH])
        gv = sb("gv", [P, C])
        t_stats = sb("t_stats", [P, 6])
        t_mv = sb("t_mv", [P, 2])
        t_rstd = sb("t_rstd", [P, 1])
        t_lnv = sb("t_lnv", [P, 1])
        tT = sb("tT", [P, CC, P])
        cls_gv = sb("cls_gv", [IMAGES, WINDOWS, C])
        cls_gs = sb("cls_gs", [IMAGES, WINDOWS, LH])
        cls_out = sb("cls_out", [IMAGES, C])
        p_conv = ctx.enter_context(nc.psum_tensor("p_conv", [P, CONV_SLOTS, 2 * C], F32))
        p_xhT = ctx.enter_context(nc.psum_tensor("p_xhT", [P, 2, 4, P], F32))
        p_kv = ctx.enter_context(nc.psum_tensor("p_kv", [P, KV_SLOTS, 2 * C], F32))
        p_T = ctx.enter_context(nc.psum_tensor("p_T", [P, 4, P], F32))
        p_mm = ctx.enter_context(nc.psum_tensor("p_mm", [P, 2 * C], F32))

        names = ("w_in v_in wc_in x_first ident_ok consts beta_ok bias_mm bias_out gamma_in cls_norm clsT cls_qT cls_q "
                 "conv_ok pe_out stat_ok rstd_ok norm_ok red_ok qv_ok qr_ok qn_ok qT_ok qT_out q_mm q_ok "
                 "xT_ok xT_out kv_ok k_read v_out score_ok m_ok e_ok att_ok vw_ok agg_ok aggT_ok aggT_out proj_ok "
                 "lo_ok loT_ok loT_out mod_ok patch_ok tv_ok tr_ok tn_ok tnT_ok tnT_out gkv_ok g_ok redb_ok "
                 "c_in c_max c_exp c_att c_agg cT_ok cT_out c_mm c_out gq_ok dve_1 act_1 pool_1").split()
        S = {n: sem(n) for n in names}
        x_in = [sem("x_in0"), sem("x_in1")]
        st_patch = [sem("st_patch0"), sem("st_patch1")]
        st_g = [sem("st_g0"), sem("st_g1")]
        st_cls = sem("st_cls")
        block = ctx.enter_context(nc.Block())
        weights = [(w_q, 'la_wq'), (w_kv, 'la_wkv'), (w_gq, 'ga_wq'), (w_gkv, 'ga_wkv'),
                   (w_proj, 'la_proj_w'), (w_gproj, 'ga_proj_w'), (w_mod, 'mod_w')]
        ITER = STEPS + 3

        @block.sync
        def _(sp):
            def load_x(s):
                m = CELLS * TOK_M[s]
                if s >= 2:
                    sp.wait_ge(S['conv_ok'], CELLS * (s - 1))
                c0 = 0
                if s == 0:
                    c0 = FIRST_CELLS * P
                    sp.dma_start(xcols[:, 0, :, 0:c0], io['x_cols'][0, :, 0:c0].rearrange("(k p) m -> p k m", p=KROWS)
                                 ).then_inc(S['x_first'], 16)
                for k in range(KCH):
                    src = io['x_cols'][s, KROWS * k:KROWS * (k + 1), c0:m]
                    sp.dma_start(xcols[:, s % 2, k, c0:m], src).then_inc(x_in[s % 2], 16)

            h_rows = h_dram.rearrange("(b s) c -> b s c", s=SEQ)
            sp.dma_start(w_conv[:], io['conv_w'].rearrange("(k p) n -> p k n", p=KROWS)).then_inc(S['wc_in'], 16)
            load_x(0)
            sp.dma_start(cols[:], io['cols']).then_inc(S['v_in'], 16)
            sp.dma_start(rows[:], io['rows'].unsqueeze(0).broadcast_to([P, len(ROWS), C])).then_inc(S['v_in'], 16)
            for w, name in weights:
                sp.dma_start(w[:], io[name].rearrange("(k p) n -> p k n", p=P)).then_inc(S['w_in'], 16)
            load_x(1)
            consts.load(nc, sp, io)
            sp.dma_start(h_rows[:, WINDOWS + 1:, :], io['txt']).then_inc(st_cls, 16)
            for it in range(1, ITER + 1):
                if it + 1 < STEPS:
                    load_x(it + 1)
                w = it - 3
                if 0 <= w < STEPS:
                    M, w0 = TOK_M[w], P * w
                    sp.wait_ge(S['patch_ok'], w + 1)
                    sp.dma_start(patch_dram[w0:w0 + M, :], patch[0:M, :]).then_inc(st_patch[w % 2], 16)
                    sp.wait_ge(S['g_ok'], 2 * (w + 1))
                    sp.dma_start(gv_dram[w0:w0 + M, :], gv[0:M, :]).then_inc(st_g[w % 2], 16)
                    sp.dma_start(gs_dram[w0:w0 + M, :], gs[0:M, :]).then_inc(st_g[w % 2], 16)
            for h in range(2):
                n = len(range(h, STEPS, 2))
                sp.wait_ge(st_patch[h], 16 * n)
                sp.wait_ge(st_g[h], 32 * n)
            sp.dma_start(h_rows[:, 0:WINDOWS, :], patch_dram.rearrange("(b n) c -> b n c", n=WINDOWS)
                         ).then_inc(st_cls, 16)
            sp.dma_start(cls_gv[:], gv_dram.rearrange("(b n) c -> b n c", n=WINDOWS)).then_inc(S['c_in'], 16)
            sp.dma_start(cls_gs[:], gs_dram.rearrange("(b n) h -> b n h", n=WINDOWS)).then_inc(S['c_in'], 16)
            sp.wait_ge(S['c_out'], 1)
            sp.dma_start(h_rows[:, WINDOWS, :], cls_out[:]).then_inc(st_cls, 16)
            sp.wait_ge(st_cls, 48)
            consts.loaded(sp)

        @block.gpsimd
        def _(pool):
            link = counted(pool, S['pool_1'])
            link(nc.gpsimd.memset(ident[:], 0.0))
            nc.gpsimd.affine_select(out=ident[:], in_=ident[:], compare_op=ALU.not_equal, fill=1.0, base=0,
                                    pattern=[[-1, P]], channel_multiplier=1).then_inc(S['ident_ok'], 1)
            nc.gpsimd.memset(eps[:], 1e-5).then_inc(S['consts'], 1)
            consts.fill(nc, pool)
            for it in range(ITER):
                s, u = it, it - 2
                for n in range(1, CELLS):
                    if s < STEPS:
                        M, k = TOK_M[s], (CELLS - 1) * s + n
                        pool.wait_ge(S['pe_out'], CELLS * s + n + 1)
                        first = pe[0:M, s % 2, 0] if n == 1 else red[0:M, s % 3]
                        nc.gpsimd.tensor_tensor(red[0:M, s % 3], first, pe[0:M, s % 2, n],
                                                ALU.add).then_inc(S['red_ok'], 1)
                        pool.wait_ge(S['red_ok'], k)
                    if n != 4 or not 0 <= u < STEPS:
                        continue
                    M = TOK_M[u]
                    pool.wait_ge(S['att_ok'], u + 1)
                    pool.wait_ge(S['v_out'], CELLS * (u + 1))
                    if u >= 1:
                        pool.wait_ge(S['agg_ok'], u)
                    nc.gpsimd.tensor_tensor(
                        vw[0:M].rearrange("p n (h d) -> p (n h) d", h=LH),
                        v[0:M, u % 2].rearrange("p n (h d) -> p (n h) d", h=LH),
                        attn[0:M].rearrange("p n h -> p (n h)").unsqueeze(2).broadcast_to([M, CELLS * LH, LD]),
                        ALU.mult).then_inc(S['vw_ok'], 1)
                    if u >= 1:
                        pool.wait_ge(S['lo_ok'], u)
                    pool.wait_ge(S['v_in'], 32)
                    nc.gpsimd.tensor_tensor(redb[0:M], red[0:M, u % 3], row('la_proj_b')[0:M],
                                            ALU.add).then_inc(S['redb_ok'], 1)

        @block.scalar
        def _(act):
            link = counted(act, S['act_1'])
            act.preload_act_table_set("natural_log_exp_and_others")
            act.wait_ge(S['consts'], 1)

            def rstd_of(M, var, tmp, out, signal):
                link(nc.scalar.activation(tmp, var, ACT.Ln, bias=eps[0:M, 0:1]))
                nc.scalar.activation(out, tmp, ACT.Exp, scale=-0.5).then_inc(S[signal], 1)

            for it in range(ITER):
                s, r, u, w = it, it - 1, it - 2, it - 3
                for n in range(CELLS + 3):
                    if it == 0 and n == 4:
                        act.wait_ge(S['cls_norm'], 1)
                        rstd_of(P, t_mv[:, 1:2], t_lnv[:], t_rstd[:], 'tr_ok')
                    if it == 0 and n == 8:
                        act.wait_ge(S['clsT'], 1)
                        nc.scalar.copy(tT[:], p_T[:, 0:CC]).then_inc(S['cls_qT'], 1)
                    if s < STEPS and n < CELLS:
                        M, k = TOK_M[s], CELLS * s + n
                        act.wait_ge(S['conv_ok'], k + 1)
                        if n == 0 and s >= 2:
                            act.wait_ge(S['xT_ok'], CELLS * (s - 1))
                        nc.scalar.copy(pe[0:M, s % 2, n], p_conv[0:M, k % CONV_SLOTS, 0:C]).then_inc(S['pe_out'], 1)
                    if 0 <= r < STEPS and n == 1:
                        M = TOK_M[r]
                        act.wait_ge(S['qv_ok'], r + 1)
                        rstd_of(M, s_mv[0:M, 1:2], s_lnv[0:M], s_rstd[0:M], 'qr_ok')
                    if 0 <= w < STEPS:
                        M = TOK_M[w]
                        if n == 4:
                            act.wait_ge(S['aggT_ok'], w + 1)
                            nc.scalar.copy(tT[:, :, 0:M], p_T[:, 0:CC, 0:M]).then_inc(S['aggT_out'], 1)
                        if n == 6:
                            act.wait_ge(S['tv_ok'], w + 1)
                            rstd_of(M, t_mv[0:M, 1:2], t_lnv[0:M], t_rstd[0:M], 'tr_ok')
                        if n == 6:
                            act.wait_ge(S['loT_ok'], w + 1)
                            nc.scalar.copy(tT[:, :, 0:M], p_T[:, 0:CC, 0:M]).then_inc(S['loT_out'], 1)
                        if n == 8:
                            act.wait_ge(S['tnT_ok'], w + 1)
                            nc.scalar.copy(tT[:, :, 0:M], p_T[:, 0:CC, 0:M]).then_inc(S['tnT_out'], 1)
                    if 0 <= r < STEPS and n == 2:
                        M = TOK_M[r]
                        act.wait_ge(S['qT_ok'], r + 1)
                        nc.scalar.copy(smT[:, :, 0:M], p_T[:, 0:CC, 0:M]).then_inc(S['qT_out'], 1)
                    if 0 <= r < STEPS and n >= 2 and n - 2 < CELLS:
                        M, m = TOK_M[r], n - 2
                        k = CELLS * r + m
                        act.wait_ge(S['xT_ok'], k + 1)
                        if k >= XHT_SLOTS:
                            act.wait_ge(S['kv_ok'], k - XHT_SLOTS + 1)
                        nc.scalar.copy(xhT[:, k % XHT_SLOTS, :, 0:M], p_xhT[:, k % 2, 0:CC, 0:M]).then_inc(S['xT_out'], 1)
                    if 0 <= r < STEPS and n >= 3:
                        M, m = TOK_M[r], n - 3
                        k = CELLS * r + m
                        act.wait_ge(S['k_read'], k + 1)
                        if m == 0 and r >= 2:
                            act.wait_ge(S['vw_ok'], r - 1)
                        nc.scalar.copy(v[0:M, r % 2, m], p_kv[0:M, k % KV_SLOTS, C:2 * C]).then_inc(S['v_out'], 1)
                    if 0 <= u < STEPS and n == 4:
                        M = TOK_M[u]
                        act.wait_ge(S['m_ok'], u + 1)
                        nc.scalar.activation(attn[0:M], attn[0:M], ACT.Exp).then_inc(S['e_ok'], 1)
                if s < STEPS:
                    M = TOK_M[s]
                    act.wait_ge(S['stat_ok'], CELLS * (s + 1))
                    rstd_of(M, mv[0:M, s % 2, :, 1], lnv[0:M], rstd[0:M, s % 2], 'rstd_ok')
            act.wait_ge(S['c_max'], 1)
            nc.scalar.activation(cls_gs[:], cls_gs[:], ACT.Exp).then_inc(S['c_exp'], 1)
            act.wait_ge(S['cT_ok'], 1)
            nc.scalar.copy(tT[:, :, 0:IMAGES], p_T[:, 0:CC, 0:IMAGES]).then_inc(S['cT_out'], 1)

        @block.vector
        def _(dve):
            link = counted(dve, S['dve_1'])

            def moments(M, x, st, m_v, signal):
                link(nc.vector.bn_stats(st, x))
                nc.vector.bn_aggr(m_v, st).then_inc(S[signal], 1)

            dve.wait_ge(S['v_in'], 32)
            for k in range(3):
                for c in range(CC):
                    nc.vector.tensor_copy(beta_wide[:, k, c],
                                          cols[:, 3 + k, c:c + 1].broadcast_to([P, P])).then_inc(S['beta_ok'], 1)
            moments(P, row('class_emb'), t_stats[:], t_mv[:], 'cls_norm')
            def setup(n):
                if n == 5:
                    dve.wait_ge(S['tr_ok'], 1)
                    link(nc.vector.tensor_scalar(cls_n[:], row('class_emb'), t_mv[:, 0:1], t_rstd[:, 0:1],
                                                 ALU.subtract, ALU.mult))
                    link(nc.vector.tensor_tensor(cls_n[:], cls_n[:], row('ga_ln_q_g'), ALU.mult))
                    nc.vector.tensor_tensor(cls_n[:], cls_n[:], row('ga_ln_q_b'), ALU.add).then_inc(S['cls_norm'], 1)
                if n == 6:
                    dve.wait_ge(S['bias_mm'], 1)
                    nc.vector.tensor_scalar(bias_q[:], p_kv[:, 0, 0:C], C ** -0.5, None,
                                            ALU.mult).then_inc(S['bias_out'], 1)
                    dve.wait_ge(S['bias_mm'], 2)
                    nc.vector.tensor_copy(bias_kv[:], p_kv[:, 1]).then_inc(S['bias_out'], 1)
                if n == 7:
                    dve.wait_ge(S['bias_mm'], 3)
                    nc.vector.tensor_copy(bias_gkv[:], p_kv[:, 0]).then_inc(S['bias_out'], 1)
                    for k, w in enumerate((w_q, w_kv, w_gkv)):
                        for c in range(CC):
                            nc.vector.tensor_scalar(w[:, c], w[:, c], cols[:, k, c:c + 1], None,
                                                    ALU.mult).then_inc(S['gamma_in'], 1)
                if n == 9:
                    dve.wait_ge(S['cls_q'], 1)
                    nc.vector.tensor_scalar(gq[:], p_mm[:, 0:C], C ** -0.5, None, ALU.mult).then_inc(S['gq_ok'], 1)
                    dve.wait_ge(S['gq_ok'], 1)
                    dve.wait_ge(S['bias_out'], 3)
                    link(nc.vector.tensor_tensor(prod[:], gq[:], bias_gkv[:, 0:C], ALU.mult))
                    link(nc.vector.reduce_sum(gq_kb[:], prod[:].rearrange("p (h d) -> p h d", h=LH), AX_X))

            def normalise(r, n):
                M = TOK_M[r]
                nc.vector.tensor_scalar(pe[0:M, r % 2, n], pe[0:M, r % 2, n], mv[0:M, r % 2, n, 0:1],
                                        rstd[0:M, r % 2, n:n + 1], ALU.subtract, ALU.mult).then_inc(S['norm_ok'], 1)

            for it in range(ITER):
                s, r, u, w = it, it - 1, it - 2, it - 3
                for n in range(CELLS + 3):
                    if it == 0:
                        setup(n)
                    if it == 4 and n == 0:
                        consts.centre(nc, dve)
                    if it == 4 and 0 < n <= 2 * TILES:
                        consts.table(nc, dve, (n - 1) // 2, (n - 1) % 2)
                    if s < STEPS and n < CELLS:
                        M, k = TOK_M[s], CELLS * s + n
                        dve.wait_ge(S['pe_out'], k + 1)
                        moments(M, pe[0:M, s % 2, n], stats[0:M, s % 2, n], mv[0:M, s % 2, n], 'stat_ok')
                    if 0 <= w < STEPS:
                        M = TOK_M[w]
                        if n == 5:
                            dve.wait_ge(S['proj_ok'], w + 1)
                            dve.wait_ge(S['redb_ok'], w + 1)
                            nc.vector.tensor_tensor(lo[0:M], p_mm[0:M, 0:C], redb[0:M], ALU.add).then_inc(S['lo_ok'], 1)
                            dve.wait_ge(S['lo_ok'], w + 1)
                            moments(M, lo[0:M], t_stats[0:M], t_mv[0:M], 'tv_ok')
                        if n == 6:
                            dve.wait_ge(S['tr_ok'], w + 2)
                            nc.vector.tensor_scalar(ln_lo[0:M], lo[0:M], t_mv[0:M, 0:1], t_rstd[0:M, 0:1],
                                                    ALU.subtract, ALU.mult).then_inc(S['tn_ok'], 1)
                        if n == 7:
                            dve.wait_ge(S['mod_ok'], w + 1)
                            if w >= 1:
                                dve.wait_ge(st_patch[(w - 1) % 2], 16 * ((w - 1) // 2 + 1))
                            nc.vector.tensor_tensor(patch[0:M], p_mm[0:M, 0:C], row('mod_b')[0:M],
                                                    ALU.add).then_inc(S['patch_ok'], 1)
                        if n == 10:
                            dve.wait_ge(S['gkv_ok'], w + 1)
                            link(nc.vector.tensor_tensor(prod[0:M], p_mm[0:M, 0:C], gq[0:M], ALU.mult))
                            if w >= 1:
                                dve.wait_ge(st_g[(w - 1) % 2], 32 * ((w - 1) // 2 + 1))
                            link(nc.vector.reduce_sum(gs[0:M], prod[0:M].rearrange("p (h d) -> p h d", h=LH), AX_X))
                            nc.vector.tensor_tensor(gs[0:M], gs[0:M], gq_kb[0:M], ALU.add).then_inc(S['g_ok'], 1)
                            nc.vector.tensor_tensor(gv[0:M], p_mm[0:M, C:2 * C], bias_gkv[0:M, C:2 * C],
                                                    ALU.add).then_inc(S['g_ok'], 1)
                            dve.wait_ge(S['g_ok'], 2 * (w + 1))
                    if 0 <= r < STEPS:
                        M = TOK_M[r]
                        if n == 0:
                            dve.wait_ge(S['rstd_ok'], r + 1)
                            dve.wait_ge(S['red_ok'], (CELLS - 1) * (r + 1))
                        if n < 3:
                            for m in range(3 * n, 3 * n + 3):
                                normalise(r, m)
                        if n == 0:
                            link(nc.vector.tensor_scalar(red[0:M, r % 3], red[0:M, r % 3], 1.0 / CELLS, None, ALU.mult))
                            moments(M, red[0:M, r % 3], s_stats[0:M], s_mv[0:M], 'qv_ok')
                        if n == 1:
                            dve.wait_ge(S['qr_ok'], r + 1)
                            if r >= 1:
                                dve.wait_ge(S['qT_ok'], r)
                            nc.vector.tensor_scalar(qn[0:M], red[0:M, r % 3], s_mv[0:M, 0:1], s_rstd[0:M, 0:1],
                                                    ALU.subtract, ALU.mult).then_inc(S['qn_ok'], 1)
                        if n == 3:
                            dve.wait_ge(S['q_mm'], r + 1)
                            nc.vector.scalar_tensor_tensor(q[0:M], p_mm[0:M, 0:C], C ** -0.5, bias_q[0:M],
                                                           ALU.mult, ALU.add).then_inc(S['q_ok'], 1)
                            dve.wait_ge(S['q_ok'], r + 1)
                            link(nc.vector.tensor_tensor(prod[0:M], q[0:M], bias_kv[0:M, 0:C], ALU.mult))
                            link(nc.vector.reduce_sum(q_kb[0:M, r % 2], prod[0:M].rearrange("p (h d) -> p h d", h=LH),
                                                      AX_X))
                        if n >= 3:
                            m = n - 3
                            k = CELLS * r + m
                            dve.wait_ge(S['kv_ok'], k + 1)
                            nc.vector.tensor_tensor(prod[0:M], p_kv[0:M, k % KV_SLOTS, 0:C], q[0:M],
                                                    ALU.mult).then_inc(S['k_read'], 1)
                            dve.wait_ge(S['k_read'], k + 1)
                            nc.vector.reduce_sum(score[0:M, r % 2, m], prod[0:M].rearrange("p (h d) -> p h d", h=LH),
                                                 AX_X).then_inc(S['score_ok'], 1)
                            dve.wait_ge(S['score_ok'], k + 1)
                    if 0 <= u < STEPS:
                        M = TOK_M[u]
                        if n == 2:
                            dve.wait_ge(S['score_ok'], CELLS * (u + 1))
                            if u >= 1:
                                dve.wait_ge(S['vw_ok'], u)
                            link(nc.vector.tensor_tensor(attn[0:M], score[0:M, u % 2],
                                                         q_kb[0:M, u % 2].unsqueeze(1).broadcast_to([M, CELLS, LH]),
                                                         ALU.add))
                            link(nc.vector.reduce_max(smax[0:M], attn[0:M].rearrange("p n h -> p h n"), AX_X))
                            nc.vector.tensor_tensor(attn[0:M], attn[0:M],
                                                    smax[0:M].unsqueeze(1).broadcast_to([M, CELLS, LH]),
                                                    ALU.subtract).then_inc(S['m_ok'], 1)
                        if n == 5:
                            dve.wait_ge(S['e_ok'], u + 1)
                            link(nc.vector.reduce_sum(ssum[0:M], attn[0:M].rearrange("p n h -> p h n"), AX_X))
                            link(nc.vector.reciprocal(ssum[0:M], ssum[0:M]))
                            nc.vector.tensor_tensor(attn[0:M], attn[0:M],
                                                    ssum[0:M].unsqueeze(1).broadcast_to([M, CELLS, LH]),
                                                    ALU.mult).then_inc(S['att_ok'], 1)
                        if n == 8:
                            dve.wait_ge(S['vw_ok'], u + 1)
                            link(nc.vector.reduce_sum(agg[0:M], vw[0:M].rearrange("p n c -> p c n"), AX_X))
                            nc.vector.tensor_tensor(agg[0:M], agg[0:M], bias_kv[0:M, C:2 * C],
                                                    ALU.add).then_inc(S['agg_ok'], 1)
            M = IMAGES
            dve.wait_ge(S['c_in'], 32)
            link(nc.vector.reduce_max(smax[0:M], cls_gs[:].rearrange("p n h -> p h n"), AX_X))
            nc.vector.tensor_tensor(cls_gs[:], cls_gs[:], smax[0:M].unsqueeze(1).broadcast_to([M, WINDOWS, LH]),
                                    ALU.subtract).then_inc(S['c_max'], 1)
            dve.wait_ge(S['c_exp'], 1)
            link(nc.vector.reduce_sum(ssum[0:M], cls_gs[:].rearrange("p n h -> p h n"), AX_X))
            link(nc.vector.reciprocal(ssum[0:M], ssum[0:M]))
            link(nc.vector.tensor_tensor(
                cls_gv[:].rearrange("p n (h d) -> p (n h) d", h=LH), cls_gv[:].rearrange("p n (h d) -> p (n h) d", h=LH),
                cls_gs[:].rearrange("p n h -> p (n h)").unsqueeze(2).broadcast_to([M, WINDOWS * LH, LD]), ALU.mult))
            link(nc.vector.reduce_sum(agg[0:M], cls_gv[:].rearrange("p n c -> p c n"), AX_X))
            nc.vector.tensor_tensor(agg[0:M].rearrange("p (h d) -> p h d", h=LH),
                                    agg[0:M].rearrange("p (h d) -> p h d", h=LH),
                                    ssum[0:M].unsqueeze(2).broadcast_to([M, LH, LD]), ALU.mult).then_inc(S['c_agg'], 1)
            link(nc.vector.tensor_tensor(lo[0:M], row('class_emb')[0:M], row('ga_proj_b')[0:M], ALU.add))
            dve.wait_ge(S['c_mm'], 1)
            nc.vector.tensor_tensor(cls_out[:], p_mm[0:M, 0:C], lo[0:M], ALU.add).then_inc(S['c_out'], 1)

        @block.tensor
        def _(pe_):
            def mm(out, lhs, rhs, signal=None):
                for c, (a, b) in enumerate(zip(lhs, rhs)):
                    last = nc.tensor.matmul(out, a, b, start=(c == 0), stop=(c == len(lhs) - 1))
                if signal:
                    last.then_inc(S[signal], 1)

            def transpose(out, x, M, signal):
                for c in range(CC):
                    last = nc.tensor.transpose(out[:, c, 0:M], x[0:M, c * P:(c + 1) * P], ident[0:M, 0:M])
                last.then_inc(S[signal], 1)

            def xh_transpose(r, m):
                k = CELLS * r + m
                pe_.wait_ge(S['norm_ok'], k + 1)
                if k >= 2:
                    pe_.wait_ge(S['xT_out'], k - 1)
                transpose(p_xhT[:, k % 2], pe[:, r % 2, m], TOK_M[r], 'xT_ok')

            def kv(r, m):
                M, k = TOK_M[r], CELLS * r + m
                pe_.wait_ge(S['xT_out'], k + 1)
                if k >= KV_SLOTS:
                    pe_.wait_ge(S['v_out'], k - KV_SLOTS + 1)
                if k == 0:
                    pe_.wait_ge(S['gamma_in'], 6)
                    pe_.wait_ge(S['bias_out'], 3)
                mm(p_kv[0:M, k % KV_SLOTS], [xhT[:, k % XHT_SLOTS, c, 0:M] for c in range(CC)],
                   [w_kv[:, c] for c in range(CC)], 'kv_ok')

            def setup(n):
                if n == 5 or n == 6:
                    pe_.wait_ge(S['w_in'], 16 * len(weights))
                    pe_.wait_ge(S['beta_ok'], 3 * CC)
                    for k in (0, 1) if n == 5 else (2,):
                        w, width = ((w_q, C), (w_kv, 2 * C), (w_gkv, 2 * C))[k]
                        if k == 2:
                            pe_.wait_ge(S['bias_out'], 1)
                        mm(p_kv[:, k % 2, 0:width], [beta_wide[:, k, c] for c in range(CC)],
                           [w[:, c] for c in range(CC)], 'bias_mm')
                if n == 7:
                    pe_.wait_ge(S['ident_ok'], 1)
                    pe_.wait_ge(S['cls_norm'], 2)
                    transpose(p_T, cls_n, P, 'clsT')
                if n == 8:
                    pe_.wait_ge(S['cls_qT'], 1)
                    mm(p_mm[:, 0:C], [tT[:, c] for c in range(CC)], [w_gq[:, c] for c in range(CC)], 'cls_q')

            for it in range(ITER):
                s, r, w = it, it - 1, it - 3
                for n in range(CELLS + 3):
                    if it == 0:
                        setup(n)
                    if s < STEPS and n < CELLS:
                        M, k = TOK_M[s], CELLS * s + n
                        if k == 0:
                            pe_.wait_ge(S['wc_in'], 16)
                            pe_.wait_ge(S['x_first'], 16)
                        if k == FIRST_CELLS or n == 0 and s > 0:
                            pe_.wait_ge(x_in[s % 2], 16 * KCH * (s // 2 + 1))
                        if k >= CONV_SLOTS:
                            pe_.wait_ge(S['pe_out'], k - CONV_SLOTS + 1)
                        mm(p_conv[0:M, k % CONV_SLOTS, 0:C], [xcols[:, s % 2, j, n * M:(n + 1) * M] for j in range(KCH)],
                           [w_conv[:, j] for j in range(KCH)], 'conv_ok')
                    if 0 <= w < STEPS:
                        M = TOK_M[w]
                        if n == 4:
                            pe_.wait_ge(S['agg_ok'], w + 1)
                            pe_.wait_ge(S['qT_out'], min(r + 1, STEPS))
                            transpose(p_T, agg, M, 'aggT_ok')
                        if n == 5:
                            pe_.wait_ge(S['aggT_out'], w + 1)
                            pe_.wait_ge(S['q_ok'], min(r + 1, STEPS))
                            if w >= 1:
                                pe_.wait_ge(S['g_ok'], 2 * w)
                            mm(p_mm[0:M, 0:C], [tT[:, c, 0:M] for c in range(CC)], [w_proj[:, c] for c in range(CC)],
                               'proj_ok')
                        if n == 6:
                            pe_.wait_ge(S['lo_ok'], w + 1)
                            transpose(p_T, lo, M, 'loT_ok')
                        if n == 7:
                            pe_.wait_ge(S['loT_out'], w + 1)
                            mm(p_mm[0:M, 0:C], [tT[:, c, 0:M] for c in range(CC)], [w_mod[:, c] for c in range(CC)],
                               'mod_ok')
                        if n == 8:
                            pe_.wait_ge(S['tn_ok'], w + 1)
                            transpose(p_T, ln_lo, M, 'tnT_ok')
                        if n == 9:
                            pe_.wait_ge(S['tnT_out'], w + 1)
                            pe_.wait_ge(S['patch_ok'], w + 1)
                            mm(p_mm[0:M], [tT[:, c, 0:M] for c in range(CC)], [w_gkv[:, c] for c in range(CC)],
                               'gkv_ok')
                    if 0 <= r < STEPS:
                        M = TOK_M[r]
                        if n == 1:
                            xh_transpose(r, 0)
                        if n == 2:
                            pe_.wait_ge(S['qn_ok'], r + 1)
                            transpose(p_T, qn, M, 'qT_ok')
                        if n == 3:
                            pe_.wait_ge(S['qT_out'], r + 1)
                            if w >= 1:
                                pe_.wait_ge(S['g_ok'], 2 * min(w, STEPS))
                            if r == 0:
                                pe_.wait_ge(S['gamma_in'], 6)
                                pe_.wait_ge(S['gq_ok'], 1)
                            mm(p_mm[0:M, 0:C], [smT[:, c, 0:M] for c in range(CC)], [w_q[:, c] for c in range(CC)],
                               'q_mm')
                        if n >= 3:
                            if n - 2 < CELLS:
                                xh_transpose(r, n - 2)
                            kv(r, n - 3)
            pe_.wait_ge(S['c_agg'], 1)
            transpose(p_T, agg, IMAGES, 'cT_ok')
            pe_.wait_ge(S['cT_out'], 1)
            pe_.wait_ge(S['g_ok'], 2 * STEPS)
            mm(p_mm[0:IMAGES, 0:C], [tT[:, c, 0:IMAGES] for c in range(CC)], [w_gproj[:, c] for c in range(CC)],
               'c_mm')


class Group:

    def __init__(self, c, pair=0):
        self.c, self.pair, self.half = c, pair, c % 2

    def plus(self, n):
        return Group(self.c + n, self.pair)

    def after(self, per_group, k):
        n = per_group * self.c + k + 1
        return n if isinstance(self.pair, int) else self.pair * (2 * per_group) + n

    def uses(self, inc, back=0):
        n = inc * (self.c // 2 + 1 - back)
        return n if isinstance(self.pair, int) else self.pair * inc + n

    def index(self, scale=1):
        n = self.c * scale
        return n if isinstance(self.pair, int) else self.pair * (2 * scale) + n


def run_iterations(engine, body, first=-1, last=GROUPS, loop=(2, GROUPS - 2)):
    lo, hi = loop
    hi = lo + (hi - lo) // 2 * 2

    def one(i, group):
        body(group, i + 1 < GROUPS, 0 <= i < GROUPS, i >= 1)

    for i in range(first, lo):
        one(i, Group(i))
    with engine.Fori(0, (hi - lo) // 2) as pair:
        for n in range(2):
            one(lo, Group(lo + n, pair))
    for i in range(hi, last + 1):
        one(i, Group(i))


A_AT = {2: [('xT', 0)], 3: [('qk', 0)], 4: [('v', 0)], 5: [('xT', 1)], 6: [('qk', 1)], 7: [('qkT', 0)],
        8: [('xT', 2)], 9: [('qk', 2)], 10: [('qkT', 1)], 11: [('v', 1)], 12: [('v', 2)], 13: [('qkT', 2)],
        14: [('v', 3)]}
C_AT = {0: [('proj', 0)], 2: [('yT', 0)], 3: [('ffn', 0)], 4: [('proj', 1)], 5: [('proj', 2)], 6: [('yT', 1)],
        7: [('ffn', 1)], 8: [('yT', 2)], 9: [('ffn', 2)], 12: [('twT', 0)], 13: [('lora', 0)], 15: [('lora', 1)]}
NORM_AT = {0: 0, 3: 1, 6: 2}
K_AT = {11: 0, 14: 1}
GATE_AT = 10
LORA_TILES = [(0, 1), (2,)]
A_BANK = [s for h in sorted(A_AT) for s in A_AT[h]]
C_BANK = [s for h in sorted(C_AT) for s in C_AT[h]]


def attention_ffn(nc, io, consts, h_dram, out_flat):
    with ExitStack() as ctx:
        def sb(name, shape, dt=F32):
            return ctx.enter_context(nc.sbuf_tensor(name, shape, dt))

        def ps(name, shape, dt=F32):
            return ctx.enter_context(nc.psum_tensor(name, shape, dt))

        def sem(name):
            return ctx.enter_context(nc.semaphore(name))

        ident, ident_b, tabs, earlier = consts.ident, consts.ident_b, consts.tabs, consts.earlier
        w_qk, w_v, w_p, w_f, right = consts.w_qk, consts.w_v, consts.w_p, consts.w_f, consts.right
        b_rows, eps5, eps6 = consts.b_rows, consts.eps5, consts.eps6

        ha = sb("ha", [TP, 2, TILES, C])
        hc = sb("hc", [TP, 2, TILES, C])
        a_st, a_mv = sb("a_st", [TP, 2, 6]), sb("a_mv", [TP, 2, 3])
        a_ln, a_rs = sb("a_ln", [TP, 2]), sb("a_rs", [TP, 2])
        xn = sb("xn", [TP, 2, C])
        xnT = sb("xnT", [P, 2, CC, GT])
        sq = sb("sq", [TP, 2 * C])
        ss, ss_ln, ss_rs = sb("ss", [TP, 2, 2 * HEADS]), sb("ss_ln", [TP, 2 * HEADS]), sb("ss_rs", [TP, 2, 2 * HEADS])
        t1, t2 = sb("t1", [TP, 2, 2 * C]), sb("t2", [TP, 2, 2 * C])
        qkT = sb("qkT", [P, 2, 4, GT + QP - SEQ])
        kb = sb("kb", [P, 2, 2, HALF, GT])
        vp = sb("vp", [QP, 2, GB, HEADS, 2 * HD])
        mx = sb("mx", [QP, 2, HALF], BF16)
        pr = sb("pr", [QP, 2, 2, 4 * SEQ])
        prT = sb("prT", [QP, 2, HALF, SEQ])
        oT = sb("oT", [P, 4, SEQ])
        rd = sb("rd", [SEQ, HEADS])
        on = sb("on", [QP, C])
        onT = sb("onT", [P, 2, CC, GT])
        hb, h2, h2l = sb("hb", [TP, 2, C]), sb("h2", [TP, 2, C]), sb("h2l", [TP, 3, C])
        c_st, c_mv = sb("c_st", [TP, 6]), sb("c_mv", [TP, 3])
        c_ln, c_rs = sb("c_ln", [TP, 1]), sb("c_rs", [TP, 1])
        yn = sb("yn", [TP, C])
        yT = sb("yT", [P, CC, TP])
        f = sb("f", [TP, 3, FFN_N])
        g_max, g_sum, g_rs = sb("g_max", [TP, TILES]), sb("g_sum", [TP, TILES]), sb("g_rs", [TP, TILES])
        g_e, g_rank, g_w = (sb(n, [TP, TILES, EXPERTS]) for n in ("g_e", "g_rank", "g_w"))
        g_gt, g_eq = (sb(n, [TP, TILES, EXPERTS, EXPERTS]) for n in ("g_gt", "g_eq"))
        tw = sb("tw", [TP, TILES, LR])
        twT = sb("twT", [TILES * LR, TP])
        out_sb = sb("out_sb", [TP, 3, C])

        p_s = ps("p_s", [P, 2, 2, 512])
        p_o = ps("p_o", [P, 512])
        p_n = ps("p_n", [P, 512])
        p_a = ps("p_a", [P, 512])
        p_c = ps("p_c", [P, 512])

        names = ("vp_0 rows_0 kb_0 dve_n dve_r dve_c dve_g act_a act_r act_c act_g pool_r pool_1 "
                 "a_var a_rstd xn_ok xT xT_out qk sq_ok ss_ok ss_rstd rot_ok rope_ok qkT_ok qkT_out v_mm v_out "
                 "s_mm s_max s_shift s_exp pT pT_out pv o_out oN o_norm oB oB_out "
                 "proj h2_ok c_var c_rstd yn_ok yT_ok yT_out ffn ffn_out g_m g_exp tw_ok twT_ok twT_out lora out_ok "
                 "hb_ok h2l_ok fb_ok").split()
        S = {n: sem("b_" + n) for n in names}
        ha_in = [sem("ha_in0"), sem("ha_in1")]
        hc_in = [sem("hc_in0"), sem("hc_in1")]
        k_in = [[sem(f"k_in{h}{n}") for n in range(2)] for h in range(2)]
        stored = [sem(f"stored{t}") for t in range(TILES)]
        block = ctx.enter_context(nc.Block())

        h_group = h_dram.rearrange("(g t p) c -> g p t c", t=TILES, p=TP)
        out_group = out_flat.rearrange("(g t p) c -> g t p c", t=TILES, p=TP)
        K_COLS = [(0, 2 * TP), (2 * TP, GT)]

        def pick(view, g):
            return view[g.index()] if isinstance(g.pair, int) else view[bass.ds(g.index(), 1)].squeeze(0)

        @block.sync
        def _(sp):
            def value(x):
                return x if isinstance(x, int) else sp.snap(x)

            def load(dst, g, landed, sem_=None, done=None):
                src = pick(h_group, g)
                if sem_ is not None:
                    sp.wait_ge(sem_, done)
                sp.dma_start(dst[:, g.half], src).then_inc(landed[g.half], 16)

            load(ha, Group(0), ha_in)

            def iteration(i, A, B, C_):
                g = i.plus(2)
                if i.c + 2 < GROUPS:
                    if i.c >= 0:
                        load(ha, g, ha_in, S['xn_ok'], value(i.after(3, 2)))
                    else:
                        load(ha, g, ha_in)
                if B:
                    if i.c >= 2:
                        load(hc, i, hc_in, S['hb_ok'], value(i.plus(-2).after(3, 2)))
                    else:
                        load(hc, i, hc_in)
                for h in range(16):
                    if A and h in K_AT:
                        n, g = K_AT[h], i.plus(1)
                        c0, c1 = K_COLS[n]
                        if n == 0 and g.c < 2:
                            sp.wait_ge(S['kb_0'], g.c + 1)
                        sp.wait_ge(S['qkT_out'], g.after(3, n + 1))
                        for k in range(2):
                            for hh in range(HALF):
                                r = slice(HD * hh, HD * hh + HD)
                                sp.dma_start(kb[r, g.half, k, hh, c0:c1],
                                             qkT[r, g.half, 2 + k, c0:c1]).then_inc(k_in[g.half][n], 16)
                    if C_:
                        for step, t in C_AT.get(h, []):
                            if step == 'lora':
                                g = i.plus(-1)
                                for t in LORA_TILES[t]:
                                    dst = out_group[g.index(), t] if isinstance(g.pair, int) else \
                                        out_group[bass.ds(g.index(), 1), t].squeeze(0)
                                    sp.wait_ge(S['out_ok'], value(g.after(3, t)))
                                    sp.dma_start(dst, out_sb[:, t]).then_inc(stored[t], 16)

            run_iterations(sp, iteration)
            for t in range(TILES):
                sp.wait_ge(stored[t], 16 * GROUPS)

        @block.gpsimd
        def _(pool):
            link = counted(pool, S['pool_1'])

            def fill_vp(half):
                link(nc.gpsimd.memset(vp[:, half, :, :, HD:], 1.0))
                link(nc.gpsimd.memset(vp[64:QP, half], 0.0))
                nc.gpsimd.memset(vp[64:SEQ, half, :, :, HD:], 1.0).then_inc(S['vp_0'], 1)
                pool.wait_ge(S['vp_0'], half + 1)

            nc.gpsimd.memset(kb[:, 0], 0.0).then_inc(S['kb_0'], 1)
            pool.wait_ge(S['kb_0'], 1)
            fill_vp(0)

            def iteration(i, A, B, C_):
                for h in range(16):
                    if i.c == -1 and h == 8:
                        for n, x in enumerate((qkT[:, :, :, GT:], prT[64:QP], on[64:QP])):
                            nc.gpsimd.memset(x, 0.0).then_inc(S['rows_0'], 1)
                            pool.wait_ge(S['rows_0'], n + 1)
                    if i.c == -1 and h == 14:
                        fill_vp(1)
                    if C_:
                        g = i.plus(-1)
                        for step, t in C_AT.get(h, []):
                            if step == 'proj':
                                if t == 0:
                                    pool.wait_ge(hc_in[g.half], g.uses(16))
                                if t > 1 or i.c > 1:
                                    pool.wait_ge(S['h2_ok'], g.after(3, t - 2))
                                nc.gpsimd.tensor_tensor(hb[:, t % 2], hc[:, g.half, t], b_rows[0:TP, 0],
                                                        ALU.add).then_inc(S['hb_ok'], 1)
                            if step == 'yT':
                                pool.wait_ge(S['h2_ok'], g.after(3, t))
                                nc.gpsimd.tensor_tensor(h2l[:, t], h2[:, t % 2], b_rows[0:TP, 1],
                                                        ALU.add).then_inc(S['h2l_ok'], 1)
                            if step == 'ffn':
                                pool.wait_ge(S['ffn_out'], g.after(3, t))
                                pool.wait_ge(S['h2l_ok'], g.after(3, t))
                                nc.gpsimd.tensor_tensor(h2l[:, t], h2l[:, t], f[:, t, 0:C],
                                                        ALU.add).then_inc(S['fb_ok'], 1)
                    if A:
                        for step, t in A_AT.get(h - 1, []):
                            if step == 'qk':
                                g, b = i.plus(1), t % 2
                                pool.wait_ge(S['rot_ok'], g.after(6, 2 * t + 1))
                                nc.gpsimd.tensor_tensor(t1[:, b], t1[:, b], t2[:, b], ALU.add).then_inc(S['pool_r'], 1)
                                pool.wait_ge(S['pool_r'], g.after(6, 2 * t))
                                pool.wait_ge(S['ss_rstd'], g.after(3, t))
                                x = t1[:, b].rearrange("p (h d) -> p h d", d=HD)
                                nc.gpsimd.tensor_tensor(x, x, ss_rs[:, b].unsqueeze(2).broadcast_to([TP, 2 * HEADS, HD]),
                                                        ALU.mult).then_inc(S['pool_r'], 1)
                                pool.wait_ge(S['pool_r'], g.after(6, 2 * t + 1))
                                nc.gpsimd.tensor_tensor(t1[:, b], t1[:, b], tabs[:, 2, t],
                                                        ALU.add).then_inc(S['rope_ok'], 1)

            run_iterations(pool, iteration)

        @block.scalar
        def _(act):
            act.preload_act_table_set("natural_log_exp_and_others")

            def iteration(i, A, B, C_):
                def pT_out(g, u):
                    if g.c == 0 and u == 0:
                        act.wait_ge(S['rows_0'], 3)
                    act.wait_ge(S['pT'], g.after(UNITS, u))
                    src = p_s[0:SEQ, u % 2, :, 0:4 * QP].rearrange("p x (h q) -> p x h q", q=QP)[:, :, :, 0:SEQ]
                    nc.scalar.copy(prT[0:SEQ, u % 2].rearrange("p (x h) q -> p x h q", x=2), src).then_inc(S['pT_out'], 1)

                def small_a(h):
                    g = i.plus(1)
                    if h in NORM_AT:
                        t = NORM_AT[h]
                        act.wait_ge(S['a_var'], g.after(3, t))
                        nc.scalar.activation(a_ln[:, t % 2:t % 2 + 1], a_mv[:, t % 2, 1:2], ACT.Ln,
                                             bias=eps5[0:TP, 0:1]).then_inc(S['act_a'], 1)
                        act.wait_ge(S['act_a'], g.after(3, t))
                        nc.scalar.activation(a_rs[:, t % 2:t % 2 + 1], a_ln[:, t % 2:t % 2 + 1], ACT.Exp,
                                             scale=-0.5).then_inc(S['a_rstd'], 1)
                    for step, t in A_AT.get(h - 1, []):
                        if step == 'qk':
                            act.wait_ge(S['ss_ok'], g.after(3, t))
                            nc.scalar.activation(ss_ln[:], ss[:, t % 2], ACT.Ln, bias=eps6[0:TP, 0:1],
                                                 scale=1.0 / HD).then_inc(S['act_r'], 1)
                            act.wait_ge(S['act_r'], g.after(3, t))
                            nc.scalar.activation(ss_rs[:, t % 2], ss_ln[:], ACT.Exp, scale=-0.5).then_inc(S['ss_rstd'], 1)

                def part_a(h):
                    g = i.plus(1)
                    for step, t in A_AT.get(h, []):
                        c0 = t * TP
                        if step == 'xT':
                            act.wait_ge(S['xT'], g.after(3, t))
                            nc.scalar.copy(xnT[:, g.half, :, c0:c0 + TP],
                                           p_a[:, 0:CC * TP].rearrange("p (c n) -> p c n", c=CC)).then_inc(S['xT_out'], 1)
                        if step == 'qk':
                            act.wait_ge(S['qk'], g.after(3, t))
                            nc.scalar.activation(sq[:], p_a[0:TP, :], ACT.Square).then_inc(S['sq_ok'], 1)
                        if step == 'qkT':
                            act.wait_ge(S['qkT_ok'], g.after(3, t))
                            nc.scalar.copy(qkT[:, g.half, :, c0:c0 + TP],
                                           p_a[:, 0:4 * TP].rearrange("p (c n) -> p c n", c=4)).then_inc(S['qkT_out'], 1)
                        if step == 'v':
                            if t == 0 and g.c < 2:
                                act.wait_ge(S['vp_0'], g.c + 1)
                            act.wait_ge(S['v_mm'], g.after(GB, t))
                            nc.scalar.copy(vp[0:SEQ, g.half, t, :, 0:HD],
                                           p_a[0:SEQ, 0:C].rearrange("p (h d) -> p h d", d=HD)).then_inc(S['v_out'], 1)

                def part_c(h):
                    g = i.plus(-1)
                    for step, t in C_AT.get(h, []):
                        if step == 'yT':
                            act.wait_ge(S['yT_ok'], g.after(3, t))
                            nc.scalar.copy(yT[:], p_c[:, 0:CC * TP].rearrange("p (c n) -> p c n", c=CC)
                                           ).then_inc(S['yT_out'], 1)
                        if step == 'ffn':
                            act.wait_ge(S['ffn'], g.after(3, t))
                            nc.scalar.copy(f[:, t], p_c[0:TP, 0:FFN_N]).then_inc(S['ffn_out'], 1)
                        if step == 'twT':
                            act.wait_ge(S['twT_ok'], g.after(1, 0))
                            nc.scalar.copy(twT[:], p_c[0:TILES * LR, 0:TP]).then_inc(S['twT_out'], 1)

                def small_c(h):
                    g = i.plus(-1)
                    for step, t in C_AT.get(h - 1, []):
                        if step == 'proj':
                            act.wait_ge(S['c_var'], g.after(3, t))
                            nc.scalar.activation(c_ln[:], c_mv[:, 1:2], ACT.Ln, bias=eps5[0:TP, 0:1]).then_inc(S['act_c'], 1)
                            act.wait_ge(S['act_c'], g.after(3, t))
                            nc.scalar.activation(c_rs[:], c_ln[:], ACT.Exp, scale=-0.5).then_inc(S['c_rstd'], 1)
                    if h == GATE_AT:
                        act.wait_ge(S['g_m'], g.after(1, 0))
                        nc.scalar.activation(g_e[:], g_e[:], ACT.Exp).then_inc(S['g_exp'], 1)

                for h in range(16):
                    u, even = h // 2, h % 2 == 0
                    if even:
                        if u % 2 == 1 and (B or u == 1):
                            g, b = (i, (u - 3) // 2) if u > 1 else (i.plus(-1), GB - 1)
                            if B and u > 1 or C_ and u == 1:
                                act.wait_ge(S['pv'], g.after(UNITS, 2 * b + 1))
                                nc.scalar.copy(oT[:], p_o[:, 0:4 * SEQ].rearrange("p (c q) -> p c q", c=4)
                                               ).then_inc(S['o_out'], 1)
                        if u % 2 == 0:
                            g, b = (i, (u - 4) // 2) if u > 2 else (i.plus(-1), GB - 2 + u // 2)
                            if B and u > 2 or C_ and u <= 2:
                                act.wait_ge(S['oB'], g.after(GB, b))
                                nc.scalar.copy(onT[:, g.half, :, b * SEQ:(b + 1) * SEQ],
                                               p_n[:, 0:CC * QP].rearrange("p (c q) -> p c q", c=CC)[:, :, 0:SEQ]
                                               ).then_inc(S['oB_out'], 1)
                    elif B:
                        act.wait_ge(S['s_shift'], i.after(UNITS, u))
                        nc.scalar.activation(pr[:, u % 2], p_s[0:QP, u % 2, :, 0:4 * SEQ], ACT.Exp,
                                             scale=HD ** -0.5).then_inc(S['s_exp'], 1)
                    if A:
                        part_a(h)
                    if C_:
                        part_c(h)
                    if even:
                        if B and u > 0:
                            pT_out(i, u - 1)
                        if C_ and u == 0:
                            pT_out(i.plus(-1), UNITS - 1)
                    if C_:
                        small_c(h)
                    if A:
                        small_a(h)

            run_iterations(act, iteration)

        @block.vector
        def _(dve):
            def iteration(i, A, B, C_):
                def a_moments(g, t):
                    b = t % 2
                    if t == 0:
                        dve.wait_ge(ha_in[g.half], g.uses(16))
                    nc.vector.bn_stats(a_st[:, b], ha[:, g.half, t]).then_inc(S['dve_r'], 1)
                    dve.wait_ge(S['dve_r'], g.after(3, t))
                    nc.vector.tensor_copy(a_mv[:, b, 2:3], a_st[:, b, 0:1])
                    nc.vector.bn_aggr(a_mv[:, b, 0:2], a_st[:, b]).then_inc(S['a_var'], 1)

                def a_norm(g, t):
                    b = t % 2
                    dve.wait_ge(S['a_rstd'], g.after(3, t))
                    if g.c * 3 + t >= 2:
                        dve.wait_ge(S['xT'], g.after(3, t - 2))
                    nc.vector.tensor_scalar(xn[:, b], ha[:, g.half, t], a_mv[:, b, 0:1], a_rs[:, b:b + 1],
                                            ALU.subtract, ALU.mult).then_inc(S['xn_ok'], 1)

                def rotate(g, t):
                    b = t % 2
                    dve.wait_ge(S['sq_ok'], g.after(3, t))
                    if g.c * 3 + t >= 2:
                        dve.wait_ge(S['qkT_ok'], g.after(3, t - 2))
                    x = p_a[0:TP, :]
                    nc.vector.tensor_tensor(t1[:, b], x, tabs[:, 0, t], ALU.mult)
                    x4 = x.rearrange("p (h s d) -> p h s d", s=2, d=HD // 2)
                    o4 = t2[:, b].rearrange("p (h s d) -> p h s d", s=2, d=HD // 2)
                    w4_ = tabs[:, 1, t].rearrange("p (h s d) -> p h s d", s=2, d=HD // 2)
                    for s in range(2):
                        nc.vector.tensor_tensor(o4[:, :, s], x4[:, :, 1 - s], w4_[:, :, s],
                                                ALU.mult).then_inc(S['rot_ok'], 1)
                    nc.vector.reduce_sum(ss[:, b], sq[:].rearrange("p (h d) -> p h d", d=HD), AX_X).then_inc(S['ss_ok'], 1)

                def part_c(h):
                    g = i.plus(-1)
                    for step, t in C_AT.get(h - 1, []):
                        if step == 'proj':
                            dve.wait_ge(S['c_rstd'], g.after(3, t))
                            if t > 0 or i.c > 1:
                                dve.wait_ge(S['yT_ok'], g.after(3, t - 1))
                            nc.vector.tensor_scalar(yn[:], h2[:, t % 2], c_mv[:, 0:1], c_rs[:, 0:1],
                                                    ALU.subtract, ALU.mult).then_inc(S['yn_ok'], 1)
                            dve.wait_ge(S['yn_ok'], g.after(3, t))
                    for step, t in C_AT.get(h, []):
                        if step == 'proj':
                            dve.wait_ge(S['proj'], g.after(3, t))
                            dve.wait_ge(S['hb_ok'], g.after(3, t))
                            if t > 1 or i.c > 1:
                                dve.wait_ge(S['h2l_ok'], g.after(3, t - 2))
                            nc.vector.tensor_tensor(h2[:, t % 2], p_c[0:TP, 0:C], hb[:, t % 2], ALU.add).then_inc(S['h2_ok'], 1)
                            dve.wait_ge(S['h2_ok'], g.after(3, t))
                            nc.vector.bn_stats(c_st[:], h2[:, t % 2]).then_inc(S['dve_c'], 1)
                            dve.wait_ge(S['dve_c'], g.after(3, t))
                            nc.vector.tensor_copy(c_mv[:, 2:3], c_st[:, 0:1])
                            nc.vector.bn_aggr(c_mv[:, 0:2], c_st[:]).then_inc(S['c_var'], 1)
                        if step == 'lora':
                            dve.wait_ge(S['lora'], g.after(2, t))
                            for n, t in enumerate(LORA_TILES[t]):
                                dve.wait_ge(S['fb_ok'], g.after(3, t))
                                if i.c > 1:
                                    dve.wait_ge(stored[t], g.after(1, -1) * 16)
                                nc.vector.tensor_tensor(out_sb[:, t], p_c[0:TP, n * C:(n + 1) * C], h2l[:, t],
                                                        ALU.add).then_inc(S['out_ok'], 1)
                    if h == GATE_AT:
                        rank_experts(g)
                    if h == GATE_AT + 1:
                        weigh_experts(g)

                gate_steps = 9

                def rank_experts(g):
                    then = lambda n, ins: (ins.then_inc(S['dve_g'], 1), dve.wait_ge(S['dve_g'], g.after(gate_steps, n)))
                    dve.wait_ge(S['ffn_out'], g.after(3, 2))
                    lg = f[:, :, C + LR:FFN_N]
                    shape = [TP, TILES, EXPERTS, EXPERTS]
                    by_e, by_j = lg.unsqueeze(3).broadcast_to(shape), lg.unsqueeze(2).broadcast_to(shape)
                    then(0, nc.vector.reduce_max(g_max[:], lg, AX_X))
                    nc.vector.tensor_tensor(g_e[:], lg, g_max[:].unsqueeze(2).broadcast_to([TP, TILES, EXPERTS]),
                                            ALU.subtract).then_inc(S['g_m'], 1)
                    nc.vector.tensor_tensor(g_gt[:], by_j, by_e, ALU.is_gt)
                    then(1, nc.vector.tensor_tensor(g_eq[:], by_j, by_e, ALU.is_equal))
                    then(2, nc.vector.tensor_tensor(g_eq[:], g_eq[:], earlier[:].unsqueeze(1).broadcast_to(shape),
                                                    ALU.mult))
                    then(3, nc.vector.tensor_tensor(g_gt[:], g_gt[:], g_eq[:], ALU.add))
                    then(4, nc.vector.reduce_sum(g_rank[:], g_gt[:], AX_X))

                def weigh_experts(g):
                    then = lambda n, ins: (ins.then_inc(S['dve_g'], 1), dve.wait_ge(S['dve_g'], g.after(gate_steps, n)))
                    dve.wait_ge(S['g_exp'], g.after(1, 0))
                    then(5, nc.vector.reduce_sum(g_sum[:], g_e[:], AX_X))
                    then(6, nc.vector.reciprocal(g_rs[:], g_sum[:]))
                    then(7, nc.vector.scalar_tensor_tensor(g_w[:], g_rank[:], 2.0, g_e[:], ALU.is_lt, ALU.mult))
                    then(8, nc.vector.tensor_tensor(g_w[:], g_w[:], g_rs[:].unsqueeze(2).broadcast_to([TP, TILES, EXPERTS]),
                                                    ALU.mult))
                    nc.vector.tensor_tensor(
                        tw[:].rearrange("p t (e r) -> p t e r", r=RANK),
                        f[:, :, C:C + LR].rearrange("p t (e r) -> p t e r", r=RANK),
                        g_w[:].unsqueeze(3).broadcast_to([TP, TILES, EXPERTS, RANK]), ALU.mult).then_inc(S['tw_ok'], 1)

                for h in range(16):
                    u, even = h // 2, h % 2 == 0
                    if i.c == -1 and h == 12:
                        nc.vector.memset(kb[:, 1], 0.0).then_inc(S['kb_0'], 1)
                    if even and B:
                        dve.wait_ge(S['s_mm'], i.after(UNITS, u))
                        if i.c * UNITS + u >= 2:
                            dve.wait_ge(S['s_shift'], i.after(UNITS, u - 2))
                        nc.vector.reduce_max(mx[:, u % 2].rearrange("p (x h) -> p x h", x=2),
                                             p_s[0:QP, u % 2, :, 0:4 * SEQ].rearrange("p x (h k) -> p x h k", k=SEQ),
                                             AX_X, negate=True).then_inc(S['s_max'], 1)
                    if not even and u % 2 == 1:
                        g, b = (i, (u - 3) // 2) if u > 1 else (i.plus(-1), GB - 1)
                        if B and u > 1 or C_ and u == 1:
                            if g.c == 0 and b == 0:
                                dve.wait_ge(S['rows_0'], 3)
                            dve.wait_ge(S['oN'], g.after(GB, b))
                            o3 = p_n[0:SEQ, :].rearrange("p (h e) -> p h e", e=2 * HD)
                            nc.vector.reciprocal(rd[:], o3[:, :, HD]).then_inc(S['dve_n'], 1)
                            dve.wait_ge(S['dve_n'], g.after(GB, b))
                            nc.vector.tensor_tensor(on[0:SEQ].rearrange("p (h d) -> p h d", d=HD), o3[:, :, 0:HD],
                                                    rd[:].unsqueeze(2).broadcast_to([SEQ, HEADS, HD]),
                                                    ALU.mult).then_inc(S['o_norm'], 1)
                    if A and h - 1 in NORM_AT:
                        a_norm(i.plus(1), NORM_AT[h - 1])
                    if A and h in NORM_AT:
                        a_moments(i.plus(1), NORM_AT[h])
                    if A:
                        for step, t in A_AT.get(h, []):
                            if step == 'qk':
                                rotate(i.plus(1), t)
                    if C_:
                        part_c(h)

            run_iterations(dve, iteration)

        @block.tensor
        def _(pe):
            def mm(out, lhs, rhs, done=None):
                for c, (a, b) in enumerate(zip(lhs, rhs)):
                    last = nc.tensor.matmul(out, a, b, start=(c == 0), stop=(c == len(lhs) - 1))
                if done is not None:
                    last.then_inc(done, 1)
                return last

            A_FREE = {'xT': ('xT_out', 3), 'qk': ('rot_ok', 6), 'qkT': ('qkT_out', 3), 'v': ('v_out', GB)}
            C_FREE = {'proj': ('h2_ok', 3), 'yT': ('yT_out', 3), 'ffn': ('ffn_out', 3), 'twT': ('twT_out', 1),
                      'lora': ('out_ok', 3)}

            def wait_bank(order, free, g, item, first):
                n = order.index(item)
                if n == 0 and first:
                    return
                step, t = order[n - 1]
                name, per = free[step]
                k = {'rot_ok': 2 * t + 1, 'out_ok': LORA_TILES[t % 2][-1]}.get(name, t)
                pe.wait_ge(S[name], (g if n else g.plus(-1)).after(per, k))

            def iteration(i, A, B, C_):
                def part_a(h):
                    g = i.plus(1)
                    for step, t in A_AT.get(h, []):
                        wait_bank(A_BANK, A_FREE, g, (step, t), g.c == 0)
                        c0 = t * TP
                        if step == 'xT':
                            pe.wait_ge(S['xn_ok'], g.after(3, t))
                            for c in range(CC):
                                last = nc.tensor.transpose(p_a[:, c * TP:(c + 1) * TP], xn[:, t % 2, c * P:(c + 1) * P],
                                                           ident[0:TP, 0:TP])
                            last.then_inc(S['xT'], 1)
                        if step == 'qk':
                            pe.wait_ge(S['xT_out'], g.after(3, t))
                            mm(p_a[0:TP, :], [xnT[:, g.half, c, c0:c0 + TP] for c in range(CC)],
                               [w_qk[:, c] for c in range(CC)], S['qk'])
                        if step == 'qkT':
                            pe.wait_ge(S['rope_ok'], g.after(3, t))
                            for c in range(4):
                                last = nc.tensor.transpose(p_a[:, c * TP:(c + 1) * TP], t1[:, t % 2, c * P:(c + 1) * P],
                                                           ident[0:TP, 0:TP])
                            last.then_inc(S['qkT_ok'], 1)
                        if step == 'v':
                            mm(p_a[0:SEQ, 0:C], [xnT[:, g.half, c, t * SEQ:(t + 1) * SEQ] for c in range(CC)],
                               [w_v[:, c] for c in range(CC)], S['v_mm'])

                def part_c(h):
                    g = i.plus(-1)
                    for step, t in C_AT.get(h, []):
                        wait_bank(C_BANK, C_FREE, g, (step, t), g.c == 0)
                        c0 = t * TP
                        if step == 'proj':
                            pe.wait_ge(S['oB_out'], g.after(GB, min(t + 1, GB - 1)))
                            mm(p_c[0:TP, 0:C], [onT[:, g.half, c, c0:c0 + TP] for c in range(CC)],
                               [w_p[:, c] for c in range(CC)], S['proj'])
                        if step == 'yT':
                            pe.wait_ge(S['yn_ok'], g.after(3, t))
                            for c in range(CC):
                                last = nc.tensor.transpose(p_c[:, c * TP:(c + 1) * TP], yn[:, c * P:(c + 1) * P],
                                                           ident[0:TP, 0:TP])
                            last.then_inc(S['yT_ok'], 1)
                        if step == 'ffn':
                            pe.wait_ge(S['yT_out'], g.after(3, t))
                            mm(p_c[0:TP, 0:FFN_N], [yT[:, c] for c in range(CC)], [w_f[:, c] for c in range(CC)],
                               S['ffn'])
                        if step == 'twT':
                            pe.wait_ge(S['tw_ok'], g.after(1, 0))
                            nc.tensor.transpose(p_c[0:TILES * LR, 0:TP], tw[:].rearrange("p t n -> p (t n)"),
                                                ident[0:TP, 0:TP]).then_inc(S['twT_ok'], 1)
                        if step == 'lora':
                            pe.wait_ge(S['twT_out'], g.after(1, 0))
                            for n, tile in enumerate(LORA_TILES[t]):
                                last = mm(p_c[0:TP, n * C:(n + 1) * C], [twT[:]], [right[:, tile]])
                            last.then_inc(S['lora'], 1)

                def scores(u):
                    b, k = u // 2, u % 2
                    if i.c == 0 and u == 0:
                        pe.wait_ge(S['rows_0'], 3)
                    if k == 0 and b == 0:
                        pe.wait_ge(k_in[i.half][0], i.uses(16 * HEADS))
                    if k == 0 and b == 2:
                        pe.wait_ge(k_in[i.half][1], i.uses(16 * HEADS))
                    if i.c * UNITS + u >= 2:
                        pe.wait_ge(S['pT_out'], i.after(UNITS, u - 2))
                    for x in range(2):
                        last = nc.tensor.matmul(p_s[0:QP, u % 2, x, 0:4 * SEQ], qkT[:, i.half, k, b * SEQ:b * SEQ + QP],
                                                kb[:, i.half, k, 4 * x:4 * x + 4, b * SEQ:(b + 1) * SEQ],
                                                start=True, stop=False, skip_group_check=True)
                    last.then_inc(S['s_mm'], 1)

                def shift(u):
                    pe.wait_ge(S['s_max'], i.after(UNITS, u))
                    for x in range(2):
                        last = nc.tensor.matmul(p_s[0:QP, u % 2, x, 0:4 * SEQ], ident_b[0:QP, 0:QP],
                                                mx[:, u % 2, 4 * x:4 * x + 4].unsqueeze(2).broadcast_to([QP, 4, SEQ]),
                                                start=False, stop=True, skip_group_check=True)
                    last.then_inc(S['s_shift'], 1)

                def transpose_probs(g, u):
                    pe.wait_ge(S['s_exp'], g.after(UNITS, u))
                    for x in range(2):
                        for n in range(4):
                            last = nc.tensor.transpose(p_s[0:SEQ, u % 2, x, n * QP:(n + 1) * QP],
                                                       pr[:, u % 2, x, n * SEQ:(n + 1) * SEQ], ident[0:QP, 0:QP])
                    last.then_inc(S['pT'], 1)

                def weigh_values(g, u):
                    b, k = u // 2, u % 2
                    pe.wait_ge(S['pT_out'], g.after(UNITS, u))
                    if k == 0 and not (b == 0 and g.c == 0):
                        pe.wait_ge(S['o_out'], g.after(GB, b - 1))
                    for n in range(HALF):
                        c, j = 2 * k + n // 4, n % 4
                        last = nc.tensor.matmul(p_o[32 * j:32 * j + 32, c * SEQ:(c + 1) * SEQ],
                                                vp[:, g.half, b, HALF * k + n, :], prT[:, u % 2, n, :],
                                                start=True, stop=True)
                    last.then_inc(S['pv'], 1)

                for h in range(16):
                    u, even = h // 2, h % 2 == 0
                    out_of = None
                    if u % 2 == 1:
                        if u > 1 and B:
                            out_of = (i, (u - 3) // 2)
                        if u == 1 and C_:
                            out_of = (i.plus(-1), GB - 1)
                    before = (i, u - 1) if u > 0 else (i.plus(-1), UNITS - 1)
                    has_before = B if u > 0 else C_
                    if even:
                        if B:
                            scores(u)
                    elif B:
                        shift(u)
                    if A:
                        part_a(h)
                    if C_:
                        part_c(h)
                    if even:
                        if has_before:
                            transpose_probs(*before)
                        if out_of:
                            g, b = out_of
                            pe.wait_ge(S['o_out'], g.after(GB, b))
                            if not (g.c == 0 and b == 0):
                                pe.wait_ge(S['oB_out'], g.after(GB, b - 1))
                            for c in range(4):
                                last = nc.tensor.transpose(p_n[0:SEQ, c * P:(c + 1) * P], oT[:, c], ident[:])
                            last.then_inc(S['oN'], 1)
                    else:
                        if has_before:
                            weigh_values(*before)
                        if out_of:
                            g, b = out_of
                            pe.wait_ge(S['o_norm'], g.after(GB, b))
                            for c in range(CC):
                                last = nc.tensor.transpose(p_n[:, c * QP:(c + 1) * QP], on[:, c * P:(c + 1) * P],
                                                           ident[0:QP, 0:QP])
                            last.then_inc(S['oB'], 1)

            run_iterations(pe, iteration)


def build(nc, io, out):
    h_dram = nc.dram_tensor("h_tokens", [IMAGES * SEQ, C], F32).ap()
    patch_dram = nc.dram_tensor("patch_tokens", [ALL_W, C], F32).ap()
    gv_dram = nc.dram_tensor("class_values", [ALL_W, C], F32).ap()
    gs_dram = nc.dram_tensor("class_scores", [ALL_W, LH], F32).ap()
    with ExitStack() as ctx:
        consts = Constants(nc, ctx)
        patch_tokens(nc, io, consts, h_dram, patch_dram, gv_dram, gs_dram)
        attention_ffn(nc, io, consts, h_dram, out.rearrange("b s c -> (b s) c"))


def arrays_of(inputs):
    a = {k.replace('L0_tok_', '').replace('L0_attn_', '').replace('L0_ffn_', ''): np.asarray(v)
         for k, v in inputs.items()}
    side = PATCH * GRID * GRID
    x = a['x'][:, :, :side, :side].reshape(IMAGES, 3, GRID, GRID, PATCH, GRID, GRID, PATCH)
    x = x.transpose(1, 4, 7, 0, 2, 5, 3, 6).reshape(PIXELS, ALL_W, CELLS)
    x_cols = np.zeros((STEPS, KROWS * KCH, CELLS * P), x.dtype)
    for s, m in enumerate(TOK_M):
        part = x[:, P * s:P * s + m, :].transpose(0, 2, 1)
        x_cols[s, :PIXELS, :CELLS * m] = part.reshape(PIXELS, CELLS * m)
    conv_w = np.zeros((KROWS * KCH, C), a['conv_w'].dtype)
    conv_w[:PIXELS] = a['conv_w'].reshape(C, PIXELS).T
    vec = {**a, 'b_lin': a['b_lin']}
    half = HD // 2
    rope_g = np.stack([a['q_gamma'], a['k_gamma'], np.roll(a['q_gamma'], half), np.roll(a['k_gamma'], half),
                       a['q_beta'], a['k_beta'], np.roll(a['q_beta'], half), np.roll(a['k_beta'], half)])
    inv = (1.0 / 10000.0 ** (np.arange(half, dtype=np.float32) / half)).astype(np.float32)
    ang = np.outer(np.arange(GT) % SEQ, inv).astype(np.float32)
    sin = np.concatenate([-np.sin(ang), np.sin(ang)], axis=1)
    cos = np.concatenate([np.cos(ang), np.cos(ang)], axis=1)
    rope = np.stack([cos, sin]).reshape(2, TILES, TP, HD).transpose(2, 1, 0, 3)
    wf = np.concatenate([a['W_lin'].T, a['left'].transpose(1, 0, 2).reshape(C, LR), a['gate_w'].T], axis=1)
    out = {
        'x_cols': x_cols, 'conv_w': conv_w, 'txt': a['txt'],
        'rows': np.stack([vec[r] for r in ROWS]),
        'cols': np.stack([vec[c] for c in COLS]).reshape(len(COLS), CC, P).transpose(2, 0, 1),
        'w_qkv': a['w_qkv'].T, 'w_proj': a['w_proj'].T, 'w_ffn': wf, 'right': a['right'].reshape(LR, C),
        'rope_g': rope_g, 'rope': rope.astype(np.float32),
    }
    for n in ('la_wq', 'la_wkv', 'la_proj_w', 'ga_wq', 'ga_wkv', 'ga_proj_w', 'mod_w'):
        out[n] = a[n]
    return {k: np.ascontiguousarray(v) for k, v in out.items()}


def kernel(**inputs):
    import concourse.bacc as bacc
    from concourse.bass_utils import run_bass_kernel_spmd

    arrays = arrays_of(inputs)
    nc = bacc.Bacc("TRN2", target_bir_lowering=False, num_devices=1)
    io = {k: nc.dram_tensor("in_" + k, v.shape, mybir.dt.from_np(v.dtype), kind="ExternalInput").ap()
          for k, v in arrays.items()}
    out = nc.dram_tensor("out", (IMAGES, SEQ, C), F32, kind="ExternalOutput").ap()
    build(nc, io, out)
    r = run_bass_kernel_spmd(nc, [{"in_" + k: v for k, v in arrays.items()}], core_ids=[0])
    return r.results[0]["out"]
```

```python
import numpy as np
import concourse.bass as bass
import concourse.mybir as mybir
from contextlib import ExitStack

F32 = mybir.dt.float32
F32R = mybir.dt.float32r
BF16 = mybir.dt.bfloat16
ALU = mybir.AluOpType
ACT = mybir.ActivationFunctionType
AX_X = mybir.AxisListType.X

P = 128
C = 256
CC = C // P
IMAGES = 64
PATCH = 14
GRID = 3
WINDOWS = GRID * GRID
CELLS = GRID * GRID
TXT = 77
SEQ = WINDOWS + 1 + TXT
ALL_W = IMAGES * WINDOWS

PIXELS = 3 * PATCH * PATCH
KROWS = 120
KCH = -(-PIXELS // KROWS)
STEPS = -(-ALL_W // P)
TOK_M = [min(P, ALL_W - P * s) for s in range(STEPS)]
LH, LD = 8, 32
LOAD_CELLS = 3
LOADS = CELLS // LOAD_CELLS * STEPS
X_SLOTS, XS_SLOTS = 3, 3
CONV_SLOTS, XHT_SLOTS, KV_SLOTS = 2, 3, 2

HEADS, HD = 16, 16
GB = 4
GROUPS = IMAGES // GB
GT = GB * SEQ
TILES = 3
TP = GT // TILES
QP = 96
HALF = HEADS // 2
UNITS = 2 * GB
EXPERTS, RANK = 8, 4
LR = EXPERTS * RANK
FFN_N = C + LR + EXPERTS

ROWS = ['la_proj_b', 'class_emb', 'ga_ln_q_g', 'ga_ln_q_b', 'ga_proj_b', 'mod_b', 'b_proj', 'b_lin']
TOKEN_ROWS = 6
COLS = ['la_ln_q_g', 'la_ln_kv_g', 'ga_ln_kv_g', 'la_ln_q_b', 'la_ln_kv_b', 'ga_ln_kv_b']


def counted(engine, semaphore, start=0):
    n = [start]

    def link(instruction):
        n[0] = n[0] + 1
        instruction.then_inc(semaphore, 1)
        engine.wait_ge(semaphore, n[0])
        return instruction

    return link


class Split:

    def __init__(self, hi, lo):
        self.hi, self.lo = hi, lo

    def chunks(self, pick, n=CC):
        return Split([pick(self.hi, c) for c in range(n)], [pick(self.lo, c) for c in range(n)])


class Constants:

    def __init__(self, nc, ctx):
        def sb(name, shape, dt=F32):
            return ctx.enter_context(nc.sbuf_tensor(name, shape, dt))

        self.ident = sb("ident", [P, P])
        self.ident_b = sb("ident_b", [P, P], BF16)
        self.w_qk = sb("w_qk", [P, CC, 2 * C])
        self.w_v = sb("w_v", [P, CC, C])
        self.w_p = sb("w_p", [P, CC, C])
        self.w_f = sb("w_f", [P, CC, FFN_N])
        self.right = sb("right", [TILES * LR, TILES, C])
        self.b_rows = sb("b_rows", [P, 2, C])
        self.w_mean = sb("w_mean", [P, CC, 2 * HEADS])
        self.rope_in = sb("rope_in", [TP, TILES, 2, HD])
        self.rope_g = sb("rope_g", [TP, 8, HD])
        self.rope_s = sb("rope_s", [TP, 7, HD])
        self.tabs = sb("tabs", [TP, 3, TILES, 2 * C])
        self.earlier = sb("earlier", [TP, EXPERTS, EXPERTS])
        self.weights = [self.w_qk, self.w_v, self.w_p, self.w_f, self.right]
        self.high = [sb(n, shape) for n, shape in (
            ("w_qk_hi", [P, CC, 2 * C]), ("w_v_hi", [P, CC, C]), ("w_p_hi", [P, CC, C]), ("w_f_hi", [P, CC, FFN_N]),
            ("right_hi", [TILES * LR, TILES, C]))]
        self.eps5 = sb("eps5", [P, 1])
        self.eps6 = sb("eps6", [P, 1])
        names = "w_split rope_in w_ok tab_ok zeroed dve_k pool_k"
        self.S = {n: ctx.enter_context(nc.semaphore("k_" + n)) for n in names.split()}
        self.w_in = [ctx.enter_context(nc.semaphore(f"k_w_in{n}")) for n in range(2)]

    def place_raw(self, a, b):
        two = lambda x: x.rearrange("p (k n) -> p k n", k=CC)
        n = [0, 4 * C, 6 * C, 8 * C]
        self.raw = [two(a[:, n[k]:n[k + 1]]) for k in range(3)]
        self.raw.append(two(b[:, 0:CC * FFN_N]))
        self.raw.append(b[0:TILES * LR, CC * FFN_N:CC * FFN_N + TILES * C].rearrange("p (t n) -> p t n", t=TILES))

    def load_tables(self, nc, sp, io):
        sp.dma_start(self.b_rows[:], io['rows'][TOKEN_ROWS:].unsqueeze(0).broadcast_to([P, 2, C])
                     ).then_inc(self.S['rope_in'], 16)
        sp.dma_start(self.rope_in[:], io['rope']).then_inc(self.S['rope_in'], 16)
        sp.dma_start(self.rope_g[:], io['rope_g'].unsqueeze(0).broadcast_to([TP, 8, HD])).then_inc(self.S['rope_in'], 16)

    def load_weights(self, nc, sp, io, part):
        sources = (io['w_qkv'][:, 0:2 * C], io['w_qkv'][:, 2 * C:3 * C], io['w_proj'], io['w_ffn'])
        for n in ((0, 1, 2), (3,))[part]:
            sp.dma_start(self.raw[n], sources[n].rearrange("(k p) n -> p k n", p=P)).then_inc(self.w_in[part], 16)
        if part == 1:
            sp.wait_ge(self.S['zeroed'], 1)
            for t in range(TILES):
                sp.dma_start(self.raw[4][LR * t:LR * (t + 1), t], io['right']).then_inc(self.w_in[1], 16)

    def fill(self, nc, pool):
        link = counted(pool, self.S['pool_k'])
        link(nc.gpsimd.memset(self.ident_b[:], 0.0))
        link(nc.gpsimd.affine_select(out=self.ident_b[:], in_=self.ident_b[:], compare_op=ALU.not_equal, fill=1.0,
                                     base=0, pattern=[[-1, P]], channel_multiplier=1))
        link(nc.gpsimd.memset(self.earlier[:], 1.0))
        link(nc.gpsimd.affine_select(out=self.earlier[:], in_=self.earlier[:], compare_op=ALU.is_gt, fill=0.0, base=0,
                                     pattern=[[1, EXPERTS], [-1, EXPERTS]], channel_multiplier=0))
        link(nc.gpsimd.memset(self.eps5[:], 1e-5))
        link(nc.gpsimd.memset(self.eps6[:], 1e-6))

    def centre(self, nc, dve):
        link = counted(dve, self.S['dve_k'], 5 * 2 * TILES)
        dve.wait_ge(self.w_in[0], 16 * 3)
        w4 = self.raw[0].rearrange("p c (h d) -> p c h d", d=HD)
        link(nc.vector.reduce_sum(self.w_mean[:], w4, AX_X))
        link(nc.vector.tensor_scalar(self.w_mean[:], self.w_mean[:], 1.0 / HD, None, ALU.mult))
        for c in range(CC):
            nc.vector.tensor_tensor(w4[:, c], w4[:, c], self.w_mean[:, c].unsqueeze(2).broadcast_to([P, 2 * HEADS, HD]),
                                    ALU.subtract).then_inc(self.S['w_ok'], 1)

    def split(self, nc, dve, n):
        low, high, raw = self.weights[n][:], self.high[n][:], self.raw[n]
        if n == 0:
            dve.wait_ge(self.S['w_ok'], CC)
        if n == 3:
            dve.wait_ge(self.w_in[1], 16 * (1 + TILES))
        nc.vector.tensor_copy(high.bitcast(F32R), raw).then_inc(self.S['w_split'], 1)
        dve.wait_ge(self.S['w_split'], 2 * n + 1)
        nc.vector.tensor_tensor(low.bitcast(F32R), raw, high, ALU.subtract).then_inc(self.S['w_split'], 1)
        dve.wait_ge(self.S['w_split'], 2 * n + 2)

    def table(self, nc, dve, t, k):
        unit = 2 * t + k
        link = counted(dve, self.S['dve_k'], 5 * unit)
        dve.wait_ge(self.S['rope_in'], 48)
        if unit:
            dve.wait_ge(self.S['tab_ok'], 3 * unit)
        rope_s, rope_g = self.rope_s, self.rope_g
        cos, sin = self.rope_in[:, t, 0], self.rope_in[:, t, 1]
        link(nc.vector.tensor_tensor(rope_s[:, k], cos, rope_g[:, k], ALU.mult))
        link(nc.vector.tensor_tensor(rope_s[:, 2 + k], sin, rope_g[:, 2 + k], ALU.mult))
        link(nc.vector.tensor_tensor(rope_s[:, 4 + k], cos, rope_g[:, 4 + k], ALU.mult))
        link(nc.vector.tensor_tensor(rope_s[:, 6], sin, rope_g[:, 6 + k], ALU.mult))
        link(nc.vector.tensor_tensor(rope_s[:, 4 + k], rope_s[:, 4 + k], rope_s[:, 6], ALU.add))
        for n in range(3):
            nc.vector.tensor_copy(
                self.tabs[:, n, t, k * C:(k + 1) * C].rearrange("p (h d) -> p h d", d=HD),
                rope_s[:, 2 * n + k].unsqueeze(1).broadcast_to([TP, HEADS, HD])).then_inc(self.S['tab_ok'], 1)


def patch_tokens(nc, io, consts, h_dram, patch_dram, gv_dram, gs_dram):
    with ExitStack() as ctx:
        def sb(name, shape, dt=F32):
            return ctx.enter_context(nc.sbuf_tensor(name, shape, dt))

        def sem(name):
            return ctx.enter_context(nc.semaphore(name))

        def row(name):
            return rows[:, ROWS.index(name), :]

        ident = consts.ident
        xcols = sb("xcols", [KROWS, X_SLOTS, KCH, LOAD_CELLS * P])
        xs = Split(sb("xs_hi", [KROWS, XS_SLOTS, KCH, P]), sb("xs_lo", [KROWS, XS_SLOTS, KCH, P]))
        w_conv = Split(sb("w_conv_hi", [KROWS, KCH, C]), sb("w_conv_lo", [KROWS, KCH, C]))
        w_q = sb("w_q", [P, CC, C])
        w_kv = Split(sb("w_kv_hi", [P, CC, 2 * C]), sb("w_kv_lo", [P, CC, 2 * C]))
        w_proj = sb("w_proj", [P, CC, C])
        w_gq = sb("w_gq", [P, CC, C])
        w_gkv = sb("w_gkv", [P, CC, 2 * C])
        w_gproj = sb("w_gproj", [P, CC, C])
        w_mod = sb("w_mod", [P, CC, C])
        rows = sb("rows", [P, TOKEN_ROWS, C])
        cols = sb("cols", [P, len(COLS), CC])
        beta_wide = sb("beta_wide", [P, 3, CC, P])
        eps = sb("eps1", [P, 1])
        bias_q = sb("bias_q", [P, C])
        bias_kv = sb("bias_kv", [P, 2 * C])
        bias_gkv = sb("bias_gkv", [P, 2 * C])
        gq = sb("gq", [P, C])
        gq_kb = sb("gq_kb", [P, LH])
        cls_n = sb("cls_n", [P, C])
        pe = sb("pe", [P, 2, CELLS, C])
        stats = sb("stats", [P, 2, CELLS, 6])
        mv = sb("mv", [P, 2, CELLS, 2])
        rstd = sb("rstd", [P, 2, CELLS])
        lnv = sb("lnv", [P, CELLS])
        red = sb("red", [P, 3, C])
        qn = sb("qn", [P, C])
        s_stats = sb("s_stats", [P, 6])
        s_mv = sb("s_mv", [P, 2])
        s_rstd = sb("s_rstd", [P, 1])
        s_lnv = sb("s_lnv", [P, 1])
        smT = sb("smT", [P, CC, P])
        q = sb("q", [P, C])
        q_kb = sb("q_kb", [P, 2, LH])
        xhT = Split(sb("xhT_hi", [P, XHT_SLOTS, CC, P]), sb("xhT_lo", [P, XHT_SLOTS, CC, P]))
        prod = sb("prod", [P, C])
        score = sb("score", [P, 2, CELLS, LH])
        v = sb("v", [P, 2, CELLS, C])
        attn = sb("attn", [P, CELLS, LH])
        smax = sb("smax", [P, LH])
        ssum = sb("ssum", [P, LH])
        vw = sb("vw", [P, CELLS, C])
        agg = sb("agg", [P, C])
        redb = sb("redb", [P, C])
        lo = sb("lo", [P, C])
        ln_lo = sb("ln_lo", [P, C])
        patch = sb("patch", [P, C])
        gs = sb("gs", [P, LH])
        gv = sb("gv", [P, C])
        t_stats = sb("t_stats", [P, 6])
        t_mv = sb("t_mv", [P, 2])
        t_rstd = sb("t_rstd", [P, 1])
        t_lnv = sb("t_lnv", [P, 1])
        tT = sb("tT", [P, CC, P])
        vw_row, pe_row = vw[:].rearrange("p n c -> p (n c)"), pe[:].rearrange("p s n c -> p s (n c)")
        w_conv_raw = vw_row[0:KROWS, 0:KCH * C].rearrange("p (k n) -> p k n", k=KCH)
        w_kv_raw = vw_row[:, KCH * C:KCH * C + CC * 2 * C].rearrange("p (k n) -> p k n", k=CC)
        consts.place_raw(pe_row[:, (STEPS - 2) % 2], pe_row[:, (STEPS - 1) % 2])
        cls_gv = vw[:, :, 0:P]
        cls_gs = sb("cls_gs", [P, WINDOWS, LH // 2])
        cls_out = sb("cls_out", [IMAGES, C])
        p_conv = ctx.enter_context(nc.psum_tensor("p_conv", [P, CONV_SLOTS, 2 * C], F32))
        p_xhT = ctx.enter_context(nc.psum_tensor("p_xhT", [P, 2, 4, P], F32))
        p_kv = ctx.enter_context(nc.psum_tensor("p_kv", [P, KV_SLOTS, 2 * C], F32))
        p_T = ctx.enter_context(nc.psum_tensor("p_T", [P, 4, P], F32))
        p_mm = ctx.enter_context(nc.psum_tensor("p_mm", [P, 2 * C], F32))

        names = ("w_in v_in wc_in wc_hi w_lo xs_hi xs_lo xT_lo ident_ok consts beta_ok bias_mm bias_out gamma_in cls_norm clsT cls_qT cls_q "
                 "conv_ok pe_out stat_ok rstd_ok norm_ok red_ok qv_ok qr_ok qn_ok qT_ok qT_out q_mm q_ok "
                 "xT_ok xT_out kv_ok k_read v_out score_ok m_ok e_ok att_ok vw_ok agg_ok aggT_ok aggT_out proj_ok "
                 "lo_ok loT_ok loT_out mod_ok patch_ok tv_ok tr_ok tn_ok tnT_ok tnT_out gkv_ok g_ok redb_ok "
                 "c_in c_max c_exp c_out gq_ok dve_1 act_1 pool_1").split()
        S = {n: sem(n) for n in names}
        x_in = [sem(f"x_in{n}") for n in range(X_SLOTS)]
        st_patch = [sem("st_patch0"), sem("st_patch1")]
        st_g = [sem("st_g0"), sem("st_g1")]
        st_cls = sem("st_cls")
        block = ctx.enter_context(nc.Block())
        weights = [(w_q[:], 'la_wq'), (w_kv_raw, 'la_wkv'), (w_gq[:], 'ga_wq'), (w_gkv[:], 'ga_wkv'),
                   (w_proj[:], 'la_proj_w'), (w_gproj[:], 'ga_proj_w'), (w_mod[:], 'mod_w')]
        ITER = STEPS + 3
        SETUP_LATE = 2
        VW_AT = [5, 6, 7]
        XS_AHEAD = XS_SLOTS - 1

        def cell(k):
            m, q, c = TOK_M[k // CELLS], k // LOAD_CELLS, k % LOAD_CELLS
            return m, xcols[:, q % X_SLOTS, :, c * m:(c + 1) * m]

        @block.sync
        def _(sp):
            def load_x(q):
                s, j = q // (CELLS // LOAD_CELLS), q % (CELLS // LOAD_CELLS)
                m = LOAD_CELLS * TOK_M[s]
                if q >= X_SLOTS:
                    sp.wait_ge(S['xs_lo'], LOAD_CELLS * (q - X_SLOTS + 1))
                src = io['x_cols'][s, :, j * m:(j + 1) * m].rearrange("(k p) m -> p k m", p=KROWS)
                sp.dma_start(xcols[:, q % X_SLOTS, :, 0:m], src).then_inc(x_in[q % X_SLOTS], 16)

            h_rows = h_dram.rearrange("(b s) c -> b s c", s=SEQ)
            sp.dma_start(w_conv_raw, io['conv_w'].rearrange("(k p) n -> p k n", p=KROWS)).then_inc(S['wc_in'], 16)
            for q in range(X_SLOTS):
                load_x(q)
            sp.dma_start(cols[:], io['cols']).then_inc(S['v_in'], 16)
            sp.dma_start(rows[:], io['rows'][0:TOKEN_ROWS].unsqueeze(0).broadcast_to([P, TOKEN_ROWS, C])).then_inc(S['v_in'], 16)
            load_x(X_SLOTS)
            for w, name in weights:
                sp.dma_start(w, io[name].rearrange("(k p) n -> p k n", p=P)).then_inc(S['w_in'], 16)
            sp.dma_start(h_rows[:, WINDOWS + 1:, :], io['txt']).then_inc(st_cls, 16)
            for it in range(ITER):
                if it == 1:
                    consts.load_tables(nc, sp, io)
                if it >= STEPS and it < STEPS + 2:
                    sp.wait_ge(S['xT_ok'], CELLS * (it - 1))
                    consts.load_weights(nc, sp, io, it - STEPS)
                q = X_SLOTS + it * (CELLS // LOAD_CELLS)
                w = it - 3
                for n in range(CELLS // LOAD_CELLS):
                    if X_SLOTS < q + n < LOADS:
                        load_x(q + n)
                    if n == 1 and 0 <= w < STEPS:
                        M, w0 = TOK_M[w], P * w
                        sp.wait_ge(S['patch_ok'], w + 1)
                        sp.dma_start(patch_dram[w0:w0 + M, :], patch[0:M, :]).then_inc(st_patch[w % 2], 16)
                if 0 <= w < STEPS:
                    sp.wait_ge(S['g_ok'], 2 * (w + 1))
                    sp.dma_start(gv_dram[w0:w0 + M, :], gv[0:M, :]).then_inc(st_g[w % 2], 16)
                    for s in range(2):
                        sp.dma_start(gs_dram[s, w0:w0 + M, :], gs[0:M, s * LH // 2:(s + 1) * LH // 2]
                                     ).then_inc(st_g[w % 2], 16)
            for h in range(2):
                n = len(range(h, STEPS, 2))
                sp.wait_ge(st_g[h], 48 * n)
                sp.wait_ge(st_patch[h], 16 * n)
            for s in range(2):
                r = slice(IMAGES * s, IMAGES * (s + 1))
                sp.dma_start(cls_gs[r], gs_dram[s].rearrange("(b n) h -> b n h", n=WINDOWS)).then_inc(S['c_in'], 16)
                sp.dma_start(cls_gv[r], gv_dram.rearrange("(b n) c -> b n c", n=WINDOWS)[:, :, P * s:P * (s + 1)]
                             ).then_inc(S['c_in'], 16)
            sp.dma_start(h_rows[:, 0:WINDOWS, :], patch_dram.rearrange("(b n) c -> b n c", n=WINDOWS)
                         ).then_inc(st_cls, 16)
            sp.wait_ge(S['c_out'], 1)
            sp.dma_start(h_rows[:, WINDOWS, :], cls_out[:]).then_inc(st_cls, 16)
            sp.wait_ge(st_cls, 48)

        @block.gpsimd
        def _(pool):
            link = counted(pool, S['pool_1'])
            link(nc.gpsimd.memset(ident[:], 0.0))
            nc.gpsimd.affine_select(out=ident[:], in_=ident[:], compare_op=ALU.not_equal, fill=1.0, base=0,
                                    pattern=[[-1, P]], channel_multiplier=1).then_inc(S['ident_ok'], 1)
            nc.gpsimd.memset(eps[:], 1e-5).then_inc(S['consts'], 1)
            consts.fill(nc, pool)
            def split_low(k):
                m, raw = cell(k)
                pool.wait_ge(S['xs_hi'], k + 1)
                nc.gpsimd.tensor_tensor(xs.lo[:, k % XS_SLOTS, :, 0:m].bitcast(F32R), raw, xs.hi[:, k % XS_SLOTS, :, 0:m],
                                        ALU.subtract).then_inc(S['xs_lo'], 1)
                pool.wait_ge(S['xs_lo'], k + 1)

            for k in range(XS_AHEAD):
                split_low(k)
            for it in range(ITER):
                if it == STEPS + 1:
                    pool.wait_ge(S['xT_ok'], CELLS * STEPS)
                    nc.gpsimd.memset(consts.raw[4], 0.0).then_inc(consts.S['zeroed'], 1)
                    pool.wait_ge(consts.S['zeroed'], 1)
                s, u = it, it - 2
                for n in range(CELLS):
                    if s < STEPS and n > 0:
                        M, k = TOK_M[s], (CELLS - 1) * s + n
                        pool.wait_ge(S['pe_out'], CELLS * s + n + 1)
                        first = pe[0:M, s % 2, 0] if n == 1 else red[0:M, s % 3]
                        nc.gpsimd.tensor_tensor(red[0:M, s % 3], first, pe[0:M, s % 2, n],
                                                ALU.add).then_inc(S['red_ok'], 1)
                        pool.wait_ge(S['red_ok'], k)
                    if CELLS * s + n + XS_AHEAD < CELLS * STEPS:
                        split_low(CELLS * s + n + XS_AHEAD)
                    if not 0 <= u < STEPS:
                        continue
                    M = TOK_M[u]
                    if n in VW_AT:
                        j = VW_AT.index(n)
                        c0, c1 = j * CELLS // len(VW_AT), (j + 1) * CELLS // len(VW_AT)
                        pool.wait_ge(S['att_ok'], u + 1)
                        pool.wait_ge(S['v_out'], CELLS * (u + 1))
                        if u >= 1:
                            pool.wait_ge(S['agg_ok'], u)
                        nc.gpsimd.tensor_tensor(
                            vw[0:M, c0:c1].rearrange("p n (h d) -> p (n h) d", h=LH),
                            v[0:M, u % 2, c0:c1].rearrange("p n (h d) -> p (n h) d", h=LH),
                            attn[0:M, c0:c1].rearrange("p n h -> p (n h)").unsqueeze(2).broadcast_to(
                                [M, (c1 - c0) * LH, LD]), ALU.mult).then_inc(S['vw_ok'], 1)
                    if n == CELLS - 1:
                        if u >= 1:
                            pool.wait_ge(S['lo_ok'], u)
                        pool.wait_ge(S['v_in'], 32)
                        nc.gpsimd.tensor_tensor(redb[0:M], red[0:M, u % 3], row('la_proj_b')[0:M],
                                                ALU.add).then_inc(S['redb_ok'], 1)

        @block.scalar
        def _(act):
            link = counted(act, S['act_1'])
            act.preload_act_table_set("natural_log_exp_and_others")
            act.wait_ge(S['consts'], 1)

            def rstd_of(M, var, tmp, out, signal):
                link(nc.scalar.activation(tmp, var, ACT.Ln, bias=eps[0:M, 0:1]))
                nc.scalar.activation(out, tmp, ACT.Exp, scale=-0.5).then_inc(S[signal], 1)

            def split_high(k):
                m, raw = cell(k)
                q = k // LOAD_CELLS
                if k % LOAD_CELLS == 0:
                    act.wait_ge(x_in[q % X_SLOTS], 16 * (q // X_SLOTS + 1))
                if k >= XS_SLOTS:
                    act.wait_ge(S['conv_ok'], k - XS_SLOTS + 1)
                nc.scalar.copy(xs.hi[:, k % XS_SLOTS, :, 0:m].bitcast(F32R), raw).then_inc(S['xs_hi'], 1)

            act.wait_ge(S['wc_in'], 16)
            nc.scalar.copy(w_conv.hi[:].bitcast(F32R), w_conv_raw).then_inc(S['wc_hi'], 1)
            for k in range(XS_AHEAD):
                split_high(k)
            for it in range(ITER):
                s, r, u, w = it, it - 1, it - 2, it - 3
                for n in range(CELLS + 3):
                    if it == 0 and n == 4 + SETUP_LATE:
                        act.wait_ge(S['cls_norm'], 1)
                        rstd_of(P, t_mv[:, 1:2], t_lnv[:], t_rstd[:], 'tr_ok')
                    if it == 0 and n == 8 + SETUP_LATE:
                        act.wait_ge(S['clsT'], 1)
                        nc.scalar.copy(tT[:], p_T[:, 0:CC]).then_inc(S['cls_qT'], 1)
                    if s < STEPS and n < CELLS:
                        M, k = TOK_M[s], CELLS * s + n
                        act.wait_ge(S['conv_ok'], k + 1)
                        if n == 0 and s >= 2:
                            act.wait_ge(S['xT_ok'], CELLS * (s - 1))
                        nc.scalar.copy(pe[0:M, s % 2, n], p_conv[0:M, k % CONV_SLOTS, 0:C]).then_inc(S['pe_out'], 1)
                        if k + XS_AHEAD < CELLS * STEPS:
                            split_high(k + XS_AHEAD)
                    if 0 <= r < STEPS and n == 1:
                        M = TOK_M[r]
                        act.wait_ge(S['qv_ok'], r + 1)
                        rstd_of(M, s_mv[0:M, 1:2], s_lnv[0:M], s_rstd[0:M], 'qr_ok')
                    if 0 <= w < STEPS:
                        M = TOK_M[w]
                        if n == 4:
                            act.wait_ge(S['aggT_ok'], w + 1)
                            nc.scalar.copy(tT[:, :, 0:M], p_T[:, 0:CC, 0:M]).then_inc(S['aggT_out'], 1)
                        if n == 6:
                            act.wait_ge(S['tv_ok'], w + 1)
                            rstd_of(M, t_mv[0:M, 1:2], t_lnv[0:M], t_rstd[0:M], 'tr_ok')
                        if n == 6:
                            act.wait_ge(S['loT_ok'], w + 1)
                            nc.scalar.copy(tT[:, :, 0:M], p_T[:, 0:CC, 0:M]).then_inc(S['loT_out'], 1)
                        if n == 8:
                            act.wait_ge(S['tnT_ok'], w + 1)
                            nc.scalar.copy(tT[:, :, 0:M], p_T[:, 0:CC, 0:M]).then_inc(S['tnT_out'], 1)
                    if 0 <= r < STEPS and n == 2:
                        M = TOK_M[r]
                        act.wait_ge(S['qT_ok'], r + 1)
                        nc.scalar.copy(smT[:, :, 0:M], p_T[:, 0:CC, 0:M]).then_inc(S['qT_out'], 1)
                    if 0 <= r < STEPS and n >= 2 and n - 2 < CELLS:
                        M, m = TOK_M[r], n - 2
                        k = CELLS * r + m
                        act.wait_ge(S['xT_ok'], k + 1)
                        if k >= XHT_SLOTS:
                            act.wait_ge(S['kv_ok'], k - XHT_SLOTS + 1)
                        nc.scalar.copy(xhT.hi[:, k % XHT_SLOTS, :, 0:M].bitcast(F32R), p_xhT[:, k % 2, 0:CC, 0:M]).then_inc(S['xT_out'], 1)
                    if 0 <= r < STEPS and n >= 3:
                        M, m = TOK_M[r], n - 3
                        k = CELLS * r + m
                        act.wait_ge(S['k_read'], k + 1)
                        if m == 0 and r >= 2:
                            act.wait_ge(S['vw_ok'], len(VW_AT) * (r - 1))
                        nc.scalar.copy(v[0:M, r % 2, m], p_kv[0:M, k % KV_SLOTS, C:2 * C]).then_inc(S['v_out'], 1)
                    if 0 <= u < STEPS and n == 4:
                        M = TOK_M[u]
                        act.wait_ge(S['m_ok'], u + 1)
                        nc.scalar.activation(attn[0:M], attn[0:M], ACT.Exp).then_inc(S['e_ok'], 1)
                if s < STEPS:
                    M = TOK_M[s]
                    act.wait_ge(S['stat_ok'], CELLS * (s + 1))
                    rstd_of(M, mv[0:M, s % 2, :, 1], lnv[0:M], rstd[0:M, s % 2], 'rstd_ok')
            act.wait_ge(S['c_max'], 1)
            nc.scalar.activation(cls_gs[:], cls_gs[:], ACT.Exp).then_inc(S['c_exp'], 1)
            act.wait_ge(S['aggT_ok'], STEPS + 1)
            nc.scalar.copy(tT[:, :, 0:IMAGES], p_T[:, 0].rearrange("p (c b) -> p c b", c=CC)).then_inc(S['aggT_out'], 1)

        @block.vector
        def _(dve):
            link = counted(dve, S['dve_1'])

            def moments(M, x, st, m_v, signal):
                link(nc.vector.bn_stats(st, x))
                nc.vector.bn_aggr(m_v, st).then_inc(S[signal], 1)

            dve.wait_ge(S['wc_hi'], 1)
            nc.vector.tensor_tensor(w_conv.lo[:].bitcast(F32R), w_conv_raw, w_conv.hi[:],
                                    ALU.subtract).then_inc(S['w_lo'], 1)
            dve.wait_ge(S['v_in'], 32)
            for k in range(3):
                for c in range(CC):
                    nc.vector.tensor_copy(beta_wide[:, k, c],
                                          cols[:, 3 + k, c:c + 1].broadcast_to([P, P])).then_inc(S['beta_ok'], 1)
            moments(P, row('class_emb'), t_stats[:], t_mv[:], 'cls_norm')
            def setup(n):
                if n == 5:
                    dve.wait_ge(S['tr_ok'], 1)
                    link(nc.vector.tensor_scalar(cls_n[:], row('class_emb'), t_mv[:, 0:1], t_rstd[:, 0:1],
                                                 ALU.subtract, ALU.mult))
                    link(nc.vector.tensor_tensor(cls_n[:], cls_n[:], row('ga_ln_q_g'), ALU.mult))
                    nc.vector.tensor_tensor(cls_n[:], cls_n[:], row('ga_ln_q_b'), ALU.add).then_inc(S['cls_norm'], 1)
                if n == 6:
                    dve.wait_ge(S['bias_mm'], 1)
                    nc.vector.tensor_scalar(bias_q[:], p_kv[:, 0, 0:C], C ** -0.5, None,
                                            ALU.mult).then_inc(S['bias_out'], 1)
                    dve.wait_ge(S['bias_mm'], 2)
                    nc.vector.tensor_copy(bias_kv[:], p_kv[:, 1]).then_inc(S['bias_out'], 1)
                if n == 7:
                    dve.wait_ge(S['bias_mm'], 3)
                    nc.vector.tensor_copy(bias_gkv[:], p_kv[:, 0]).then_inc(S['bias_out'], 1)
                    for k, (raw, out) in enumerate(((w_q[:], w_q[:]), (w_kv_raw, w_kv.hi[:].bitcast(F32R)),
                                                    (w_gkv[:], w_gkv[:]))):
                        for c in range(CC):
                            nc.vector.tensor_scalar(out[:, c], raw[:, c], cols[:, k, c:c + 1], None,
                                                    ALU.mult).then_inc(S['gamma_in'], 1)
                if n == 8:
                    dve.wait_ge(S['gamma_in'], 6)
                    for c in range(CC):
                        nc.vector.scalar_tensor_tensor(w_kv.lo[:, c].bitcast(F32R), w_kv_raw[:, c], cols[:, 1, c:c + 1],
                                                       w_kv.hi[:, c], ALU.mult, ALU.subtract).then_inc(S['w_lo'], 1)
                if n == 9:
                    dve.wait_ge(S['cls_q'], 1)
                    nc.vector.tensor_scalar(gq[:], p_mm[:, 0:C], C ** -0.5, None, ALU.mult).then_inc(S['gq_ok'], 1)
                    dve.wait_ge(S['gq_ok'], 1)
                    dve.wait_ge(S['bias_out'], 3)
                    link(nc.vector.tensor_tensor(prod[:], gq[:], bias_gkv[:, 0:C], ALU.mult))
                    link(nc.vector.reduce_sum(gq_kb[:], prod[:].rearrange("p (h d) -> p h d", h=LH), AX_X))

            def sum_values(w):
                M = TOK_M[w]
                dve.wait_ge(S['vw_ok'], len(VW_AT) * (w + 1))
                link(nc.vector.reduce_sum(agg[0:M], vw[0:M].rearrange("p n c -> p c n"), AX_X))
                nc.vector.tensor_tensor(agg[0:M], agg[0:M], bias_kv[0:M, C:2 * C], ALU.add).then_inc(S['agg_ok'], 1)

            def normalise(r, n):
                M = TOK_M[r]
                nc.vector.tensor_scalar(pe[0:M, r % 2, n], pe[0:M, r % 2, n], mv[0:M, r % 2, n, 0:1],
                                        rstd[0:M, r % 2, n:n + 1], ALU.subtract, ALU.mult).then_inc(S['norm_ok'], 1)

            for it in range(ITER):
                s, r, u, w = it, it - 1, it - 2, it - 3
                for n in range(CELLS + 3):
                    if it == 0:
                        setup(n - SETUP_LATE)
                    if it == 4 and n < 2 * TILES:
                        consts.table(nc, dve, n // 2, n % 2)
                    if it == STEPS + 1 and n == 6:
                        consts.centre(nc, dve)
                    if it == STEPS + 1 and 7 <= n < 10:
                        consts.split(nc, dve, n - 7)
                    if it == STEPS + 2 and n in (4, 6):
                        consts.split(nc, dve, 3 if n == 4 else 4)
                    if s < STEPS and n < CELLS:
                        M, k = TOK_M[s], CELLS * s + n
                        dve.wait_ge(S['pe_out'], k + 1)
                        moments(M, pe[0:M, s % 2, n], stats[0:M, s % 2, n], mv[0:M, s % 2, n], 'stat_ok')
                    if 0 <= w < STEPS:
                        M = TOK_M[w]
                        if n == 5:
                            dve.wait_ge(S['proj_ok'], w + 1)
                            dve.wait_ge(S['redb_ok'], w + 1)
                            nc.vector.tensor_tensor(lo[0:M], p_mm[0:M, 0:C], redb[0:M], ALU.add).then_inc(S['lo_ok'], 1)
                            dve.wait_ge(S['lo_ok'], w + 1)
                            moments(M, lo[0:M], t_stats[0:M], t_mv[0:M], 'tv_ok')
                        if n == 6:
                            dve.wait_ge(S['tr_ok'], w + 2)
                            nc.vector.tensor_scalar(ln_lo[0:M], lo[0:M], t_mv[0:M, 0:1], t_rstd[0:M, 0:1],
                                                    ALU.subtract, ALU.mult).then_inc(S['tn_ok'], 1)
                        if n == 7:
                            dve.wait_ge(S['mod_ok'], w + 1)
                            if w >= 1:
                                dve.wait_ge(st_patch[(w - 1) % 2], 16 * ((w - 1) // 2 + 1))
                            nc.vector.tensor_tensor(patch[0:M], p_mm[0:M, 0:C], row('mod_b')[0:M],
                                                    ALU.add).then_inc(S['patch_ok'], 1)
                        if n == 10:
                            dve.wait_ge(S['gkv_ok'], w + 1)
                            link(nc.vector.tensor_tensor(prod[0:M], p_mm[0:M, 0:C], gq[0:M], ALU.mult))
                            if w >= 1:
                                dve.wait_ge(st_g[(w - 1) % 2], 48 * ((w - 1) // 2 + 1))
                            link(nc.vector.reduce_sum(gs[0:M], prod[0:M].rearrange("p (h d) -> p h d", h=LH), AX_X))
                            nc.vector.tensor_tensor(gs[0:M], gs[0:M], gq_kb[0:M], ALU.add).then_inc(S['g_ok'], 1)
                            nc.vector.tensor_tensor(gv[0:M], p_mm[0:M, C:2 * C], bias_gkv[0:M, C:2 * C],
                                                    ALU.add).then_inc(S['g_ok'], 1)
                            dve.wait_ge(S['g_ok'], 2 * (w + 1))
                    if 0 <= r < STEPS:
                        M = TOK_M[r]
                        if n == 0:
                            dve.wait_ge(S['rstd_ok'], r + 1)
                            dve.wait_ge(S['red_ok'], (CELLS - 1) * (r + 1))
                        if n < 3:
                            for m in range(3 * n, 3 * n + 3):
                                normalise(r, m)
                        if n == 0:
                            link(nc.vector.tensor_scalar(red[0:M, r % 3], red[0:M, r % 3], 1.0 / CELLS, None, ALU.mult))
                            moments(M, red[0:M, r % 3], s_stats[0:M], s_mv[0:M], 'qv_ok')
                        if n == 1:
                            dve.wait_ge(S['qr_ok'], r + 1)
                            if r >= 1:
                                dve.wait_ge(S['qT_ok'], r)
                            nc.vector.tensor_scalar(qn[0:M], red[0:M, r % 3], s_mv[0:M, 0:1], s_rstd[0:M, 0:1],
                                                    ALU.subtract, ALU.mult).then_inc(S['qn_ok'], 1)
                        if n == 3:
                            dve.wait_ge(S['q_mm'], r + 1)
                            nc.vector.scalar_tensor_tensor(q[0:M], p_mm[0:M, 0:C], C ** -0.5, bias_q[0:M],
                                                           ALU.mult, ALU.add).then_inc(S['q_ok'], 1)
                            dve.wait_ge(S['q_ok'], r + 1)
                            link(nc.vector.tensor_tensor(prod[0:M], q[0:M], bias_kv[0:M, 0:C], ALU.mult))
                            link(nc.vector.reduce_sum(q_kb[0:M, r % 2], prod[0:M].rearrange("p (h d) -> p h d", h=LH),
                                                      AX_X))
                        if 2 <= n < CELLS + 2:
                            k = CELLS * r + n - 2
                            dve.wait_ge(S['xT_out'], k + 1)
                            nc.vector.tensor_tensor(xhT.lo[:, k % XHT_SLOTS, :, 0:M].bitcast(F32R),
                                                    p_xhT[:, k % 2, 0:CC, 0:M], xhT.hi[:, k % XHT_SLOTS, :, 0:M],
                                                    ALU.subtract).then_inc(S['xT_lo'], 1)
                        if n >= 3:
                            m = n - 3
                            k = CELLS * r + m
                            dve.wait_ge(S['kv_ok'], k + 1)
                            nc.vector.tensor_tensor(prod[0:M], p_kv[0:M, k % KV_SLOTS, 0:C], q[0:M],
                                                    ALU.mult).then_inc(S['k_read'], 1)
                            dve.wait_ge(S['k_read'], k + 1)
                            nc.vector.reduce_sum(score[0:M, r % 2, m], prod[0:M].rearrange("p (h d) -> p h d", h=LH),
                                                 AX_X).then_inc(S['score_ok'], 1)
                            dve.wait_ge(S['score_ok'], k + 1)
                    if 0 <= u < STEPS:
                        M = TOK_M[u]
                        if n == 2:
                            dve.wait_ge(S['score_ok'], CELLS * (u + 1))
                            if u >= 1:
                                dve.wait_ge(S['vw_ok'], len(VW_AT) * u)
                            link(nc.vector.tensor_tensor(attn[0:M], score[0:M, u % 2],
                                                         q_kb[0:M, u % 2].unsqueeze(1).broadcast_to([M, CELLS, LH]),
                                                         ALU.add))
                            link(nc.vector.reduce_max(smax[0:M], attn[0:M].rearrange("p n h -> p h n"), AX_X))
                            nc.vector.tensor_tensor(attn[0:M], attn[0:M],
                                                    smax[0:M].unsqueeze(1).broadcast_to([M, CELLS, LH]),
                                                    ALU.subtract).then_inc(S['m_ok'], 1)
                        if n == 4:
                            dve.wait_ge(S['e_ok'], u + 1)
                            link(nc.vector.reduce_sum(ssum[0:M], attn[0:M].rearrange("p n h -> p h n"), AX_X))
                            link(nc.vector.reciprocal(ssum[0:M], ssum[0:M]))
                            nc.vector.tensor_tensor(attn[0:M], attn[0:M],
                                                    ssum[0:M].unsqueeze(1).broadcast_to([M, CELLS, LH]),
                                                    ALU.mult).then_inc(S['att_ok'], 1)
                    if 0 <= w < STEPS - 2 and n == 2:
                        sum_values(w)
                    if STEPS - 2 <= u < STEPS and n == 10:
                        sum_values(u)
            H2 = LH // 2
            dve.wait_ge(S['c_in'], 64)
            link(nc.vector.reduce_max(smax[:, 0:H2], cls_gs[:].rearrange("p n h -> p h n"), AX_X))
            nc.vector.tensor_tensor(cls_gs[:], cls_gs[:], smax[:, 0:H2].unsqueeze(1).broadcast_to([P, WINDOWS, H2]),
                                    ALU.subtract).then_inc(S['c_max'], 1)
            dve.wait_ge(S['c_exp'], 1)
            link(nc.vector.reduce_sum(ssum[:, 0:H2], cls_gs[:].rearrange("p n h -> p h n"), AX_X))
            link(nc.vector.reciprocal(ssum[:, 0:H2], ssum[:, 0:H2]))
            gv4 = cls_gv.rearrange("p n (h d) -> p n h d", h=H2)
            link(nc.vector.tensor_tensor(gv4, gv4, cls_gs[:].unsqueeze(3).broadcast_to([P, WINDOWS, H2, LD]), ALU.mult))
            link(nc.vector.reduce_sum(agg[:, 0:P], cls_gv.rearrange("p n c -> p c n"), AX_X))
            agg3 = agg[:, 0:P].rearrange("p (h d) -> p h d", h=H2)
            nc.vector.tensor_tensor(agg3, agg3, ssum[:, 0:H2].unsqueeze(2).broadcast_to([P, H2, LD]),
                                    ALU.mult).then_inc(S['agg_ok'], 1)
            M = IMAGES
            link(nc.vector.tensor_tensor(lo[0:M], row('class_emb')[0:M], row('ga_proj_b')[0:M], ALU.add))
            dve.wait_ge(S['proj_ok'], STEPS + 1)
            nc.vector.tensor_tensor(cls_out[:], p_mm[0:M, 0:C], lo[0:M], ALU.add).then_inc(S['c_out'], 1)

        @block.tensor
        def _(pe_):
            def mm(out, lhs, rhs, signal=None):
                for c, (a, b) in enumerate(zip(lhs, rhs)):
                    last = nc.tensor.matmul(out, a, b, start=(c == 0), stop=(c == len(lhs) - 1))
                if signal:
                    last.then_inc(S[signal], 1)

            def mm_split(out, lhs, rhs, signal):
                parts = [(lhs.hi, rhs.hi), (lhs.hi, rhs.lo), (lhs.lo, rhs.hi)]
                mm(out, [x.bitcast(F32R) for a, _ in parts for x in a], [x.bitcast(F32R) for _, b in parts for x in b],
                   signal)

            def transpose(out, x, M, signal):
                for c in range(CC):
                    last = nc.tensor.transpose(out[:, c, 0:M], x[0:M, c * P:(c + 1) * P], ident[0:M, 0:M])
                last.then_inc(S[signal], 1)

            def xh_transpose(r, m):
                k = CELLS * r + m
                pe_.wait_ge(S['norm_ok'], k + 1)
                if k >= 2:
                    pe_.wait_ge(S['xT_lo'], k - 1)
                transpose(p_xhT[:, k % 2], pe[:, r % 2, m], TOK_M[r], 'xT_ok')

            def kv(r, m):
                M, k = TOK_M[r], CELLS * r + m
                pe_.wait_ge(S['xT_lo'], k + 1)
                if k >= KV_SLOTS:
                    pe_.wait_ge(S['v_out'], k - KV_SLOTS + 1)
                if k == 0:
                    pe_.wait_ge(S['w_lo'], 1 + CC)
                    pe_.wait_ge(S['bias_out'], 3)
                mm_split(p_kv[0:M, k % KV_SLOTS], xhT.chunks(lambda x, c: x[:, k % XHT_SLOTS, c, 0:M]),
                         w_kv.chunks(lambda x, c: x[:, c]), 'kv_ok')

            def setup(n):
                if n == 5 or n == 6:
                    pe_.wait_ge(S['w_in'], 16 * len(weights))
                    pe_.wait_ge(S['beta_ok'], 3 * CC)
                    for k in (0, 1) if n == 5 else (2,):
                        w, width = ((w_q[:], C), (w_kv_raw, 2 * C), (w_gkv[:], 2 * C))[k]
                        if k == 2:
                            pe_.wait_ge(S['bias_out'], 1)
                        mm(p_kv[:, k % 2, 0:width], [beta_wide[:, k, c] for c in range(CC)],
                           [w[:, c] for c in range(CC)], 'bias_mm')
                if n == 7:
                    pe_.wait_ge(S['ident_ok'], 1)
                    pe_.wait_ge(S['cls_norm'], 2)
                    transpose(p_T, cls_n, P, 'clsT')
                if n == 8:
                    pe_.wait_ge(S['cls_qT'], 1)
                    mm(p_mm[:, 0:C], [tT[:, c] for c in range(CC)], [w_gq[:, c] for c in range(CC)], 'cls_q')

            for it in range(ITER):
                s, r, w = it, it - 1, it - 3
                for n in range(CELLS + 3):
                    if it == 0:
                        setup(n - SETUP_LATE)
                    if s < STEPS and n < CELLS:
                        M, k = TOK_M[s], CELLS * s + n
                        if k == 0:
                            pe_.wait_ge(S['w_lo'], 1)
                        pe_.wait_ge(S['xs_lo'], k + 1)
                        if k >= CONV_SLOTS:
                            pe_.wait_ge(S['pe_out'], k - CONV_SLOTS + 1)
                        mm_split(p_conv[0:M, k % CONV_SLOTS, 0:C],
                                 xs.chunks(lambda x, j: x[:, k % XS_SLOTS, j, 0:M], KCH),
                                 w_conv.chunks(lambda x, j: x[:, j], KCH), 'conv_ok')
                    if 0 <= w < STEPS:
                        M = TOK_M[w]
                        if n == 4:
                            pe_.wait_ge(S['agg_ok'], w + 1)
                            pe_.wait_ge(S['qT_out'], min(r + 1, STEPS))
                            transpose(p_T, agg, M, 'aggT_ok')
                        if n == 5:
                            pe_.wait_ge(S['aggT_out'], w + 1)
                            pe_.wait_ge(S['q_ok'], min(r + 1, STEPS))
                            if w >= 1:
                                pe_.wait_ge(S['g_ok'], 2 * w)
                            mm(p_mm[0:M, 0:C], [tT[:, c, 0:M] for c in range(CC)], [w_proj[:, c] for c in range(CC)],
                               'proj_ok')
                        if n == 6:
                            pe_.wait_ge(S['lo_ok'], w + 1)
                            transpose(p_T, lo, M, 'loT_ok')
                        if n == 7:
                            pe_.wait_ge(S['loT_out'], w + 1)
                            mm(p_mm[0:M, 0:C], [tT[:, c, 0:M] for c in range(CC)], [w_mod[:, c] for c in range(CC)],
                               'mod_ok')
                        if n == 8:
                            pe_.wait_ge(S['tn_ok'], w + 1)
                            transpose(p_T, ln_lo, M, 'tnT_ok')
                        if n == 9:
                            pe_.wait_ge(S['tnT_out'], w + 1)
                            pe_.wait_ge(S['patch_ok'], w + 1)
                            mm(p_mm[0:M], [tT[:, c, 0:M] for c in range(CC)], [w_gkv[:, c] for c in range(CC)],
                               'gkv_ok')
                    if 0 <= r < STEPS:
                        M = TOK_M[r]
                        if n == 1:
                            xh_transpose(r, 0)
                        if n == 2:
                            pe_.wait_ge(S['qn_ok'], r + 1)
                            transpose(p_T, qn, M, 'qT_ok')
                        if n == 3:
                            pe_.wait_ge(S['qT_out'], r + 1)
                            if w >= 1:
                                pe_.wait_ge(S['g_ok'], 2 * min(w, STEPS))
                            if r == 0:
                                pe_.wait_ge(S['gamma_in'], 6)
                                pe_.wait_ge(S['gq_ok'], 1)
                            mm(p_mm[0:M, 0:C], [smT[:, c, 0:M] for c in range(CC)], [w_q[:, c] for c in range(CC)],
                               'q_mm')
                        if n >= 3:
                            if n - 2 < CELLS:
                                xh_transpose(r, n - 2)
                            kv(r, n - 3)
            pe_.wait_ge(S['agg_ok'], STEPS + 1)
            nc.tensor.transpose(p_T[:, 0, :], agg[:, 0:P], ident[:]).then_inc(S['aggT_ok'], 1)
            pe_.wait_ge(S['aggT_out'], STEPS + 1)
            pe_.wait_ge(S['g_ok'], 2 * STEPS)
            mm(p_mm[0:IMAGES, 0:C], [tT[:, c, 0:IMAGES] for c in range(CC)], [w_gproj[:, c] for c in range(CC)],
               'proj_ok')


class Group:

    def __init__(self, c, pair=0):
        self.c, self.pair, self.half = c, pair, c % 2

    def plus(self, n):
        return Group(self.c + n, self.pair)

    def after(self, per_group, k):
        n = per_group * self.c + k + 1
        return n if isinstance(self.pair, int) else self.pair * (2 * per_group) + n

    def uses(self, inc, back=0):
        n = inc * (self.c // 2 + 1 - back)
        return n if isinstance(self.pair, int) else self.pair * inc + n

    def index(self, scale=1):
        n = self.c * scale
        return n if isinstance(self.pair, int) else self.pair * (2 * scale) + n


def run_iterations(engine, body, first=-1, last=GROUPS, loop=(2, GROUPS - 2)):
    lo, hi = loop
    hi = lo + (hi - lo) // 2 * 2

    def one(i, group):
        body(group, i + 1 < GROUPS, 0 <= i < GROUPS, i >= 1)

    for i in range(first, lo):
        one(i, Group(i))
    with engine.Fori(0, (hi - lo) // 2) as pair:
        for n in range(2):
            one(lo, Group(lo + n, pair))
    for i in range(hi, last + 1):
        one(i, Group(i))


A_AT = {2: [('xT', 0)], 4: [('qk', 0)], 5: [('xT', 1)], 7: [('qk', 1)], 8: [('qkT', 0)], 9: [('xT', 2)],
        10: [('qkT', 1)], 11: [('qk', 2)], 12: [('v', 0)], 13: [('v', 1)], 15: [('qkT', 2)]}
C_AT = {0: [('proj', 0)], 2: [('yT', 0)], 3: [('ffn', 0)], 4: [('proj', 1)], 5: [('proj', 2)], 6: [('yT', 1)],
        7: [('ffn', 1)], 8: [('yT', 2)], 9: [('ffn', 2)], 12: [('twT', 0)], 13: [('lora', 0)],
        14: [('lora', 1)]}
NORM_AT = {0: 0, 3: 1, 6: 2}
K_AT = {10: 0, 15: 1}
ORDER_PE = (('scores', 'A', 'oB', 'C', 'pT', 'oN'),
            ('A', 'shift', 'C', 'pv'))
ORDER_ACT = (('oT', 'A', 'small C', 'oB', 'C', 'small A', 'pT'),
             ('A', 'exp', 'C', 'small C', 'small A'))
ORDER_DVE = (('max', 'stats A', 'norm A', 'A', 'norm C', 'oB', 'C'),
             ('o_norm', 'stats A', 'norm A', 'A', 'norm C', 'C'))
GATE_AT = 10
LORA_TILES = [(0, 1), (2,)]
A_BANK = [s for h in sorted(A_AT) for s in A_AT[h]]
C_BANK = [s for h in sorted(C_AT) for s in C_AT[h]]


def attention_ffn(nc, io, consts, h_dram, out_flat):
    with ExitStack() as ctx:
        def sb(name, shape, dt=F32):
            return ctx.enter_context(nc.sbuf_tensor(name, shape, dt))

        def ps(name, shape, dt=F32):
            return ctx.enter_context(nc.psum_tensor(name, shape, dt))

        def sem(name):
            return ctx.enter_context(nc.semaphore(name))

        ident, ident_b, tabs, earlier = consts.ident, consts.ident_b, consts.tabs, consts.earlier
        w_qk, w_v, w_p, w_f, right = (Split(hi, w) for hi, w in zip(consts.high, consts.weights))
        b_rows, eps5, eps6 = consts.b_rows, consts.eps5, consts.eps6

        ha = sb("ha", [TP, 2, TILES, C])
        hc = sb("hc", [TP, 2, TILES, C])
        a_st, a_mv = sb("a_st", [TP, 2, 6]), sb("a_mv", [TP, 2, 3])
        a_ln, a_rs = sb("a_ln", [TP, 2]), sb("a_rs", [TP, 2])
        xn = sb("xn", [TP, 2, C])
        xnT = Split(sb("xnT_hi", [P, 2, CC, GT]), sb("xnT_lo", [P, 2, CC, GT]))
        sq = sb("sq", [TP, 2 * C])
        ss, ss_ln, ss_rs = sb("ss", [TP, 2, 2 * HEADS]), sb("ss_ln", [TP, 2 * HEADS]), sb("ss_rs", [TP, 2, 2 * HEADS])
        t1, t2 = sb("t1", [TP, 2, 2 * C]), sb("t2", [TP, 2, 2 * C])
        qkT = sb("qkT", [P, 2, 4, GT + QP - SEQ])
        kb = sb("kb", [P, 2, 2, HALF, GT])
        vp = sb("vp", [QP, 2, GB, HEADS, 2 * HD])
        mx = sb("mx", [QP, 2, HALF], BF16)
        pr = sb("pr", [QP, 2, 2, 4 * SEQ])
        prT = sb("prT", [QP, 2, HALF, SEQ])
        oT = sb("oT", [P, 4, SEQ])
        rd = sb("rd", [SEQ, HEADS])
        on = sb("on", [QP, C])
        onT = Split(sb("onT_hi", [P, 2, CC, GT]), sb("onT_lo", [P, 2, CC, GT]))
        hb, h2, h2l = sb("hb", [TP, 2, C]), sb("h2", [TP, 2, C]), sb("h2l", [TP, 3, C])
        c_st, c_mv = sb("c_st", [TP, 6]), sb("c_mv", [TP, 3])
        c_ln, c_rs = sb("c_ln", [TP, 1]), sb("c_rs", [TP, 1])
        yn = sb("yn", [TP, C])
        yT = Split(sb("yT_hi", [P, CC, TP]), sb("yT_lo", [P, CC, TP]))
        f = sb("f", [TP, 3, FFN_N])
        g_max, g_sum, g_rs = sb("g_max", [TP, TILES]), sb("g_sum", [TP, TILES]), sb("g_rs", [TP, TILES])
        g_e, g_rank, g_w = (sb(n, [TP, TILES, EXPERTS]) for n in ("g_e", "g_rank", "g_w"))
        g_gt, g_eq = (sb(n, [TP, TILES, EXPERTS, EXPERTS]) for n in ("g_gt", "g_eq"))
        tw = sb("tw", [TP, TILES, LR])
        twT = Split(sb("twT_hi", [TILES * LR, TP]), sb("twT_lo", [TILES * LR, TP]))
        out_sb = sb("out_sb", [TP, 3, C])

        p_s = ps("p_s", [P, 2, 2, 512])
        p_o = ps("p_o", [P, 512])
        p_n = ps("p_n", [P, 512])
        p_a = ps("p_a", [P, 512])
        p_c = ps("p_c", [P, 512])

        names = ("vp_0 rows_0 kb_0 dve_n dve_r dve_c dve_g act_a act_r act_c pool_r pool_1 "
                 "a_var a_rstd xn_ok xT xT_out qk sq_ok ss_ok ss_rstd rot_ok rope_ok qkT_ok qkT_out v_mm v_out "
                 "s_mm s_max s_shift s_exp pT pT_out pv o_out oN o_norm oB oB_out "
                 "proj h2_ok c_var c_rstd yn_ok yT_ok yT_out ffn ffn_out g_m g_exp tw_ok twT_ok twT_out lora out_ok "
                 "hb_ok h2l_ok fb_ok xT_lo yT_lo oB_lo twT_lo").split()
        S = {n: sem("b_" + n) for n in names}
        ha_in = [sem("ha_in0"), sem("ha_in1")]
        hc_in = [sem("hc_in0"), sem("hc_in1")]
        k_in = [[sem(f"k_in{h}{n}") for n in range(2)] for h in range(2)]
        stored = [sem(f"stored{t}") for t in range(TILES)]
        block = ctx.enter_context(nc.Block())

        h_group = h_dram.rearrange("(g t p) c -> g p t c", t=TILES, p=TP)
        out_group = out_flat.rearrange("(g t p) c -> g t p c", t=TILES, p=TP)
        K_COLS = [(0, 2 * TP), (2 * TP, GT)]

        def pick(view, g):
            return view[g.index()] if isinstance(g.pair, int) else view[bass.ds(g.index(), 1)].squeeze(0)

        @block.sync
        def _(sp):
            def value(x):
                return x if isinstance(x, int) else sp.snap(x)

            def load(dst, g, landed, sem_=None, done=None):
                src = pick(h_group, g)
                if sem_ is not None:
                    sp.wait_ge(sem_, done)
                sp.dma_start(dst[:, g.half], src).then_inc(landed[g.half], 16)

            load(ha, Group(0), ha_in)

            def iteration(i, A, B, C_):
                g = i.plus(2)
                if i.c + 2 < GROUPS:
                    if i.c >= 0:
                        load(ha, g, ha_in, S['xn_ok'], value(i.after(3, 2)))
                    else:
                        load(ha, g, ha_in)
                if B:
                    if i.c >= 2:
                        load(hc, i, hc_in, S['hb_ok'], value(i.plus(-2).after(3, 2)))
                    else:
                        load(hc, i, hc_in)
                for h in range(16):
                    if A and h in K_AT:
                        n, g = K_AT[h], i.plus(1)
                        c0, c1 = K_COLS[n]
                        if n == 0 and g.c < 2:
                            sp.wait_ge(S['kb_0'], g.c + 1)
                        sp.wait_ge(S['qkT_out'], g.after(3, n + 1))
                        for k in range(2):
                            for hh in range(HALF):
                                r = slice(HD * hh, HD * hh + HD)
                                sp.dma_start(kb[r, g.half, k, hh, c0:c1],
                                             qkT[r, g.half, 2 + k, c0:c1]).then_inc(k_in[g.half][n], 16)
                    if C_:
                        for step, t in C_AT.get(h, []):
                            if step == 'lora':
                                g = i.plus(-1)
                                for t in LORA_TILES[t]:
                                    dst = out_group[g.index(), t] if isinstance(g.pair, int) else \
                                        out_group[bass.ds(g.index(), 1), t].squeeze(0)
                                    sp.wait_ge(S['out_ok'], value(g.after(3, t)))
                                    sp.dma_start(dst, out_sb[:, t]).then_inc(stored[t], 16)

            run_iterations(sp, iteration)
            for t in range(TILES):
                sp.wait_ge(stored[t], 16 * GROUPS)

        @block.gpsimd
        def _(pool):
            link = counted(pool, S['pool_1'])

            def fill_vp(half):
                link(nc.gpsimd.memset(vp[:, half, :, :, HD:], 1.0))
                link(nc.gpsimd.memset(vp[64:QP, half], 0.0))
                nc.gpsimd.memset(vp[64:SEQ, half, :, :, HD:], 1.0).then_inc(S['vp_0'], 1)
                pool.wait_ge(S['vp_0'], half + 1)

            nc.gpsimd.memset(kb[:, 0], 0.0).then_inc(S['kb_0'], 1)
            pool.wait_ge(S['kb_0'], 1)
            fill_vp(0)

            def iteration(i, A, B, C_):
                for h in range(16):
                    if i.c == -1 and h == 8:
                        for n, x in enumerate((qkT[:, :, :, GT:], prT[64:QP], on[64:QP])):
                            nc.gpsimd.memset(x, 0.0).then_inc(S['rows_0'], 1)
                            pool.wait_ge(S['rows_0'], n + 1)
                    if i.c == -1 and h == 14:
                        fill_vp(1)
                    if C_:
                        g = i.plus(-1)
                        for step, t in C_AT.get(h, []):
                            if step == 'proj':
                                if t == 0:
                                    pool.wait_ge(hc_in[g.half], g.uses(16))
                                if t > 1 or i.c > 1:
                                    pool.wait_ge(S['h2_ok'], g.after(3, t - 2))
                                nc.gpsimd.tensor_tensor(hb[:, t % 2], hc[:, g.half, t], b_rows[0:TP, 0],
                                                        ALU.add).then_inc(S['hb_ok'], 1)
                            if step == 'yT':
                                pool.wait_ge(S['h2_ok'], g.after(3, t))
                                nc.gpsimd.tensor_tensor(h2l[:, t], h2[:, t % 2], b_rows[0:TP, 1],
                                                        ALU.add).then_inc(S['h2l_ok'], 1)
                            if step == 'ffn':
                                pool.wait_ge(S['ffn_out'], g.after(3, t))
                                pool.wait_ge(S['h2l_ok'], g.after(3, t))
                                nc.gpsimd.tensor_tensor(h2l[:, t], h2l[:, t], f[:, t, 0:C],
                                                        ALU.add).then_inc(S['fb_ok'], 1)
                    if A:
                        for step, t in A_AT.get(h - 1, []):
                            if step == 'qk':
                                g, b = i.plus(1), t % 2
                                pool.wait_ge(S['rot_ok'], g.after(6, 2 * t + 1))
                                nc.gpsimd.tensor_tensor(t1[:, b], t1[:, b], t2[:, b], ALU.add).then_inc(S['pool_r'], 1)
                                pool.wait_ge(S['pool_r'], g.after(6, 2 * t))
                                pool.wait_ge(S['ss_rstd'], g.after(3, t))
                                x = t1[:, b].rearrange("p (h d) -> p h d", d=HD)
                                nc.gpsimd.tensor_tensor(x, x, ss_rs[:, b].unsqueeze(2).broadcast_to([TP, 2 * HEADS, HD]),
                                                        ALU.mult).then_inc(S['pool_r'], 1)
                                pool.wait_ge(S['pool_r'], g.after(6, 2 * t + 1))
                                nc.gpsimd.tensor_tensor(t1[:, b], t1[:, b], tabs[:, 2, t],
                                                        ALU.add).then_inc(S['rope_ok'], 1)

            run_iterations(pool, iteration)

        @block.scalar
        def _(act):
            act.preload_act_table_set("natural_log_exp_and_others")

            def iteration(i, A, B, C_):
                def pT_out(g, u):
                    if g.c == 0 and u == 0:
                        act.wait_ge(S['rows_0'], 3)
                    act.wait_ge(S['pT'], g.after(UNITS, u))
                    src = p_s[0:SEQ, u % 2, :, 0:4 * QP].rearrange("p x (h q) -> p x h q", q=QP)[:, :, :, 0:SEQ]
                    nc.scalar.copy(prT[0:SEQ, u % 2].rearrange("p (x h) q -> p x h q", x=2), src).then_inc(S['pT_out'], 1)

                def small_a(h):
                    g = i.plus(1)
                    if h in NORM_AT:
                        t = NORM_AT[h]
                        act.wait_ge(S['a_var'], g.after(3, t))
                        nc.scalar.activation(a_ln[:, t % 2:t % 2 + 1], a_mv[:, t % 2, 1:2], ACT.Ln,
                                             bias=eps5[0:TP, 0:1]).then_inc(S['act_a'], 1)
                        act.wait_ge(S['act_a'], g.after(3, t))
                        nc.scalar.activation(a_rs[:, t % 2:t % 2 + 1], a_ln[:, t % 2:t % 2 + 1], ACT.Exp,
                                             scale=-0.5).then_inc(S['a_rstd'], 1)
                    for step, t in A_AT.get(h - 1, []):
                        if step == 'qk':
                            act.wait_ge(S['ss_ok'], g.after(3, t))
                            nc.scalar.activation(ss_ln[:], ss[:, t % 2], ACT.Ln, bias=eps6[0:TP, 0:1],
                                                 scale=1.0 / HD).then_inc(S['act_r'], 1)
                            act.wait_ge(S['act_r'], g.after(3, t))
                            nc.scalar.activation(ss_rs[:, t % 2], ss_ln[:], ACT.Exp, scale=-0.5).then_inc(S['ss_rstd'], 1)

                def part_a(h):
                    g = i.plus(1)
                    for step, t in A_AT.get(h, []):
                        c0 = t * TP
                        if step == 'xT':
                            act.wait_ge(S['xT'], g.after(3, t))
                            nc.scalar.copy(xnT.hi[:, g.half, :, c0:c0 + TP].bitcast(F32R),
                                           p_a[:, 0:CC * TP].rearrange("p (c n) -> p c n", c=CC)).then_inc(S['xT_out'], 1)
                        if step == 'qk':
                            act.wait_ge(S['qk'], g.after(3, t))
                            nc.scalar.activation(sq[:], p_a[0:TP, :], ACT.Square).then_inc(S['sq_ok'], 1)
                        if step == 'qkT':
                            act.wait_ge(S['qkT_ok'], g.after(3, t))
                            nc.scalar.copy(qkT[:, g.half, :, c0:c0 + TP],
                                           p_a[:, 0:4 * TP].rearrange("p (c n) -> p c n", c=4)).then_inc(S['qkT_out'], 1)
                        if step == 'v':
                            if t == 0 and g.c < 2:
                                act.wait_ge(S['vp_0'], g.c + 1)
                            act.wait_ge(S['v_mm'], g.after(2, t))
                            nc.scalar.copy(vp[0:SEQ, g.half, 2 * t:2 * t + 2, :, 0:HD].rearrange("p b h d -> p (b h) d"),
                                           p_a[0:SEQ, :].rearrange("p (h d) -> p h d", d=HD)).then_inc(S['v_out'], 1)

                def part_c(h):
                    g = i.plus(-1)
                    for step, t in C_AT.get(h, []):
                        if step == 'yT':
                            act.wait_ge(S['yT_ok'], g.after(3, t))
                            nc.scalar.copy(yT.hi[:].bitcast(F32R), p_c[:, 0:CC * TP].rearrange("p (c n) -> p c n", c=CC)
                                           ).then_inc(S['yT_out'], 1)
                        if step == 'ffn':
                            act.wait_ge(S['ffn'], g.after(3, t))
                            nc.scalar.copy(f[:, t], p_c[0:TP, 0:FFN_N]).then_inc(S['ffn_out'], 1)
                        if step == 'twT':
                            act.wait_ge(S['twT_ok'], g.after(1, 0))
                            nc.scalar.copy(twT.hi[:].bitcast(F32R), p_c[0:TILES * LR, 0:TP]).then_inc(S['twT_out'], 1)

                def small_c(h):
                    g = i.plus(-1)
                    for step, t in C_AT.get(h - 1, []):
                        if step == 'proj':
                            act.wait_ge(S['c_var'], g.after(3, t))
                            nc.scalar.activation(c_ln[:], c_mv[:, 1:2], ACT.Ln, bias=eps5[0:TP, 0:1]).then_inc(S['act_c'], 1)
                            act.wait_ge(S['act_c'], g.after(3, t))
                            nc.scalar.activation(c_rs[:], c_ln[:], ACT.Exp, scale=-0.5).then_inc(S['c_rstd'], 1)
                    if h == GATE_AT:
                        act.wait_ge(S['g_m'], g.after(1, 0))
                        nc.scalar.activation(g_e[:], g_e[:], ACT.Exp).then_inc(S['g_exp'], 1)

                for h in range(16):
                    u, even = h // 2, h % 2 == 0
                    for piece in ORDER_ACT[h % 2]:
                        if piece == 'oT' and u % 2 == 1:
                            g, b = (i, (u - 3) // 2) if u > 1 else (i.plus(-1), GB - 1)
                            if B and u > 1 or C_ and u == 1:
                                act.wait_ge(S['pv'], g.after(UNITS, 2 * b + 1))
                                nc.scalar.copy(oT[:], p_o[:, 0:4 * SEQ].rearrange("p (c q) -> p c q", c=4)
                                               ).then_inc(S['o_out'], 1)
                        if piece == 'exp' and B:
                            act.wait_ge(S['s_shift'], i.after(UNITS, u))
                            nc.scalar.activation(pr[:, u % 2], p_s[0:QP, u % 2, :, 0:4 * SEQ], ACT.Exp,
                                                 scale=HD ** -0.5).then_inc(S['s_exp'], 1)
                        if piece == 'A' and A:
                            part_a(h)
                        if piece == 'C' and C_:
                            part_c(h)
                        if piece == 'oB' and u % 2 == 0:
                            g, b = (i, (u - 4) // 2) if u > 2 else (i.plus(-1), GB - 2 + u // 2)
                            if B and u > 2 or C_ and u <= 2:
                                act.wait_ge(S['oB'], g.after(GB, b))
                                nc.scalar.copy(onT.hi[:, g.half, :, b * SEQ:(b + 1) * SEQ].bitcast(F32R),
                                               p_n[:, 0:CC * QP].rearrange("p (c q) -> p c q", c=CC)[:, :, 0:SEQ]
                                               ).then_inc(S['oB_out'], 1)
                        if piece == 'pT' and (B if u > 0 else C_):
                            pT_out(*((i, u - 1) if u > 0 else (i.plus(-1), UNITS - 1)))
                        if piece == 'small C' and C_:
                            small_c(h)
                        if piece == 'small A' and A:
                            small_a(h)

            run_iterations(act, iteration)

        @block.vector
        def _(dve):
            def iteration(i, A, B, C_):
                def a_moments(g, t):
                    b = t % 2
                    if t == 0:
                        dve.wait_ge(ha_in[g.half], g.uses(16))
                    nc.vector.bn_stats(a_st[:, b], ha[:, g.half, t]).then_inc(S['dve_r'], 1)
                    dve.wait_ge(S['dve_r'], g.after(3, t))
                    nc.vector.tensor_copy(a_mv[:, b, 2:3], a_st[:, b, 0:1])
                    nc.vector.bn_aggr(a_mv[:, b, 0:2], a_st[:, b]).then_inc(S['a_var'], 1)

                def a_norm(g, t):
                    b = t % 2
                    dve.wait_ge(S['a_rstd'], g.after(3, t))
                    if g.c * 3 + t >= 2:
                        dve.wait_ge(S['xT'], g.after(3, t - 2))
                    nc.vector.tensor_scalar(xn[:, b], ha[:, g.half, t], a_mv[:, b, 0:1], a_rs[:, b:b + 1],
                                            ALU.subtract, ALU.mult).then_inc(S['xn_ok'], 1)

                def rotate(g, t):
                    b = t % 2
                    dve.wait_ge(S['sq_ok'], g.after(3, t))
                    if g.c * 3 + t >= 2:
                        dve.wait_ge(S['qkT_ok'], g.after(3, t - 2))
                    x = p_a[0:TP, :]
                    nc.vector.tensor_tensor(t1[:, b], x, tabs[:, 0, t], ALU.mult)
                    x4 = x.rearrange("p (h s d) -> p h s d", s=2, d=HD // 2)
                    o4 = t2[:, b].rearrange("p (h s d) -> p h s d", s=2, d=HD // 2)
                    w4_ = tabs[:, 1, t].rearrange("p (h s d) -> p h s d", s=2, d=HD // 2)
                    for s in range(2):
                        nc.vector.tensor_tensor(o4[:, :, s], x4[:, :, 1 - s], w4_[:, :, s],
                                                ALU.mult).then_inc(S['rot_ok'], 1)
                    nc.vector.reduce_sum(ss[:, b], sq[:].rearrange("p (h d) -> p h d", d=HD), AX_X).then_inc(S['ss_ok'], 1)

                def norm_c(h):
                    g = i.plus(-1)
                    for step, t in C_AT.get(h - 1, []):
                        if step == 'proj':
                            dve.wait_ge(S['c_rstd'], g.after(3, t))
                            if t > 0 or i.c > 1:
                                dve.wait_ge(S['yT_ok'], g.after(3, t - 1))
                            nc.vector.tensor_scalar(yn[:], h2[:, t % 2], c_mv[:, 0:1], c_rs[:, 0:1],
                                                    ALU.subtract, ALU.mult).then_inc(S['yn_ok'], 1)
                            dve.wait_ge(S['yn_ok'], g.after(3, t))

                def part_c(h):
                    g = i.plus(-1)
                    for step, t in C_AT.get(h, []):
                        if step == 'proj':
                            dve.wait_ge(S['proj'], g.after(3, t))
                            dve.wait_ge(S['hb_ok'], g.after(3, t))
                            if t > 1 or i.c > 1:
                                dve.wait_ge(S['h2l_ok'], g.after(3, t - 2))
                            nc.vector.tensor_tensor(h2[:, t % 2], p_c[0:TP, 0:C], hb[:, t % 2], ALU.add).then_inc(S['h2_ok'], 1)
                            dve.wait_ge(S['h2_ok'], g.after(3, t))
                            nc.vector.bn_stats(c_st[:], h2[:, t % 2]).then_inc(S['dve_c'], 1)
                            dve.wait_ge(S['dve_c'], g.after(3, t))
                            nc.vector.tensor_copy(c_mv[:, 2:3], c_st[:, 0:1])
                            nc.vector.bn_aggr(c_mv[:, 0:2], c_st[:]).then_inc(S['c_var'], 1)
                        if step == 'yT':
                            dve.wait_ge(S['yT_out'], g.after(3, t))
                            nc.vector.tensor_tensor(yT.lo[:].bitcast(F32R),
                                                    p_c[:, 0:CC * TP].rearrange("p (c n) -> p c n", c=CC), yT.hi[:],
                                                    ALU.subtract).then_inc(S['yT_lo'], 1)
                        if step == 'twT':
                            dve.wait_ge(S['twT_out'], g.after(1, 0))
                            nc.vector.tensor_tensor(twT.lo[:].bitcast(F32R), p_c[0:TILES * LR, 0:TP], twT.hi[:],
                                                    ALU.subtract).then_inc(S['twT_lo'], 1)
                        if step == 'lora':
                            dve.wait_ge(S['lora'], g.after(2, t))
                            for n, t in enumerate(LORA_TILES[t]):
                                dve.wait_ge(S['fb_ok'], g.after(3, t))
                                if i.c > 1:
                                    dve.wait_ge(stored[t], g.after(1, -1) * 16)
                                nc.vector.tensor_tensor(out_sb[:, t], p_c[0:TP, n * C:(n + 1) * C], h2l[:, t],
                                                        ALU.add).then_inc(S['out_ok'], 1)
                    if h == GATE_AT:
                        rank_experts(g)
                    if h == GATE_AT + 1:
                        weigh_experts(g)

                gate_steps = 9

                def rank_experts(g):
                    then = lambda n, ins: (ins.then_inc(S['dve_g'], 1), dve.wait_ge(S['dve_g'], g.after(gate_steps, n)))
                    dve.wait_ge(S['ffn_out'], g.after(3, 2))
                    lg = f[:, :, C + LR:FFN_N]
                    shape = [TP, TILES, EXPERTS, EXPERTS]
                    by_e, by_j = lg.unsqueeze(3).broadcast_to(shape), lg.unsqueeze(2).broadcast_to(shape)
                    then(0, nc.vector.reduce_max(g_max[:], lg, AX_X))
                    nc.vector.tensor_tensor(g_e[:], lg, g_max[:].unsqueeze(2).broadcast_to([TP, TILES, EXPERTS]),
                                            ALU.subtract).then_inc(S['g_m'], 1)
                    nc.vector.tensor_tensor(g_gt[:], by_j, by_e, ALU.is_gt)
                    then(1, nc.vector.tensor_tensor(g_eq[:], by_j, by_e, ALU.is_equal))
                    then(2, nc.vector.tensor_tensor(g_eq[:], g_eq[:], earlier[:].unsqueeze(1).broadcast_to(shape),
                                                    ALU.mult))
                    then(3, nc.vector.tensor_tensor(g_gt[:], g_gt[:], g_eq[:], ALU.add))
                    then(4, nc.vector.reduce_sum(g_rank[:], g_gt[:], AX_X))

                def weigh_experts(g):
                    then = lambda n, ins: (ins.then_inc(S['dve_g'], 1), dve.wait_ge(S['dve_g'], g.after(gate_steps, n)))
                    dve.wait_ge(S['g_exp'], g.after(1, 0))
                    then(5, nc.vector.reduce_sum(g_sum[:], g_e[:], AX_X))
                    then(6, nc.vector.reciprocal(g_rs[:], g_sum[:]))
                    then(7, nc.vector.scalar_tensor_tensor(g_w[:], g_rank[:], 2.0, g_e[:], ALU.is_lt, ALU.mult))
                    then(8, nc.vector.tensor_tensor(g_w[:], g_w[:], g_rs[:].unsqueeze(2).broadcast_to([TP, TILES, EXPERTS]),
                                                    ALU.mult))
                    nc.vector.tensor_tensor(
                        tw[:].rearrange("p t (e r) -> p t e r", r=RANK),
                        f[:, :, C:C + LR].rearrange("p t (e r) -> p t e r", r=RANK),
                        g_w[:].unsqueeze(3).broadcast_to([TP, TILES, EXPERTS, RANK]), ALU.mult).then_inc(S['tw_ok'], 1)

                for h in range(16):
                    u, even = h // 2, h % 2 == 0
                    if i.c == -1 and h == 12:
                        nc.vector.memset(kb[:, 1], 0.0).then_inc(S['kb_0'], 1)
                    for piece in ORDER_DVE[h % 2]:
                        if piece == 'max' and B:
                            dve.wait_ge(S['s_mm'], i.after(UNITS, u))
                            if i.c * UNITS + u >= 2:
                                dve.wait_ge(S['s_shift'], i.after(UNITS, u - 2))
                            nc.vector.reduce_max(mx[:, u % 2].rearrange("p (x h) -> p x h", x=2),
                                                 p_s[0:QP, u % 2, :, 0:4 * SEQ].rearrange("p x (h k) -> p x h k", k=SEQ),
                                                 AX_X, negate=True).then_inc(S['s_max'], 1)
                        if piece == 'o_norm' and u % 2 == 1:
                            g, b = (i, (u - 3) // 2) if u > 1 else (i.plus(-1), GB - 1)
                            if B and u > 1 or C_ and u == 1:
                                if g.c == 0 and b == 0:
                                    dve.wait_ge(S['rows_0'], 3)
                                dve.wait_ge(S['oN'], g.after(GB, b))
                                o3 = p_n[0:SEQ, :].rearrange("p (h e) -> p h e", e=2 * HD)
                                nc.vector.reciprocal(rd[:], o3[:, :, HD]).then_inc(S['dve_n'], 1)
                                dve.wait_ge(S['dve_n'], g.after(GB, b))
                                nc.vector.tensor_tensor(on[0:SEQ].rearrange("p (h d) -> p h d", d=HD), o3[:, :, 0:HD],
                                                        rd[:].unsqueeze(2).broadcast_to([SEQ, HEADS, HD]),
                                                        ALU.mult).then_inc(S['o_norm'], 1)
                        if piece == 'norm A' and A and h - 1 in NORM_AT:
                            a_norm(i.plus(1), NORM_AT[h - 1])
                        if piece == 'stats A' and A and h in NORM_AT:
                            a_moments(i.plus(1), NORM_AT[h])
                        if piece == 'A' and A:
                            for step, t in A_AT.get(h, []):
                                if step == 'xT':
                                    g, c0 = i.plus(1), t * TP
                                    dve.wait_ge(S['xT_out'], g.after(3, t))
                                    nc.vector.tensor_tensor(
                                        xnT.lo[:, g.half, :, c0:c0 + TP].bitcast(F32R),
                                        p_a[:, 0:CC * TP].rearrange("p (c n) -> p c n", c=CC),
                                        xnT.hi[:, g.half, :, c0:c0 + TP], ALU.subtract).then_inc(S['xT_lo'], 1)
                                if step == 'qk':
                                    rotate(i.plus(1), t)
                        if piece == 'norm C' and C_:
                            norm_c(h)
                        if piece == 'C' and C_:
                            part_c(h)
                        if piece == 'oB' and u % 2 == 0:
                            g, b = (i, (u - 4) // 2) if u > 2 else (i.plus(-1), GB - 2 + u // 2)
                            if B and u > 2 or C_ and u <= 2:
                                dve.wait_ge(S['oB_out'], g.after(GB, b))
                                nc.vector.tensor_tensor(
                                    onT.lo[:, g.half, :, b * SEQ:(b + 1) * SEQ].bitcast(F32R),
                                    p_n[:, 0:CC * QP].rearrange("p (c q) -> p c q", c=CC)[:, :, 0:SEQ],
                                    onT.hi[:, g.half, :, b * SEQ:(b + 1) * SEQ], ALU.subtract).then_inc(S['oB_lo'], 1)

            run_iterations(dve, iteration)

        @block.tensor
        def _(pe):
            def mm(out, lhs, rhs, done=None):
                for c, (a, b) in enumerate(zip(lhs, rhs)):
                    last = nc.tensor.matmul(out, a, b, start=(c == 0), stop=(c == len(lhs) - 1))
                if done is not None:
                    last.then_inc(done, 1)
                return last

            def mm_split(out, lhs, rhs, done=None):
                parts = [(lhs.hi, rhs.hi), (lhs.hi, rhs.lo), (lhs.lo, rhs.hi)]
                return mm(out, [x.bitcast(F32R) for a, _ in parts for x in a], [x.bitcast(F32R) for _, b in parts for x in b],
                          done)

            A_FREE = {'xT': ('xT_lo', 3), 'qk': ('rot_ok', 6), 'qkT': ('qkT_out', 3), 'v': ('v_out', 2)}
            C_FREE = {'proj': ('h2_ok', 3), 'yT': ('yT_lo', 3), 'ffn': ('ffn_out', 3), 'twT': ('twT_lo', 1),
                      'lora': ('out_ok', 3)}

            def wait_bank(order, free, g, item, first):
                n = order.index(item)
                if n == 0 and first:
                    return
                step, t = order[n - 1]
                name, per = free[step]
                k = {'rot_ok': 2 * t + 1, 'out_ok': LORA_TILES[t % 2][-1]}.get(name, t)
                pe.wait_ge(S[name], (g if n else g.plus(-1)).after(per, k))

            def iteration(i, A, B, C_):
                def part_a(h):
                    g = i.plus(1)
                    for step, t in A_AT.get(h, []):
                        wait_bank(A_BANK, A_FREE, g, (step, t), g.c == 0)
                        c0 = t * TP
                        if step == 'xT':
                            pe.wait_ge(S['xn_ok'], g.after(3, t))
                            for c in range(CC):
                                last = nc.tensor.transpose(p_a[:, c * TP:(c + 1) * TP], xn[:, t % 2, c * P:(c + 1) * P],
                                                           ident[0:TP, 0:TP])
                            last.then_inc(S['xT'], 1)
                        if step == 'qk':
                            pe.wait_ge(S['xT_lo'], g.after(3, t))
                            mm_split(p_a[0:TP, :], xnT.chunks(lambda x, c: x[:, g.half, c, c0:c0 + TP]),
                                     w_qk.chunks(lambda x, c: x[:, c]), S['qk'])
                        if step == 'qkT':
                            pe.wait_ge(S['rope_ok'], g.after(3, t))
                            for c in range(4):
                                last = nc.tensor.transpose(p_a[:, c * TP:(c + 1) * TP], t1[:, t % 2, c * P:(c + 1) * P],
                                                           ident[0:TP, 0:TP])
                            last.then_inc(S['qkT_ok'], 1)
                        if step == 'v':
                            for n in range(2):
                                b = 2 * t + n
                                last = mm_split(p_a[0:SEQ, n * C:(n + 1) * C],
                                                xnT.chunks(lambda x, c: x[:, g.half, c, b * SEQ:(b + 1) * SEQ]),
                                                w_v.chunks(lambda x, c: x[:, c]))
                            last.then_inc(S['v_mm'], 1)

                def part_c(h):
                    g = i.plus(-1)
                    for step, t in C_AT.get(h, []):
                        wait_bank(C_BANK, C_FREE, g, (step, t), g.c == 0)
                        c0 = t * TP
                        if step == 'proj':
                            pe.wait_ge(S['oB_lo'], g.after(GB, min(t + 1, GB - 1)))
                            mm_split(p_c[0:TP, 0:C], onT.chunks(lambda x, c: x[:, g.half, c, c0:c0 + TP]),
                                     w_p.chunks(lambda x, c: x[:, c]), S['proj'])
                        if step == 'yT':
                            pe.wait_ge(S['yn_ok'], g.after(3, t))
                            for c in range(CC):
                                last = nc.tensor.transpose(p_c[:, c * TP:(c + 1) * TP], yn[:, c * P:(c + 1) * P],
                                                           ident[0:TP, 0:TP])
                            last.then_inc(S['yT_ok'], 1)
                        if step == 'ffn':
                            pe.wait_ge(S['yT_lo'], g.after(3, t))
                            mm_split(p_c[0:TP, 0:FFN_N], yT.chunks(lambda x, c: x[:, c]),
                                     w_f.chunks(lambda x, c: x[:, c]), S['ffn'])
                        if step == 'twT':
                            pe.wait_ge(S['tw_ok'], g.after(1, 0))
                            nc.tensor.transpose(p_c[0:TILES * LR, 0:TP], tw[:].rearrange("p t n -> p (t n)"),
                                                ident[0:TP, 0:TP]).then_inc(S['twT_ok'], 1)
                        if step == 'lora':
                            pe.wait_ge(S['twT_lo'], g.after(1, 0))
                            for n, tile in enumerate(LORA_TILES[t]):
                                last = mm_split(p_c[0:TP, n * C:(n + 1) * C], twT.chunks(lambda x, c: x[:], 1),
                                                right.chunks(lambda x, c: x[:, tile], 1))
                            last.then_inc(S['lora'], 1)

                def scores(u):
                    b, k = u // 2, u % 2
                    if i.c == 0 and u == 0:
                        pe.wait_ge(S['rows_0'], 3)
                    if k == 0 and b == 0:
                        pe.wait_ge(k_in[i.half][0], i.uses(16 * HEADS))
                    if k == 0 and b == 2:
                        pe.wait_ge(k_in[i.half][1], i.uses(16 * HEADS))
                    if i.c * UNITS + u >= 2:
                        pe.wait_ge(S['pT_out'], i.after(UNITS, u - 2))
                    for x in range(2):
                        last = nc.tensor.matmul(p_s[0:QP, u % 2, x, 0:4 * SEQ], qkT[:, i.half, k, b * SEQ:b * SEQ + QP],
                                                kb[:, i.half, k, 4 * x:4 * x + 4, b * SEQ:(b + 1) * SEQ],
                                                start=True, stop=False, skip_group_check=True)
                    last.then_inc(S['s_mm'], 1)

                def shift(u):
                    pe.wait_ge(S['s_max'], i.after(UNITS, u))
                    for x in range(2):
                        last = nc.tensor.matmul(p_s[0:QP, u % 2, x, 0:4 * SEQ], ident_b[0:QP, 0:QP],
                                                mx[:, u % 2, 4 * x:4 * x + 4].unsqueeze(2).broadcast_to([QP, 4, SEQ]),
                                                start=False, stop=True, skip_group_check=True)
                    last.then_inc(S['s_shift'], 1)

                def transpose_probs(g, u):
                    pe.wait_ge(S['s_exp'], g.after(UNITS, u))
                    for x in range(2):
                        for n in range(4):
                            last = nc.tensor.transpose(p_s[0:SEQ, u % 2, x, n * QP:(n + 1) * QP],
                                                       pr[:, u % 2, x, n * SEQ:(n + 1) * SEQ], ident[0:QP, 0:QP])
                    last.then_inc(S['pT'], 1)

                def weigh_values(g, u):
                    b, k = u // 2, u % 2
                    pe.wait_ge(S['pT_out'], g.after(UNITS, u))
                    if k == 0 and not (b == 0 and g.c == 0):
                        pe.wait_ge(S['o_out'], g.after(GB, b - 1))
                    for n in range(HALF):
                        c, j = 2 * k + n // 4, n % 4
                        last = nc.tensor.matmul(p_o[32 * j:32 * j + 32, c * SEQ:(c + 1) * SEQ],
                                                vp[:, g.half, b, HALF * k + n, :], prT[:, u % 2, n, :],
                                                start=True, stop=True)
                    last.then_inc(S['pv'], 1)

                for h in range(16):
                    u, even = h // 2, h % 2 == 0
                    out_of = None
                    if u % 2 == 1:
                        if u > 1 and B:
                            out_of = (i, (u - 3) // 2)
                        if u == 1 and C_:
                            out_of = (i.plus(-1), GB - 1)
                    normalised_of = None
                    if u % 2 == 0:
                        if u > 2 and B:
                            normalised_of = (i, (u - 4) // 2)
                        if u <= 2 and C_:
                            normalised_of = (i.plus(-1), GB - 2 + u // 2)
                    before = (i, u - 1) if u > 0 else (i.plus(-1), UNITS - 1)
                    has_before = B if u > 0 else C_
                    for piece in ORDER_PE[h % 2]:
                        if piece == 'scores' and B:
                            scores(u)
                        if piece == 'shift' and B:
                            shift(u)
                        if piece == 'A' and A:
                            part_a(h)
                        if piece == 'C' and C_:
                            part_c(h)
                        if piece == 'oB' and normalised_of:
                            g, b = normalised_of
                            pe.wait_ge(S['o_norm'], g.after(GB, b))
                            for c in range(CC):
                                last = nc.tensor.transpose(p_n[:, c * QP:(c + 1) * QP], on[:, c * P:(c + 1) * P],
                                                           ident[0:QP, 0:QP])
                            last.then_inc(S['oB'], 1)
                        if piece == 'pT' and has_before:
                            transpose_probs(*before)
                        if piece == 'oN' and out_of:
                            g, b = out_of
                            pe.wait_ge(S['o_out'], g.after(GB, b))
                            if not (g.c == 0 and b == 0):
                                pe.wait_ge(S['oB_lo'], g.after(GB, b - 1))
                            for c in range(4):
                                last = nc.tensor.transpose(p_n[0:SEQ, c * P:(c + 1) * P], oT[:, c], ident[:])
                            last.then_inc(S['oN'], 1)
                        if piece == 'pv' and has_before:
                            weigh_values(*before)

            run_iterations(pe, iteration)


def build(nc, io, out):
    h_dram = nc.dram_tensor("h_tokens", [IMAGES * SEQ, C], F32).ap()
    patch_dram = nc.dram_tensor("patch_tokens", [ALL_W, C], F32).ap()
    gv_dram = nc.dram_tensor("class_values", [ALL_W, C], F32).ap()
    gs_dram = nc.dram_tensor("class_scores", [2, ALL_W, LH // 2], F32).ap()
    with ExitStack() as ctx:
        consts = Constants(nc, ctx)
        patch_tokens(nc, io, consts, h_dram, patch_dram, gv_dram, gs_dram)
        attention_ffn(nc, io, consts, h_dram, out.rearrange("b s c -> (b s) c"))


def arrays_of(inputs):
    a = {k.replace('L0_tok_', '').replace('L0_attn_', '').replace('L0_ffn_', ''): np.asarray(v)
         for k, v in inputs.items()}
    side = PATCH * GRID * GRID
    x = a['x'][:, :, :side, :side].reshape(IMAGES, 3, GRID, GRID, PATCH, GRID, GRID, PATCH)
    x = x.transpose(1, 4, 7, 0, 2, 5, 3, 6).reshape(PIXELS, ALL_W, CELLS)
    x_cols = np.zeros((STEPS, KROWS * KCH, CELLS * P), x.dtype)
    for s, m in enumerate(TOK_M):
        part = x[:, P * s:P * s + m, :].transpose(0, 2, 1)
        x_cols[s, :PIXELS, :CELLS * m] = part.reshape(PIXELS, CELLS * m)
    conv_w = np.zeros((KROWS * KCH, C), a['conv_w'].dtype)
    conv_w[:PIXELS] = a['conv_w'].reshape(C, PIXELS).T
    vec = {**a, 'b_lin': a['b_lin']}
    half = HD // 2
    rope_g = np.stack([a['q_gamma'], a['k_gamma'], np.roll(a['q_gamma'], half), np.roll(a['k_gamma'], half),
                       a['q_beta'], a['k_beta'], np.roll(a['q_beta'], half), np.roll(a['k_beta'], half)])
    inv = (1.0 / 10000.0 ** (np.arange(half, dtype=np.float32) / half)).astype(np.float32)
    ang = np.outer(np.arange(GT) % SEQ, inv).astype(np.float32)
    sin = np.concatenate([-np.sin(ang), np.sin(ang)], axis=1)
    cos = np.concatenate([np.cos(ang), np.cos(ang)], axis=1)
    rope = np.stack([cos, sin]).reshape(2, TILES, TP, HD).transpose(2, 1, 0, 3)
    wf = np.concatenate([a['W_lin'].T, a['left'].transpose(1, 0, 2).reshape(C, LR), a['gate_w'].T], axis=1)
    out = {
        'x_cols': x_cols, 'conv_w': conv_w, 'txt': a['txt'],
        'rows': np.stack([vec[r] for r in ROWS]),
        'cols': np.stack([vec[c] for c in COLS]).reshape(len(COLS), CC, P).transpose(2, 0, 1),
        'w_qkv': a['w_qkv'].T, 'w_proj': a['w_proj'].T, 'w_ffn': wf, 'right': a['right'].reshape(LR, C),
        'rope_g': rope_g, 'rope': rope.astype(np.float32),
    }
    for n in ('la_wq', 'la_wkv', 'la_proj_w', 'ga_wq', 'ga_wkv', 'ga_proj_w', 'mod_w'):
        out[n] = a[n]
    return {k: np.ascontiguousarray(v) for k, v in out.items()}


def kernel(**inputs):
    import concourse.bacc as bacc
    from concourse.bass_utils import run_bass_kernel_spmd

    arrays = arrays_of(inputs)
    nc = bacc.Bacc("TRN2", target_bir_lowering=False, num_devices=1)
    io = {k: nc.dram_tensor("in_" + k, v.shape, mybir.dt.from_np(v.dtype), kind="ExternalInput").ap()
          for k, v in arrays.items()}
    out = nc.dram_tensor("out", (IMAGES, SEQ, C), F32, kind="ExternalOutput").ap()
    build(nc, io, out)
    r = run_bass_kernel_spmd(nc, [{"in_" + k: v for k, v in arrays.items()}], core_ids=[0])
    return r.results[0]["out"]
```
